# Optimizing a Trainium2 kernel written in Bass

```python
import numpy as np
import jax
import jax.numpy as jnp

def _softmax(x, axis=-1):
    return jax.nn.softmax(x, axis=axis)

def _gelu(x):
    return jax.nn.gelu(x, approximate=True)

def _silu(x):
    return jax.nn.silu(x)

def _sigmoid(x):
    return jax.nn.sigmoid(x)

def _layernorm(x, axis=-1, eps=1e-05):
    m = jnp.mean(x, axis=axis, keepdims=True)
    v = jnp.var(x, axis=axis, keepdims=True)
    return (x - m) / jnp.sqrt(v + eps)

def _scatter_add(tgt, idx, src, axis=0):
    return tgt.at[idx].add(src)

def _segment_sum(src, seg, n):
    return jax.ops.segment_sum(src, seg, n)
kernel_name = 'mk_macaron_d4_jaxref_r8_8adc66'

def setup_inputs(seed: int=0):
    np.random.seed(seed)
    _w = jnp.asarray

    def _L0_attn_setup():
        import jax, jax.numpy as jnp
        import numpy as np
        import math
        NUM_HEADS = 16
        MAX_REL = 64
        LOCAL_WINDOW = 32
        key = jax.random.key(seed)
        k1, k2, k3, k4 = jax.random.split(key, 4)
        B, L, D = (4, 128, 128)
        x = jax.random.normal(k1, (B, L, D), dtype=jnp.float32)
        w_qkv = jax.random.normal(k2, (3 * D, D), dtype=jnp.float32) * (1.0 / math.sqrt(D))
        w_out = jax.random.normal(k3, (D, D), dtype=jnp.float32) * (1.0 / math.sqrt(D))
        rel_emb = jax.random.normal(k4, (2 * MAX_REL + 1, D // NUM_HEADS), dtype=jnp.float32)
        return {'x': x, 'w_qkv': w_qkv, 'w_out': w_out, 'rel_emb': rel_emb}
    _L0_attn_in = _L0_attn_setup()

    def _L0_ffn_setup():
        import jax, jax.numpy as jnp
        import numpy as np

        def gelu(x):
            return jax.nn.gelu(x, approximate=False)
        key = jax.random.key(seed)
        ks = jax.random.split(key, 6)
        B, S, d_model = (4, 256, 128)
        n_input, n_process, n_output, d_pv = (1024, 512, 1024, 64)
        s = 0.02
        return {'x': jax.random.normal(ks[0], (B, S, d_model), jnp.float32), 'input_patterns': jax.random.normal(ks[1], (n_input, d_model), jnp.float32) * s, 'process_input_weights': jax.random.normal(ks[2], (n_process, n_input), jnp.float32) * s, 'process_values': jax.random.normal(ks[3], (n_process, d_pv), jnp.float32) * s, 'output_input_weights': jax.random.normal(ks[4], (n_output, d_pv), jnp.float32) * s, 'output_patterns': jax.random.normal(ks[5], (n_output, d_model), jnp.float32) * s}
    _L0_ffn_in = _L0_ffn_setup()

    def _L1_attn_setup():
        import jax, jax.numpy as jnp
        import numpy as np
        H = 16
        EPS = 1e-12

        def _l2norm(t):
            n = jnp.sqrt(jnp.sum(t * t, axis=-1, keepdims=True))
            return t / jnp.maximum(n, EPS)
        key = jax.random.key(seed)
        ks = jax.random.split(key, 7)
        B, L, D = (2, 256, 128)
        s = 0.02
        return {'x': jax.random.normal(ks[0], (B, L, D), dtype=jnp.float32), 'Wq': jax.random.normal(ks[1], (D, D), dtype=jnp.float32) * s, 'Wk': jax.random.normal(ks[2], (D, D), dtype=jnp.float32) * s, 'Wv': jax.random.normal(ks[3], (D, D), dtype=jnp.float32) * s, 'Wo': jax.random.normal(ks[4], (D, D), dtype=jnp.float32) * s, 'Wb': jax.random.normal(ks[5], (D, H), dtype=jnp.float32) * s, 'bb': jnp.zeros((H,), dtype=jnp.float32)}
    _L1_attn_in = _L1_attn_setup()

    def _L1_ffn_setup():
        import jax, jax.numpy as jnp
        import numpy as np
        NUM_HEADS = 16
        TOP_K = 2
        ROPE_BASE = 10000.0
        LN_EPS = 1e-05

        def _rope_sin_cos(S, D, dtype):
            inv_freq = 1.0 / ROPE_BASE ** (jnp.arange(0, D, 2, dtype=jnp.float32) / D)
            freqs = jnp.arange(S, dtype=jnp.float32)[:, None] * inv_freq[None, :]
            sin = jnp.sin(freqs).astype(dtype)[None, :, None, :]
            cos = jnp.cos(freqs).astype(dtype)[None, :, None, :]
            return (sin, cos)

        def _apply_rope(x, sin, cos):
            x1, x2 = (x[..., 0::2], x[..., 1::2])
            r1 = x1 * cos - x2 * sin
            r2 = x1 * sin + x2 * cos
            return jnp.stack([r1, r2], axis=-1).reshape(x.shape)

        def _layer_norm(x, w, b):
            mu = jnp.mean(x, axis=-1, keepdims=True)
            var = jnp.mean(jnp.square(x - mu), axis=-1, keepdims=True)
            return (x - mu) * jax.lax.rsqrt(var + LN_EPS) * w + b
        key = jax.random.key(seed)
        ks = jax.random.split(key, 8)
        B, S, E, NE = (2, 256, 128, 8)
        s = 0.02
        return {'x': jax.random.normal(ks[0], (B, S, E), dtype=jnp.float32), 'in_proj_w': jax.random.normal(ks[1], (3 * E, E), dtype=jnp.float32) * s, 'in_proj_b': jnp.zeros((3 * E,), dtype=jnp.float32), 'out_proj_w': jax.random.normal(ks[2], (E, E), dtype=jnp.float32) * s, 'out_proj_b': jnp.zeros((E,), dtype=jnp.float32), 'gate_w': jax.random.normal(ks[3], (NE, E), dtype=jnp.float32) * s, 'gate_b': jnp.zeros((NE,), dtype=jnp.float32), 'expert_w': jax.random.normal(ks[4], (NE, E, E), dtype=jnp.float32) * s, 'expert_b': jnp.zeros((NE, E), dtype=jnp.float32), 'ln1_w': jnp.ones((E,), dtype=jnp.float32), 'ln1_b': jnp.zeros((E,), dtype=jnp.float32), 'ln2_w': jnp.ones((E,), dtype=jnp.float32), 'ln2_b': jnp.zeros((E,), dtype=jnp.float32)}
    _L1_ffn_in = _L1_ffn_setup()

    def _L2_attn_setup():
        import jax, jax.numpy as jnp
        import numpy as np
        N_HEADS = 16
        BLOCK_SIZE = 32

        def _rope(x):
            B, H, L, d = x.shape
            inv_freq = 1.0 / 10000.0 ** (jnp.arange(0, d, 2, dtype=jnp.float32) / d)
            t = jnp.arange(L, dtype=jnp.float32)[:, None] * inv_freq[None, :]
            cos, sin = (jnp.cos(t), jnp.sin(t))
            x1, x2 = (x[..., 0::2], x[..., 1::2])
            return jnp.concatenate([x1 * cos - x2 * sin, x2 * cos + x1 * sin], axis=-1)
        key = jax.random.key(seed)
        k1, k2, k3 = jax.random.split(key, 3)
        B, L, D = (2, 512, 128)
        x = jax.random.normal(k1, (B, L, D), dtype=jnp.float32)
        Wqkv = jax.random.normal(k2, (3 * D, D), dtype=jnp.float32) * 0.02
        Wout = jax.random.normal(k3, (D, D), dtype=jnp.float32) * 0.02
        return {'x': x, 'Wqkv': Wqkv, 'Wout': Wout}
    _L2_attn_in = _L2_attn_setup()

    def _L2_ffn_setup():
        import jax, jax.numpy as jnp
        import numpy as np
        DIM = 128
        HIDDEN = 512
        E = 8
        B, S = (2, 512)
        key = jax.random.key(seed)
        ks = jax.random.split(key, 8)
        sd = 1.0 / np.sqrt(DIM)
        sh = 1.0 / np.sqrt(HIDDEN)
        return {'x': jax.random.normal(ks[0], (B, S, DIM), dtype=jnp.float32), 'router_w': jax.random.uniform(ks[1], (DIM, E), jnp.float32, -sd, sd), 'router_b': jax.random.uniform(ks[2], (E,), jnp.float32, -sd, sd), 'w1': jax.random.uniform(ks[3], (E, DIM, 2 * HIDDEN), jnp.float32, -sd, sd), 'b1': jax.random.uniform(ks[4], (E, 2 * HIDDEN), jnp.float32, -sd, sd), 'w2': jax.random.uniform(ks[5], (E, HIDDEN, DIM), jnp.float32, -sh, sh), 'b2': jax.random.uniform(ks[6], (E, DIM), jnp.float32, -sh, sh)}
    _L2_ffn_in = _L2_ffn_setup()

    def _L3_attn_setup():
        import jax, jax.numpy as jnp
        import numpy as np
        B, L, E, H = (2, 256, 128, 16)
        HD = E // H
        THETA = 10000.0

        def _rope_tables(seq_len, dim, dtype):
            inv_freq = 1.0 / THETA ** (jnp.arange(0, dim, 2, dtype=jnp.float32) / dim)
            freqs = jnp.arange(seq_len, dtype=jnp.float32)[:, None] * inv_freq[None, :]
            freqs = jnp.repeat(freqs, 2, axis=-1)
            return (jnp.cos(freqs).astype(dtype), jnp.sin(freqs).astype(dtype))

        def _rotate_half(x):
            x2 = x.reshape(*x.shape[:-1], -1, 2)
            x2 = jnp.stack([-x2[..., 1], x2[..., 0]], axis=-1)
            return x2.reshape(x.shape)

        def _apply_rope(x, cos, sin):
            return x * cos[None, None] + _rotate_half(x) * sin[None, None]
        key = jax.random.key(seed)
        ks = jax.random.split(key, 9)
        s = 1.0 / np.sqrt(E)
        return {'x': jax.random.normal(ks[0], (B, L, E), jnp.float32), 'Wq': jax.random.normal(ks[1], (E, E), jnp.float32) * s, 'bq': jax.random.normal(ks[2], (E,), jnp.float32) * 0.01, 'Wk': jax.random.normal(ks[3], (E, E), jnp.float32) * s, 'bk': jax.random.normal(ks[4], (E,), jnp.float32) * 0.01, 'Wv': jax.random.normal(ks[5], (E, E), jnp.float32) * s, 'bv': jax.random.normal(ks[6], (E,), jnp.float32) * 0.01, 'Wo': jax.random.normal(ks[7], (E, E), jnp.float32) * s, 'bo': jax.random.normal(ks[8], (E,), jnp.float32) * 0.01}
    _L3_attn_in = _L3_attn_setup()

    def _L3_ffn_setup():
        import jax, jax.numpy as jnp
        import numpy as np
        DIM = 128
        DEPTH = 2
        HEADS = 8
        DIM_HEAD = 64
        WINDOW = 64
        INNER = HEADS * DIM_HEAD
        HID = int(DIM * 4 * 2 / 3)
        B, N = (2, 1024)
        QK_SCALE = 8.0

        def shift_token(t):
            t1, t2 = jnp.split(t, 2, axis=-1)
            t2 = jnp.pad(t2, ((0, 0), (1, 0), (0, 0)))[:, :-1]
            return jnp.concatenate([t1, t2], axis=-1)

        def l2norm(t):
            return t / jnp.clip(jnp.linalg.norm(t, axis=-1, keepdims=True), 1e-12)

        def rotate_half(x):
            x1, x2 = jnp.split(x, 2, axis=-1)
            return jnp.concatenate([-x2, x1], axis=-1)

        def rotary_xpos(q, k):
            n = q.shape[-2]
            half_idx = jnp.arange(0, DIM_HEAD, 2, dtype=jnp.float32)
            inv_freq = 1.0 / 10000.0 ** (half_idx / DIM_HEAD)
            t = jnp.arange(n, dtype=jnp.float32)
            freqs = t[:, None] * inv_freq[None, :]
            freqs = jnp.concatenate([freqs, freqs], axis=-1)
            base = (half_idx + 0.4 * DIM_HEAD) / (1.4 * DIM_HEAD)
            power = (t - n // 2) / float(WINDOW // 2)
            scale = base[None, :] ** power[:, None]
            scale = jnp.concatenate([scale, scale], axis=-1)
            cos, sin = (jnp.cos(freqs), jnp.sin(freqs))
            q = q * cos * scale + rotate_half(q) * sin * scale
            k = k * cos / scale + rotate_half(k) * sin / scale
            return (q, k)

        def local_attention(q, k, v):
            b, h, n, d = q.shape
            w = n // WINDOW
            bq = q.reshape(b, h, w, WINDOW, d) * QK_SCALE
            bk = k.reshape(b, h, w, WINDOW, d)
            bv = v.reshape(b, h, w, WINDOW, d)

            def look_around(t):
                p = jnp.pad(t, ((0, 0), (0, 0), (1, 0), (0, 0), (0, 0)))
                return jnp.concatenate([p[:, :, :w], p[:, :, 1:]], axis=3)
            bk, bv = (look_around(bk), look_around(bv))
            bt = jnp.arange(n).reshape(w, WINDOW)
            btp = jnp.pad(bt, ((1, 0), (0, 0)), constant_values=-1)
            btk = jnp.concatenate([btp[:w], btp[1:]], axis=1)
            sim = jnp.einsum('bhwid,bhwjd->bhwij', bq, bk)
            i = bt[:, :, None]
            j = btk[:, None, :]
            mask = (i < j) | (i > j + WINDOW) | (j == -1)
            sim = jnp.where(mask, -jnp.finfo(sim.dtype).max, sim)
            attn = jax.nn.softmax(sim, axis=-1)
            out = jnp.einsum('bhwij,bhwjd->bhwid', attn, bv)
            return out.reshape(b, h, n, d)

        def _layer(x, wqkv, qs, ksc, wo, lg, lb, w1, b1, w2, b2):
            b, n, _ = x.shape
            h = shift_token(x)
            qkv = h @ wqkv
            q, k, v = jnp.split(qkv, 3, axis=-1)
            to_heads = lambda t: t.reshape(b, n, HEADS, DIM_HEAD).transpose(0, 2, 1, 3)
            q, k, v = (to_heads(q), to_heads(k), to_heads(v))
            q = l2norm(q) * qs
            k = l2norm(k) * ksc
            q, k = rotary_xpos(q, k)
            o = local_attention(q, k, v)
            o = o.transpose(0, 2, 1, 3).reshape(b, n, INNER)
            x = x + o @ wo
            h = shift_token(x)
            mu = h.mean(-1, keepdims=True)
            var = h.var(-1, keepdims=True)
            h = (h - mu) / jnp.sqrt(var + 1e-05) * lg + lb
            h = h @ w1 + b1
            a, g = jnp.split(h, 2, axis=-1)
            h = a * jax.nn.gelu(g, approximate=False)
            x = x + h @ w2 + b2
            return x
        key = jax.random.key(seed)
        ks = jax.random.split(key, 6)
        return {'x': jax.random.normal(ks[0], (B, N, DIM), jnp.float32), 'wqkv': jax.random.normal(ks[1], (DEPTH, DIM, 3 * INNER), jnp.float32) * 0.02, 'q_scale': jnp.ones((DEPTH, DIM_HEAD), jnp.float32), 'k_scale': jnp.ones((DEPTH, DIM_HEAD), jnp.float32), 'wo': jax.random.normal(ks[2], (DEPTH, INNER, DIM), jnp.float32) * 0.02, 'ln_g': jnp.ones((DEPTH, DIM), jnp.float32), 'ln_b': jnp.zeros((DEPTH, DIM), jnp.float32), 'w1': jax.random.normal(ks[3], (DEPTH, DIM, 2 * HID), jnp.float32) * 0.02, 'b1': jnp.zeros((DEPTH, 2 * HID), jnp.float32), 'w2': jax.random.normal(ks[4], (DEPTH, HID, DIM), jnp.float32) * 0.02, 'b2': jnp.zeros((DEPTH, DIM), jnp.float32)}
    _L3_ffn_in = _L3_ffn_setup()
    _d = {'L0_attn_x': _L0_attn_in['x'], 'L0_attn_w_qkv': _L0_attn_in['w_qkv'], 'L0_attn_w_out': _L0_attn_in['w_out'], 'L0_attn_rel_emb': _L0_attn_in['rel_emb'], 'L0_ffn_input_patterns': _L0_ffn_in['input_patterns'], 'L0_ffn_process_input_weights': _L0_ffn_in['process_input_weights'], 'L0_ffn_process_values': _L0_ffn_in['process_values'], 'L0_ffn_output_input_weights': _L0_ffn_in['output_input_weights'], 'L0_ffn_output_patterns': _L0_ffn_in['output_patterns'], 'L1_attn_Wq': _L1_attn_in['Wq'], 'L1_attn_Wk': _L1_attn_in['Wk'], 'L1_attn_Wv': _L1_attn_in['Wv'], 'L1_attn_Wo': _L1_attn_in['Wo'], 'L1_attn_Wb': _L1_attn_in['Wb'], 'L1_attn_bb': _L1_attn_in['bb'], 'L1_ffn_in_proj_w': _L1_ffn_in['in_proj_w'], 'L1_ffn_in_proj_b': _L1_ffn_in['in_proj_b'], 'L1_ffn_out_proj_w': _L1_ffn_in['out_proj_w'], 'L1_ffn_out_proj_b': _L1_ffn_in['out_proj_b'], 'L1_ffn_gate_w': _L1_ffn_in['gate_w'], 'L1_ffn_gate_b': _L1_ffn_in['gate_b'], 'L1_ffn_expert_w': _L1_ffn_in['expert_w'], 'L1_ffn_expert_b': _L1_ffn_in['expert_b'], 'L1_ffn_ln1_w': _L1_ffn_in['ln1_w'], 'L1_ffn_ln1_b': _L1_ffn_in['ln1_b'], 'L1_ffn_ln2_w': _L1_ffn_in['ln2_w'], 'L1_ffn_ln2_b': _L1_ffn_in['ln2_b'], 'L2_attn_Wqkv': _L2_attn_in['Wqkv'], 'L2_attn_Wout': _L2_attn_in['Wout'], 'L2_ffn_router_w': _L2_ffn_in['router_w'], 'L2_ffn_router_b': _L2_ffn_in['router_b'], 'L2_ffn_w1': _L2_ffn_in['w1'], 'L2_ffn_b1': _L2_ffn_in['b1'], 'L2_ffn_w2': _L2_ffn_in['w2'], 'L2_ffn_b2': _L2_ffn_in['b2'], 'L3_attn_Wq': _L3_attn_in['Wq'], 'L3_attn_bq': _L3_attn_in['bq'], 'L3_attn_Wk': _L3_attn_in['Wk'], 'L3_attn_bk': _L3_attn_in['bk'], 'L3_attn_Wv': _L3_attn_in['Wv'], 'L3_attn_bv': _L3_attn_in['bv'], 'L3_attn_Wo': _L3_attn_in['Wo'], 'L3_attn_bo': _L3_attn_in['bo'], 'L3_ffn_wqkv': _L3_ffn_in['wqkv'], 'L3_ffn_q_scale': _L3_ffn_in['q_scale'], 'L3_ffn_k_scale': _L3_ffn_in['k_scale'], 'L3_ffn_wo': _L3_ffn_in['wo'], 'L3_ffn_ln_g': _L3_ffn_in['ln_g'], 'L3_ffn_ln_b': _L3_ffn_in['ln_b'], 'L3_ffn_w1': _L3_ffn_in['w1'], 'L3_ffn_b1': _L3_ffn_in['b1'], 'L3_ffn_w2': _L3_ffn_in['w2'], 'L3_ffn_b2': _L3_ffn_in['b2']}
    _x0 = _d['L0_attn_x']
    _d['L0_attn_x'] = jax.random.normal(jax.random.fold_in(jax.random.key(seed), 1), (4, 512, 128), dtype=_x0.dtype)
    del _x0
    return _d

def reference(L0_attn_x, L0_attn_w_qkv, L0_attn_w_out, L0_attn_rel_emb, L0_ffn_input_patterns, L0_ffn_process_input_weights, L0_ffn_process_values, L0_ffn_output_input_weights, L0_ffn_output_patterns, L1_attn_Wq, L1_attn_Wk, L1_attn_Wv, L1_attn_Wo, L1_attn_Wb, L1_attn_bb, L1_ffn_in_proj_w, L1_ffn_in_proj_b, L1_ffn_out_proj_w, L1_ffn_out_proj_b, L1_ffn_gate_w, L1_ffn_gate_b, L1_ffn_expert_w, L1_ffn_expert_b, L1_ffn_ln1_w, L1_ffn_ln1_b, L1_ffn_ln2_w, L1_ffn_ln2_b, L2_attn_Wqkv, L2_attn_Wout, L2_ffn_router_w, L2_ffn_router_b, L2_ffn_w1, L2_ffn_b1, L2_ffn_w2, L2_ffn_b2, L3_attn_Wq, L3_attn_bq, L3_attn_Wk, L3_attn_bk, L3_attn_Wv, L3_attn_bv, L3_attn_Wo, L3_attn_bo, L3_ffn_wqkv, L3_ffn_q_scale, L3_ffn_k_scale, L3_ffn_wo, L3_ffn_ln_g, L3_ffn_ln_b, L3_ffn_w1, L3_ffn_b1, L3_ffn_w2, L3_ffn_b2):

    def _L0_attn_ref(x, w_qkv, w_out, rel_emb):
        import jax, jax.numpy as jnp
        import numpy as np
        import math
        NUM_HEADS = 16
        MAX_REL = 64
        LOCAL_WINDOW = 32
        B, L, D = x.shape
        H = NUM_HEADS
        hd = D // H
        qkv = (x @ w_qkv.T).reshape(B, L, 3, H, hd)
        q = jnp.transpose(qkv[:, :, 0], (0, 2, 1, 3))
        k = jnp.transpose(qkv[:, :, 1], (0, 2, 1, 3))
        v = jnp.transpose(qkv[:, :, 2], (0, 2, 1, 3))
        content = jnp.einsum('bhid,bhjd->bhij', q, k)
        qE = jnp.einsum('bhld,rd->bhlr', q, rel_emb)
        idx = jnp.arange(L)
        rel_idx = jnp.clip(idx[None, :] - idx[:, None], -MAX_REL, MAX_REL) + MAX_REL
        rel_scores = jnp.take_along_axis(qE, rel_idx[None, None, :, :], axis=3)
        scores = (content + rel_scores) / math.sqrt(hd)
        i = idx[:, None]
        j = idx[None, :]
        mask = (j > i) | (i - j >= LOCAL_WINDOW)
        scores = jnp.where(mask[None, None], -jnp.inf, scores)
        attn = jax.nn.softmax(scores, axis=-1)
        out = jnp.einsum('bhij,bhjd->bhid', attn, v)
        out = jnp.transpose(out, (0, 2, 1, 3)).reshape(B, L, D)
        return out @ w_out.T

    def _L0_ffn_ref(x, input_patterns, process_input_weights, process_values, output_input_weights, output_patterns):
        import jax, jax.numpy as jnp
        import numpy as np

        def gelu(x):
            return jax.nn.gelu(x, approximate=False)
        B, S, d_model = x.shape
        n_input = input_patterns.shape[0]
        n_process = process_input_weights.shape[0]
        n_output = output_input_weights.shape[0]
        k_input = max(n_input // 8, 64)
        k_process = max(n_process // 8, 32)
        k_output = max(n_output // 8, 64)
        input_acts = gelu(jnp.einsum('bsd,nd->bsn', x, input_patterns))
        input_acts_seq = input_acts.mean(axis=1)
        top_input_acts, top_input_idx = jax.lax.top_k(input_acts_seq, k_input)
        brow = jnp.arange(B)[:, None]
        input_repr = jnp.zeros((B, n_input), x.dtype).at[brow, top_input_idx].set(top_input_acts)
        process_acts = gelu(jnp.einsum('bn,pn->bp', input_repr, process_input_weights))
        top_process_acts, top_process_idx = jax.lax.top_k(process_acts, k_process)
        selected_process_values = process_values[top_process_idx]
        process_weights = jax.nn.softmax(top_process_acts, axis=-1)
        aggregated_value = jnp.einsum('bk,bkd->bd', process_weights, selected_process_values)
        output_acts_seq = gelu(jnp.einsum('bd,od->bo', aggregated_value, output_input_weights))
        top_output_acts, top_output_idx = jax.lax.top_k(output_acts_seq, k_output)
        selected_output_patterns = output_patterns[top_output_idx]
        out_per_seq = jnp.einsum('bk,bkm->bm', top_output_acts, selected_output_patterns)
        output = jnp.broadcast_to(out_per_seq[:, None, :], (B, S, d_model))
        return output

    def _L1_attn_ref(x, Wq, Wk, Wv, Wo, Wb, bb):
        import jax, jax.numpy as jnp
        import numpy as np
        H = 16
        EPS = 1e-12

        def _l2norm(t):
            n = jnp.sqrt(jnp.sum(t * t, axis=-1, keepdims=True))
            return t / jnp.maximum(n, EPS)
        B, L, Dm = x.shape
        Dh = Dm // H
        q = (x @ Wq).reshape(B, L, H, Dh)
        k = (x @ Wk).reshape(B, L, H, Dh)
        v = (x @ Wv).reshape(B, L, H, Dh)
        beta = jax.nn.sigmoid(x @ Wb + bb)
        q = _l2norm(q)
        k = _l2norm(k)
        scores = jnp.einsum('blhd,bthd->bhlt', q, k)
        scores = scores * beta.transpose(0, 2, 1)[:, :, None, :]
        mask = jnp.tril(jnp.ones((L, L), dtype=scores.dtype))
        scores = scores * mask
        out = jnp.einsum('bhlt,bthe->blhe', scores, v).reshape(B, L, Dm)
        return out @ Wo

    def _L1_ffn_ref(x, in_proj_w, in_proj_b, out_proj_w, out_proj_b, gate_w, gate_b, expert_w, expert_b, ln1_w, ln1_b, ln2_w, ln2_b):
        import jax, jax.numpy as jnp
        import numpy as np
        NUM_HEADS = 16
        TOP_K = 2
        ROPE_BASE = 10000.0
        LN_EPS = 1e-05

        def _rope_sin_cos(S, D, dtype):
            inv_freq = 1.0 / ROPE_BASE ** (jnp.arange(0, D, 2, dtype=jnp.float32) / D)
            freqs = jnp.arange(S, dtype=jnp.float32)[:, None] * inv_freq[None, :]
            sin = jnp.sin(freqs).astype(dtype)[None, :, None, :]
            cos = jnp.cos(freqs).astype(dtype)[None, :, None, :]
            return (sin, cos)

        def _apply_rope(x, sin, cos):
            x1, x2 = (x[..., 0::2], x[..., 1::2])
            r1 = x1 * cos - x2 * sin
            r2 = x1 * sin + x2 * cos
            return jnp.stack([r1, r2], axis=-1).reshape(x.shape)

        def _layer_norm(x, w, b):
            mu = jnp.mean(x, axis=-1, keepdims=True)
            var = jnp.mean(jnp.square(x - mu), axis=-1, keepdims=True)
            return (x - mu) * jax.lax.rsqrt(var + LN_EPS) * w + b
        B, S, E = x.shape
        H = NUM_HEADS
        D = E // H
        xh = x.reshape(B, S, H, D)
        sin, cos = _rope_sin_cos(S, D, x.dtype)
        q_in = _apply_rope(xh, sin, cos).reshape(B, S, E)
        k_in = q_in
        v_in = x
        Wq, Wk, Wv = jnp.split(in_proj_w, 3, axis=0)
        bq, bk, bv = jnp.split(in_proj_b, 3, axis=0)
        q = (q_in @ Wq.T + bq).reshape(B, S, H, D)
        k = (k_in @ Wk.T + bk).reshape(B, S, H, D)
        v = (v_in @ Wv.T + bv).reshape(B, S, H, D)
        scale = 1.0 / jnp.sqrt(jnp.asarray(D, dtype=x.dtype))
        scores = jnp.einsum('bqhd,bkhd->bhqk', q, k) * scale
        causal = jnp.tril(jnp.ones((S, S), dtype=bool))
        scores = jnp.where(causal[None, None], scores, jnp.asarray(-jnp.inf, dtype=scores.dtype))
        attn = jax.nn.softmax(scores, axis=-1)
        ctx = jnp.einsum('bhqk,bkhd->bqhd', attn, v).reshape(B, S, E)
        attn_out = ctx @ out_proj_w.T + out_proj_b
        x1 = _layer_norm(x + attn_out, ln1_w, ln1_b)
        gates = jax.nn.softmax(x1 @ gate_w.T + gate_b, axis=-1)
        _, top_idx = jax.lax.top_k(gates, TOP_K)
        top_gates = jnp.take_along_axis(gates, top_idx, axis=-1)
        expert_outputs = jnp.einsum('bsd,efd->bsef', x1, expert_w) + expert_b[None, None]
        sel = jnp.take_along_axis(expert_outputs, top_idx[..., None], axis=2)
        moe_out = jnp.sum(sel * top_gates[..., None], axis=2)
        return _layer_norm(x1 + moe_out, ln2_w, ln2_b)

    def _L2_attn_ref(x, Wqkv, Wout):
        import jax, jax.numpy as jnp
        import numpy as np
        N_HEADS = 16
        BLOCK_SIZE = 32

        def _rope(x):
            B, H, L, d = x.shape
            inv_freq = 1.0 / 10000.0 ** (jnp.arange(0, d, 2, dtype=jnp.float32) / d)
            t = jnp.arange(L, dtype=jnp.float32)[:, None] * inv_freq[None, :]
            cos, sin = (jnp.cos(t), jnp.sin(t))
            x1, x2 = (x[..., 0::2], x[..., 1::2])
            return jnp.concatenate([x1 * cos - x2 * sin, x2 * cos + x1 * sin], axis=-1)
        H, BS = (N_HEADS, BLOCK_SIZE)
        B, L, D = x.shape
        HD = D // H
        scale = HD ** (-0.5)
        nb = L // BS
        qkv = (x @ Wqkv.T).reshape(B, L, 3, H, HD).transpose(2, 0, 3, 1, 4)
        q, k, v = (qkv[0], qkv[1], qkv[2])
        q, k = (_rope(q), _rope(k))
        qb = q.reshape(B, H, nb, BS, HD)
        kb = k.reshape(B, H, nb, BS, HD)
        vb = v.reshape(B, H, nb, BS, HD)
        att = jnp.einsum('bhnqd,bhnkd->bhnqk', qb, kb) * scale
        causal = jnp.tril(jnp.ones((BS, BS), dtype=bool))
        att = jnp.where(causal, att, jnp.finfo(att.dtype).min)
        att = jax.nn.softmax(att, axis=-1)
        out = jnp.einsum('bhnqk,bhnkd->bhnqd', att, vb)
        out = out.reshape(B, H, L, HD).transpose(0, 2, 1, 3).reshape(B, L, D)
        return out @ Wout.T

    def _L2_ffn_ref(x, router_w, router_b, w1, b1, w2, b2):
        import jax, jax.numpy as jnp
        import numpy as np
        DIM = 128
        HIDDEN = 512
        E = 8
        B, S = (2, 512)
        logits = jnp.einsum('bsd,de->bse', x, router_w) + router_b
        probs = jax.nn.softmax(logits, axis=-1)
        top1 = jnp.argmax(probs, axis=-1)
        out = jnp.zeros_like(x)
        for i in range(E):
            h = jnp.einsum('bsd,df->bsf', x, w1[i]) + b1[i]
            a, g = jnp.split(h, 2, axis=-1)
            y = jnp.einsum('bsh,hd->bsd', a * jax.nn.sigmoid(g), w2[i]) + b2[i]
            out = out + jnp.where((top1 == i)[..., None], y, 0.0)
        return out

    def _L3_attn_ref(x, Wq, bq, Wk, bk, Wv, bv, Wo, bo):
        import jax, jax.numpy as jnp
        import numpy as np
        B, L, E, H = (2, 256, 128, 16)
        HD = E // H
        THETA = 10000.0

        def _rope_tables(seq_len, dim, dtype):
            inv_freq = 1.0 / THETA ** (jnp.arange(0, dim, 2, dtype=jnp.float32) / dim)
            freqs = jnp.arange(seq_len, dtype=jnp.float32)[:, None] * inv_freq[None, :]
            freqs = jnp.repeat(freqs, 2, axis=-1)
            return (jnp.cos(freqs).astype(dtype), jnp.sin(freqs).astype(dtype))

        def _rotate_half(x):
            x2 = x.reshape(*x.shape[:-1], -1, 2)
            x2 = jnp.stack([-x2[..., 1], x2[..., 0]], axis=-1)
            return x2.reshape(x.shape)

        def _apply_rope(x, cos, sin):
            return x * cos[None, None] + _rotate_half(x) * sin[None, None]
        b, l, e = x.shape
        q = (x @ Wq.T + bq).reshape(b, l, H, HD).transpose(0, 2, 1, 3)
        k = (x @ Wk.T + bk).reshape(b, l, H, HD).transpose(0, 2, 1, 3)
        v = (x @ Wv.T + bv).reshape(b, l, H, HD).transpose(0, 2, 1, 3)
        cos, sin = _rope_tables(l, HD, x.dtype)
        q = _apply_rope(q, cos, sin)
        k = _apply_rope(k, cos, sin)
        scale = 1.0 / np.sqrt(HD)
        scores = jnp.einsum('bhsd,bhed->bhse', q, k) * scale
        attn = jax.nn.softmax(scores, axis=-1)
        out = jnp.einsum('bhse,bhed->bhsd', attn, v)
        out = out.transpose(0, 2, 1, 3).reshape(b, l, e)
        return out @ Wo.T + bo

    def _L3_ffn_ref(x, wqkv, q_scale, k_scale, wo, ln_g, ln_b, w1, b1, w2, b2):
        import jax, jax.numpy as jnp
        import numpy as np
        DIM = 128
        DEPTH = 2
        HEADS = 8
        DIM_HEAD = 64
        WINDOW = 64
        INNER = HEADS * DIM_HEAD
        HID = int(DIM * 4 * 2 / 3)
        B, N = (2, 1024)
        QK_SCALE = 8.0

        def shift_token(t):
            t1, t2 = jnp.split(t, 2, axis=-1)
            t2 = jnp.pad(t2, ((0, 0), (1, 0), (0, 0)))[:, :-1]
            return jnp.concatenate([t1, t2], axis=-1)

        def l2norm(t):
            return t / jnp.clip(jnp.linalg.norm(t, axis=-1, keepdims=True), 1e-12)

        def rotate_half(x):
            x1, x2 = jnp.split(x, 2, axis=-1)
            return jnp.concatenate([-x2, x1], axis=-1)

        def rotary_xpos(q, k):
            n = q.shape[-2]
            half_idx = jnp.arange(0, DIM_HEAD, 2, dtype=jnp.float32)
            inv_freq = 1.0 / 10000.0 ** (half_idx / DIM_HEAD)
            t = jnp.arange(n, dtype=jnp.float32)
            freqs = t[:, None] * inv_freq[None, :]
            freqs = jnp.concatenate([freqs, freqs], axis=-1)
            base = (half_idx + 0.4 * DIM_HEAD) / (1.4 * DIM_HEAD)
            power = (t - n // 2) / float(WINDOW // 2)
            scale = base[None, :] ** power[:, None]
            scale = jnp.concatenate([scale, scale], axis=-1)
            cos, sin = (jnp.cos(freqs), jnp.sin(freqs))
            q = q * cos * scale + rotate_half(q) * sin * scale
            k = k * cos / scale + rotate_half(k) * sin / scale
            return (q, k)

        def local_attention(q, k, v):
            b, h, n, d = q.shape
            w = n // WINDOW
            bq = q.reshape(b, h, w, WINDOW, d) * QK_SCALE
            bk = k.reshape(b, h, w, WINDOW, d)
            bv = v.reshape(b, h, w, WINDOW, d)

            def look_around(t):
                p = jnp.pad(t, ((0, 0), (0, 0), (1, 0), (0, 0), (0, 0)))
                return jnp.concatenate([p[:, :, :w], p[:, :, 1:]], axis=3)
            bk, bv = (look_around(bk), look_around(bv))
            bt = jnp.arange(n).reshape(w, WINDOW)
            btp = jnp.pad(bt, ((1, 0), (0, 0)), constant_values=-1)
            btk = jnp.concatenate([btp[:w], btp[1:]], axis=1)
            sim = jnp.einsum('bhwid,bhwjd->bhwij', bq, bk)
            i = bt[:, :, None]
            j = btk[:, None, :]
            mask = (i < j) | (i > j + WINDOW) | (j == -1)
            sim = jnp.where(mask, -jnp.finfo(sim.dtype).max, sim)
            attn = jax.nn.softmax(sim, axis=-1)
            out = jnp.einsum('bhwij,bhwjd->bhwid', attn, bv)
            return out.reshape(b, h, n, d)

        def _layer(x, wqkv, qs, ksc, wo, lg, lb, w1, b1, w2, b2):
            b, n, _ = x.shape
            h = shift_token(x)
            qkv = h @ wqkv
            q, k, v = jnp.split(qkv, 3, axis=-1)
            to_heads = lambda t: t.reshape(b, n, HEADS, DIM_HEAD).transpose(0, 2, 1, 3)
            q, k, v = (to_heads(q), to_heads(k), to_heads(v))
            q = l2norm(q) * qs
            k = l2norm(k) * ksc
            q, k = rotary_xpos(q, k)
            o = local_attention(q, k, v)
            o = o.transpose(0, 2, 1, 3).reshape(b, n, INNER)
            x = x + o @ wo
            h = shift_token(x)
            mu = h.mean(-1, keepdims=True)
            var = h.var(-1, keepdims=True)
            h = (h - mu) / jnp.sqrt(var + 1e-05) * lg + lb
            h = h @ w1 + b1
            a, g = jnp.split(h, 2, axis=-1)
            h = a * jax.nn.gelu(g, approximate=False)
            x = x + h @ w2 + b2
            return x
        for l in range(DEPTH):
            x = _layer(x, wqkv[l], q_scale[l], k_scale[l], wo[l], ln_g[l], ln_b[l], w1[l], b1[l], w2[l], b2[l])
        return x
    x = L0_attn_x
    x = x + 0.5 * _L0_ffn_ref(_layernorm(x, axis=-1), L0_ffn_input_patterns, L0_ffn_process_input_weights, L0_ffn_process_values, L0_ffn_output_input_weights, L0_ffn_output_patterns)
    x = x + _L0_attn_ref(_layernorm(x, axis=-1), L0_attn_w_qkv, L0_attn_w_out, L0_attn_rel_emb)
    x = x + 0.5 * _L0_ffn_ref(_layernorm(x, axis=-1), L0_ffn_input_patterns, L0_ffn_process_input_weights, L0_ffn_process_values, L0_ffn_output_input_weights, L0_ffn_output_patterns)
    x = x + 0.5 * _L1_ffn_ref(_layernorm(x, axis=-1), L1_ffn_in_proj_w, L1_ffn_in_proj_b, L1_ffn_out_proj_w, L1_ffn_out_proj_b, L1_ffn_gate_w, L1_ffn_gate_b, L1_ffn_expert_w, L1_ffn_expert_b, L1_ffn_ln1_w, L1_ffn_ln1_b, L1_ffn_ln2_w, L1_ffn_ln2_b)
    x = x + _L1_attn_ref(_layernorm(x, axis=-1), L1_attn_Wq, L1_attn_Wk, L1_attn_Wv, L1_attn_Wo, L1_attn_Wb, L1_attn_bb)
    x = x + 0.5 * _L1_ffn_ref(_layernorm(x, axis=-1), L1_ffn_in_proj_w, L1_ffn_in_proj_b, L1_ffn_out_proj_w, L1_ffn_out_proj_b, L1_ffn_gate_w, L1_ffn_gate_b, L1_ffn_expert_w, L1_ffn_expert_b, L1_ffn_ln1_w, L1_ffn_ln1_b, L1_ffn_ln2_w, L1_ffn_ln2_b)
    x = x + 0.5 * _L2_ffn_ref(_layernorm(x, axis=-1), L2_ffn_router_w, L2_ffn_router_b, L2_ffn_w1, L2_ffn_b1, L2_ffn_w2, L2_ffn_b2)
    x = x + _L2_attn_ref(_layernorm(x, axis=-1), L2_attn_Wqkv, L2_attn_Wout)
    x = x + 0.5 * _L2_ffn_ref(_layernorm(x, axis=-1), L2_ffn_router_w, L2_ffn_router_b, L2_ffn_w1, L2_ffn_b1, L2_ffn_w2, L2_ffn_b2)
    x = x + 0.5 * _L3_ffn_ref(_layernorm(x, axis=-1), L3_ffn_wqkv, L3_ffn_q_scale, L3_ffn_k_scale, L3_ffn_wo, L3_ffn_ln_g, L3_ffn_ln_b, L3_ffn_w1, L3_ffn_b1, L3_ffn_w2, L3_ffn_b2)
    x = x + _L3_attn_ref(_layernorm(x, axis=-1), L3_attn_Wq, L3_attn_bq, L3_attn_Wk, L3_attn_bk, L3_attn_Wv, L3_attn_bv, L3_attn_Wo, L3_attn_bo)
    x = x + 0.5 * _L3_ffn_ref(_layernorm(x, axis=-1), L3_ffn_wqkv, L3_ffn_q_scale, L3_ffn_k_scale, L3_ffn_wo, L3_ffn_ln_g, L3_ffn_ln_b, L3_ffn_w1, L3_ffn_b1, L3_ffn_w2, L3_ffn_b2)
    return x

_drawn_inputs = setup_inputs


def setup_inputs(seed=0):
    import zlib

    import numpy as np

    out = dict(_drawn_inputs(seed))
    spreads = {'L1_attn_bb': (0.0, 0.69),
     'L1_ffn_in_proj_b': (0.0, 0.412),
     'L1_ffn_out_proj_b': (0.0, 0.1),
     'L1_ffn_gate_b': (0.0, 0.477),
     'L1_ffn_expert_b': (0.0, 0.511),
     'L1_ffn_ln1_w': (1.0, 0.2),
     'L1_ffn_ln1_b': (0.0, 0.1),
     'L1_ffn_ln2_w': (1.0, 0.2),
     'L1_ffn_ln2_b': (0.0, 0.1),
     'L3_ffn_q_scale': (1.0, 0.6),
     'L3_ffn_k_scale': (1.0, 0.6),
     'L3_ffn_ln_g': (1.0, 0.6),
     'L3_ffn_ln_b': (0.0, 0.8),
     'L3_ffn_b1': (0.0, 0.8),
     'L3_ffn_b2': (0.0, 0.664)}
    factors = {'L0_ffn_input_patterns': 8.0,
     'L0_ffn_process_input_weights': 8.0,
     'L0_ffn_process_values': 8.0,
     'L0_ffn_output_input_weights': 8.0,
     'L0_ffn_output_patterns': 8.0,
     'L1_attn_Wb': 4.594,
     'L1_ffn_in_proj_w': 8.0,
     'L1_ffn_out_proj_w': 3.12,
     'L2_attn_Wqkv': 5.374,
     'L2_attn_Wout': 5.313,
     'L2_ffn_b1': 7.351,
     'L2_ffn_b2': 4.412,
     'L3_attn_bq': 64.0,
     'L3_attn_bk': 64.0,
     'L3_attn_bv': 64.0,
     'L3_attn_bo': 64.0,
     'L3_ffn_wqkv': 4.317,
     'L3_ffn_wo': 4.247,
     'L3_ffn_w1': 8.0,
     'L3_ffn_w2': 8.0,
     'L3_attn_Wq': 8.0,
     'L3_attn_Wk': 8.0}
    for name, (base, spread) in spreads.items():
        noise = np.random.default_rng([zlib.crc32(name.encode()), seed]).standard_normal(out[name].shape)
        drawn = base * np.exp(spread * noise) if base else spread * noise
        out[name] = jnp.asarray(drawn.astype(out[name].dtype))
    for name, factor in factors.items():
        out[name] = (out[name] * factor).astype(out[name].dtype)
    return out
```

```python
from contextlib import ExitStack, contextmanager

import numpy as np

import concourse.bass as bass
from concourse import mybir

F32 = mybir.dt.float32
BF16 = mybir.dt.bfloat16
ALU = mybir.AluOpType
ACT = mybir.ActivationFunctionType
AX = mybir.AxisListType

P = 128
B, L, D = 4, 512, 128
NT = L // P
H, HD = 16, 8
NI, NP_, DV = 1024, 512, 64
KI, KP = NI // 8, NP_ // 8
NE = 8
HID2 = 512
NC2 = HID2 // P
DEPTH, LH, LHD, WIN = 2, 8, 64, 64
INNER = LH * LHD
HID3 = int(D * 4 * 2 / 3)
NC3 = -(-HID3 // P)
REL = 32
MAX_REL = 64
RW = 256
NEG = -1e30
EPS = 1e-5

LEVELS = [
    [("ident", P), ("tri", P), ("causalT", P), ("blockdiag", P), ("tri8", NE * NE), ("rope_cos", NT * 4),
     ("rope_sin", NT * 4), ("neg_half", NT), ("half", NT * 32), ("ones", P),
     ("rel_T", REL), ("ip_T", NI), ("pv", 4 * DV),
     ("l0_qkv", 3 * D), ("l0_out", D)],
    [("l1f_qkv", 3 * D), ("l1f_out", D), ("l1f_gate", NE), ("l1f_exp", NE * D),
     ("l1f_ln1_w", D), ("l1f_ln1_b", D), ("l1f_ln2_w", D), ("l1f_ln2_b", D),
     ("l1a_qkvb", 3 * D + H), ("l1a_out", D)],
    [("l2f_rw", NE), ("l2f_w1", NE * 2 * HID2), ("l2f_b1", NE * 2 * NC2), ("l2f_w2", NE * NC2 * D),
     ("l2a_qkv", 3 * D), ("l2a_out", D)],
    [("l3a_qkv", 3 * D), ("l3a_out", D), ("l3f_qkv", DEPTH * 3 * INNER), ("l3f_wo", DEPTH * 4 * D),
     ("l3f_w1", DEPTH * 2 * HID3), ("l3f_b1", DEPTH * 2 * NC3), ("l3f_w2", DEPTH * NC3 * D),
     ("l3f_lng", DEPTH), ("l3f_lnb", DEPTH)],
]
STREAM = [("piw_T", 8 * NP_), ("oiw_T", NI), ("op", 8 * D)]
ROWS = [[("l1f_exp_b", NE * D)], [("l2f_b2", NE * D)],
        [("l1f_qkv_b", 3 * D), ("l1f_out_b", D), ("l1f_gate_b", NE), ("l1a_bb", H), ("l2f_rb", NE)],
        [("l3a_qkv_b", 3 * D), ("l3a_out_b", D), ("l3f_b2", DEPTH * D)]]
ROW_COLS = NE * D


def offsets(fields):
    at, out = 0, {}
    for name, n in fields:
        out[name] = (at, n)
        at += n
    return out, at


class Buffers:

    def __init__(self):
        self.weight, self.row_at, self.rotary = {}, {}, {}


class Count:

    def __init__(self):
        self.n = 0

    def up(self, by=1):
        self.n += by
        return self.n


@contextmanager
def stage(nc, *names):
    sems = [nc.alloc_semaphore(f"{n}_{nc.next_id()}") for n in names]
    with nc.Block() as block:
        yield (block, *sems)
    nc.clear_and_free_semaphores(sems)
    nc.all_engine_barrier(sem_only=True)


def add_row(nc, m, out, name, a=0, b=None, **kw):
    p, at, n = m.row_at[name]
    b = n if b is None else b
    return nc.tensor.matmul(out, m.weight["ones"][p:p + 1, 0:P], m.rows[p:p + 1, at + a:at + b], start=False, stop=True, **kw)


def bank(m, i, n=512):
    return m.ps[:, i, 0:n]



def normalize(nc, m, src, dst, gain=None, shift=None, out_T=None, col_gain=None, col_shift=None):
    with stage(nc, "dve_step", "pow_done", "norm_ready", "turned") as (block, dve_step, pow_done, norm_ready, turned):
        @block.vector
        def _(dve):
            n = Count()
            for t in range(NT):
                nc.vector.bn_stats(m.st6[:, t, :], src[:, t, :]).then_inc(dve_step, 1)
                n.up()
            dve.wait_ge(dve_step, n.n)
            for t in range(NT):
                nc.vector.bn_aggr(m.mv[:, t, :], m.st6[:, t, :]).then_inc(dve_step, 1)
                n.up()
            dve.wait_ge(dve_step, n.n)
            nc.vector.tensor_scalar(m.ve[:, 0:NT], m.mv[:, :, 1], EPS, None, ALU.add).then_inc(dve_step, 1)
            dve.wait_ge(pow_done, 1)
            for t in range(NT):
                ins = nc.vector.tensor_scalar(dst[:, t, :], src[:, t, :], m.mv[:, t, 0:1], m.rstd[:, t:t + 1],
                                              ALU.subtract, ALU.mult)
                if gain is None:
                    ins.then_inc(norm_ready, 1)
                else:
                    ins.then_inc(dve_step, 1)
            n.up(NT + 1)
            if gain is not None:
                dve.wait_ge(dve_step, n.n)
                nc.vector.tensor_tensor(dst, dst, gain.unsqueeze(1).to_broadcast([P, NT, D]),
                                        ALU.mult).then_inc(dve_step, 1)
                dve.wait_ge(dve_step, n.up())
                nc.vector.tensor_tensor(dst, dst, shift.unsqueeze(1).to_broadcast([P, NT, D]),
                                        ALU.add).then_inc(norm_ready, NT)

        @block.gpsimd
        def _(pool):
            pool.wait_ge(dve_step, 2 * NT + 1)
            nc.gpsimd.tensor_tensor(m.rstd[:, 0:NT], m.ve[:, 0:NT], m.weight["neg_half"], ALU.pow).then_inc(pow_done, 1)

        if out_T is not None:
            @block.tensor
            def _(pe):
                for t in range(NT):
                    pe.wait_ge(norm_ready, NT if gain is not None else t + 1)
                    ins = nc.tensor.transpose(bank(m, 0)[:, t * P:(t + 1) * P], dst[:, t, :], m.weight["ident"])
                ins.then_inc(turned, 1)

            @block.scalar
            def _(act):
                act.wait_ge(turned, 1)
                if col_gain is None:
                    nc.scalar.copy(out_T, bank(m, 0))
                else:
                    nc.scalar.activation(out_T, bank(m, 0), ACT.Identity, bias=col_shift, scale=col_gain)


def turn_tok(nc, m, src, out_T):
    with stage(nc, "turned") as (block, turned):
        @block.tensor
        def _(pe):
            for t in range(NT):
                ins = nc.tensor.transpose(bank(m, 0)[:, t * P:(t + 1) * P], src[:, t, :], m.weight["ident"])
            ins.then_inc(turned, 1)

        @block.scalar
        def _(act):
            act.wait_ge(turned, 1)
            nc.scalar.copy(out_T, bank(m, 0))


def add_scaled(nc, m, dst, src, coef):
    with stage(nc) as (block,):
        @block.vector
        def _(dve):
            nc.vector.scalar_tensor_tensor(out=dst, in0=src, scalar=coef, in1=dst, op0=ALU.mult, op1=ALU.add)



def project_tok(nc, m, src_T, weight, width, row=None, row_at=0):
    with stage(nc) as (block,):
        @block.tensor
        def _(pe):
            for t in range(NT):
                nc.tensor.matmul(m.ps[:, t, 0:width], src_T[:, t * P:(t + 1) * P], weight,
                                 start=True, stop=True)
                if row is not None:
                    add_row(nc, m, m.ps[:, t, row_at:width], row, skip_group_check=True)


def turn_heads(nc, m):
    with stage(nc, "turned") as (block, turned):
        @block.tensor
        def _(pe):
            for s in range(2):
                for g in range(4):
                    for t in range(NT):
                        c = 16 * s + 4 * g
                        ins = nc.tensor.transpose(m.ps[:, 4 * s + g, t * P:(t + 1) * P],
                                                  m.pad[:, t, c:c + 4, :].rearrange("p a b -> p (a b)"), m.weight["ident"])
                    ins.then_inc(turned, 1)

        @block.scalar
        def _(act):
            for g in range(4):
                act.wait_ge(turned, g + 1)
                nc.scalar.copy(m.QP[:, g, :], bank(m, g))

        @block.vector
        def _(dve):
            for g in range(4):
                dve.wait_ge(turned, 4 + g + 1)
                nc.vector.tensor_copy(m.KP[:, g, :], bank(m, 4 + g))


def head_rows(m, h):
    r = slice(32 * (h % 4), 32 * (h % 4) + HD)
    return m.QP[r, h // 4, :], m.KP[r, h // 4, :]


def attend(nc, m, heads, hd, rows_of, first_tile, bias, rel_load=None):
    units = [(qt, h) for qt in range(NT) for h in range(heads)]
    U = len(units)
    NS, NTB = 3, 2

    def keys(qt):
        a, b = first_tile(qt)
        return a, b, (b - a) * P

    with stage(nc, "scores", "negmax", "exps", "turned", "pT_dve", "pT_act", "av", "o_done", "recip", "rel_in") as (
            block, scores, negmax, exps, turned, pT_dve, pT_act, av, o_done, recip, rel_in):

        if rel_load is not None:
            @block.sync
            def _(sp):
                for qt in range(NT):
                    if qt >= 1:
                        sp.wait_ge(scores, heads * qt)
                    sp.dma_start(m.rel[:, :, :], rel_load(qt)).then_inc(rel_in, 16)

        def evacuate(eng, copy, u, done):
            qt, _ = units[u]
            nk = keys(qt)[2]
            eng.wait_ge(turned, u + 1)
            if u >= NTB:
                eng.wait_ge(av, u - NTB + 1)
            copy(m.pT[:, u % NTB, 0:nk], bank(m, NS + u % NTB, nk)).then_inc(done, 1)

        @block.tensor
        def _(pe):
            for i in range(U + 3):
                if i < U:
                    qt, h = units[i]
                    a, b, nk = keys(qt)
                    q, k = rows_of(h)
                    if i >= NS:
                        pe.wait_ge(exps, i - NS + 1)
                    add = bias(qt, h, nk)
                    ins = nc.tensor.matmul(bank(m, i % NS, nk), q[:, qt * P:(qt + 1) * P], k[:, a * P:b * P],
                                           start=True, stop=True)
                    if add is not None:
                        if rel_load is not None and h == 0:
                            pe.wait_ge(rel_in, 16 * (qt + 1))
                        lhsT, rhs, at = add
                        ins = nc.tensor.matmul(m.ps[:, i % NS, at:nk], lhsT, rhs, start=False, stop=True,
                                               skip_group_check=True)
                    ins.then_inc(scores, 1)
                if 2 <= i < U + 2:
                    u = i - 2
                    nk = keys(units[u][0])[2]
                    pe.wait_ge(exps, u + 1)
                    if u >= NTB:
                        if u % 2 == 0:
                            pe.wait_ge(pT_dve, (u - NTB) // 2 + 1)
                        else:
                            pe.wait_ge(pT_act, (u - NTB) // 2 + 1)
                    for c in range(nk // P):
                        ins = nc.tensor.transpose(m.ps[:, NS + u % NTB, c * P:(c + 1) * P],
                                                  m.prob[:, u % NS, c * P:(c + 1) * P], m.weight["ident"])
                    ins.then_inc(turned, 1)
                if i >= 3:
                    u = i - 3
                    qt, h = units[u]
                    a, b, nk = keys(qt)
                    if u % 2 == 0:
                        pe.wait_ge(pT_dve, u // 2 + 1)
                    else:
                        pe.wait_ge(pT_act, u // 2 + 1)
                    if h == 0 and qt >= 2:
                        pe.wait_ge(o_done, qt - 1)
                    for c in range(b - a):
                        ins = nc.tensor.matmul(m.ps[:, 5 + qt % 2, h * hd:(h + 1) * hd],
                                               m.pT[:, u % NTB, c * P:(c + 1) * P],
                                               m.V[:, a + c, h * hd:(h + 1) * hd],
                                               start=(c == 0), stop=(c == b - a - 1))
                    ins.then_inc(av, 1)

        @block.scalar
        def _(act):
            for i in range(U + 2):
                if i < U:
                    qt, h = units[i]
                    nk = keys(qt)[2]
                    act.wait_ge(negmax, i + 1)
                    if i >= NS:
                        act.wait_ge(turned, i - NS + 1)
                    nc.scalar.activation(m.prob[:, i % NS, 0:nk], bank(m, i % NS, nk), ACT.Exp,
                                         bias=m.nm[:, i:i + 1], accum_out=m.sums[:, i:i + 1]).then_inc(exps, 1)
                if i >= 2 and (i - 2) % 2 == 1:
                    evacuate(act, nc.scalar.copy, i - 2, pT_act)

        @block.vector
        def _(dve):
            for i in range(U + 4):
                if i < U:
                    qt, h = units[i]
                    nk = keys(qt)[2]
                    dve.wait_ge(scores, i + 1)
                    nc.vector.tensor_reduce(m.nm[:, i:i + 1], bank(m, i % NS, nk), AX.X, ALU.max,
                                            negate=True).then_inc(negmax, 1)
                if 2 <= i < U + 2 and (i - 2) % 2 == 0:
                    evacuate(dve, nc.vector.tensor_copy, i - 2, pT_dve)
                if i >= 4 and (i - 3) % heads == 0:
                    qt = (i - 3) // heads - 1
                    u0 = qt * heads
                    dve.wait_ge(av, u0 + heads)
                    nc.vector.reciprocal(m.rsum[:, u0:u0 + heads], m.sums[:, u0:u0 + heads]).then_inc(recip, 1)
                    dve.wait_ge(recip, qt + 1)
                    nc.vector.tensor_tensor(
                        m.otok[:, qt, 0:heads * hd].rearrange("p (h e) -> p h e", h=heads),
                        m.ps[:, 5 + qt % 2, 0:heads * hd].rearrange("p (h e) -> p h e", h=heads),
                        m.rsum[:, u0:u0 + heads].unsqueeze(2).to_broadcast([P, heads, hd]),
                        ALU.mult).then_inc(o_done, 1)


def out_project(nc, m, weight, row, dst, add, chunks=1):
    with stage(nc, "turned", "oT_ready", "projected") as (block, turned, oT_ready, projected):
        @block.tensor
        def _(pe):
            for c in range(chunks):
                for t in range(NT):
                    ins = nc.tensor.transpose(m.ps[:, c, t * P:(t + 1) * P], m.otok[:, t, c * P:(c + 1) * P],
                                              m.weight["ident"])
                ins.then_inc(turned, 1)
            pe.wait_ge(oT_ready, chunks)
            for t in range(NT):
                for c in range(chunks):
                    ins = nc.tensor.matmul(m.ps[:, 4, t * P:(t + 1) * P], m.QP[:, c, t * P:(t + 1) * P],
                                           weight[:, c * D:(c + 1) * D], start=(c == 0),
                                           stop=(c == chunks - 1 and row is None))
                if row is not None:
                    ins = add_row(nc, m, m.ps[:, 4, t * P:(t + 1) * P], row)
            ins.then_inc(projected, 1)

        @block.scalar
        def _(act):
            for c in range(chunks):
                act.wait_ge(turned, c + 1)
                nc.scalar.copy(m.QP[:, c, :], bank(m, c)).then_inc(oT_ready, 1)

        @block.vector
        def _(dve):
            dve.wait_ge(projected, 1)
            nc.vector.tensor_tensor(dst.rearrange("p t d -> p (t d)"), bank(m, 4),
                                    add.rearrange("p t d -> p (t d)"), ALU.add)


def split_heads(nc, m, scale):
    with stage(nc, "v_out") as (block, v_out):
        @block.vector
        def _(dve):
            dve.wait_ge(v_out, 1)
            nc.vector.tensor_scalar(m.pad[:, :, 0:H, 0:HD], m.ps[:, 0:NT, 0:D].rearrange("p t (h e) -> p t h e", h=H),
                                    scale, None, ALU.mult)
            nc.vector.tensor_copy(m.pad[:, :, H:2 * H, 0:HD],
                                  m.ps[:, 0:NT, D:2 * D].rearrange("p t (h e) -> p t h e", h=H))

        @block.scalar
        def _(act):
            nc.scalar.copy(m.V[:, :, 0:D], m.ps[:, 0:NT, 2 * D:3 * D]).then_inc(v_out, 1)


def rope_heads(nc, m, scale, interleaved):
    def out_half(s, i):
        return m.pad[:, :, s, i:HD:2] if interleaved else m.pad[:, :, s, 4 * i:4 * i + 4]

    with stage(nc, "copied", "products", "rotated") as (block, copied, products, rotated):
        @block.scalar
        def _(act):
            nc.scalar.activation(m.raw[:, :, 0:D], m.ps[:, 0:NT, 0:D], ACT.Copy, scale=scale).then_inc(copied, 1)
            nc.scalar.copy(m.raw[:, :, D:2 * D], m.ps[:, 0:NT, D:2 * D]).then_inc(copied, 1)
            nc.scalar.copy(m.V[:, :, 0:D], m.ps[:, 0:NT, 2 * D:3 * D])

        @block.vector
        def _(dve):
            dve.wait_ge(copied, 2)
            x = m.raw.rearrange("p t (h e) -> p t h e", e=HD)
            x1, x2 = x[:, :, :, 0:HD:2], x[:, :, :, 1:HD:2]
            full = [P, NT, 2 * H, 4]
            c = m.weight["rope_cos"].rearrange("p (t i) -> p t i", t=NT).unsqueeze(2).to_broadcast(full)
            s = m.weight["rope_sin"].rearrange("p (t i) -> p t i", t=NT).unsqueeze(2).to_broadcast(full)
            tmp = [m.tmp[:, i, :].rearrange("p (t h e) -> p t h e", t=NT, e=4) for i in range(4)]
            nc.vector.tensor_tensor(tmp[0], x1, c, ALU.mult)
            nc.vector.tensor_tensor(tmp[1], x2, s, ALU.mult)
            nc.vector.tensor_tensor(tmp[2], x2, c, ALU.mult)
            nc.vector.tensor_tensor(tmp[3], x1, s, ALU.mult).then_inc(products, 1)
            dve.wait_ge(products, 1)
            nc.vector.tensor_tensor(out_half(slice(0, 2 * H), 0), tmp[0], tmp[1], ALU.subtract)
            nc.vector.tensor_tensor(out_half(slice(0, 2 * H), 1), tmp[2], tmp[3], ALU.add)


def causal_from(nc, m):
    return lambda qt, h, nk: (m.identb[:, :], m.negcausal[:, :], nk - P)



def rank_and_pick(nc, m, dve, step, n, vals, row, chunks, k, picked):
    N = chunks * P
    nc.vector.memset(m.cnt[:, 0:chunks, :], 0.0).then_inc(step, 1)
    dve.wait_ge(step, n.up())
    for c in range(chunks):
        v = vals[:, c:c + 1]
        a, b = c * P, (c + 1) * P
        if a > 0:
            nc.vector.tensor_scalar(m.junk[:, 0:a], row[:, 0:a], v, 0.0, ALU.is_ge, ALU.add,
                                    accum_out=m.cnt[:, c, 0:1]).then_inc(step, 1)
            n.up()
            dve.wait_ge(step, n.n)
        if b < N:
            nc.vector.tensor_scalar(m.junk[:, b:N], row[:, b:N], v, 0.0, ALU.is_gt, ALU.add,
                                    accum_out=m.cnt[:, c, 1:2]).then_inc(step, 1)
            n.up()
            dve.wait_ge(step, n.n)
        nc.vector.tensor_scalar(m.junk[:, a:b], row[:, a:b], v, 0.0, ALU.is_gt, ALU.add,
                                accum_out=m.cnt[:, c, 2:3]).then_inc(step, 1)
        n.up()
        dve.wait_ge(step, n.n)
        nc.vector.scalar_tensor_tensor(out=m.junk[:, a:b], in0=row[:, a:b], scalar=v, in1=m.weight["tri"],
                                       op0=ALU.is_equal, op1=ALU.mult, accum_out=m.cnt[:, c, 3:4]).then_inc(step, 1)
        n.up()
        dve.wait_ge(step, n.n)
    nc.vector.tensor_reduce(m.rank[:, 0:chunks], m.cnt[:, 0:chunks, :], AX.X, ALU.add).then_inc(step, 1)
    dve.wait_ge(step, n.up())
    nc.vector.tensor_scalar(picked, m.rank[:, 0:chunks], float(k), None, ALU.is_lt).then_inc(step, 1)
    dve.wait_ge(step, n.up())


def spread_row(nc, m, vals, chunks, first_bank):
    for c in range(chunks):
        ins = nc.tensor.transpose(m.ps[:, first_bank + c // 4, (c % 4) * P:(c % 4 + 1) * P],
                                  vals[:, c:c + 1].to_broadcast([P, P]), m.weight["ident"])
    return ins


def l0_ffn(nc, m):
    CI, CP = NI // P, NP_ // P
    normalize(nc, m, m.x, m.h, out_T=m.hT)
    with stage(nc, "acts_in", "acts_out", "row", "picked", "proc_in", "proc_out", "shifted", "agg_in", "agg",
               "outs_in", "outs", "mixed", "step", "piw_in", "out_w_in") as (
            block, acts_in, acts_out, row, picked, proc_in, proc_out, shifted, agg_in, agg, outs_in, outs, mixed, step,
            piw_in, out_w_in):
        ip = m.weight["ip_T"]
        piw = m.piw.rearrange("p (c n) -> p c n", c=CI)
        pv = m.weight["pv"].rearrange("p (c n) -> p c n", c=CP)
        oiw = m.oiw
        op = m.op.rearrange("p (c n) -> p c n", c=CI)
        flat2 = m.ps[:, 4:6, :].rearrange("p a b -> p (a b)")

        @block.sync
        def _(sp):
            sp.dma_start(m.piw, m.stream[:, 0:8 * NP_]).then_inc(piw_in, 16)
            sp.dma_start(m.QP[:, :, :].rearrange("p a b -> p (a b)"), m.stream[:, 8 * NP_:8 * NP_ + 2 * NI]).then_inc(out_w_in, 16)

        @block.tensor
        def _(pe):
            for c in range(CI):
                if c >= 4:
                    pe.wait_ge(acts_out, c - 3)
                nc.tensor.matmul(bank(m, c % 4), ip[:, c * P:(c + 1) * P], m.hT[:, :],
                                 start=True, stop=True).then_inc(acts_in, 1)
            pe.wait_ge(acts_out, CI)
            spread_row(nc, m, m.acc, CI, 4).then_inc(row, 1)
            pe.wait_ge(picked, 1)
            pe.wait_ge(piw_in, 16)
            for pc in range(CP):
                for c in range(CI):
                    ins = nc.tensor.matmul(m.ps[:, 6, pc:pc + 1], piw[:, c, pc * P:(pc + 1) * P], m.wv[:, c:c + 1],
                                           start=(c == 0), stop=(c == CI - 1))
            ins.then_inc(proc_in, 1)
            pe.wait_ge(proc_out, 1)
            spread_row(nc, m, m.acc, CP, 4).then_inc(row, 1)
            pe.wait_ge(picked, 2)
            for c in range(CP):
                nc.tensor.matmul(m.ps[0:DV, 7, 0:1], pv[:, c, :], m.wv[:, c:c + 1], start=(c == 0), stop=(c == CP - 1))
            for c in range(CP):
                ins = nc.tensor.matmul(m.ps[0:DV, 7, 1:2], m.weight["ones"][:, 0:DV], m.wv[:, c:c + 1],
                                       start=(c == 0), stop=(c == CP - 1))
            ins.then_inc(agg_in, 1)
            pe.wait_ge(agg, 1)
            pe.wait_ge(out_w_in, 16)
            for c in range(CI):
                ins = nc.tensor.matmul(m.ps[:, 6, c:c + 1], oiw[0:DV, c * P:(c + 1) * P], m.aggv[0:DV, 0:1],
                                       start=True, stop=True)
            ins.then_inc(outs_in, 1)
            pe.wait_ge(outs, 1)
            spread_row(nc, m, m.acc, CI, 4).then_inc(row, 1)
            pe.wait_ge(picked, 3)
            for c in range(CI):
                ins = nc.tensor.matmul(bank(m, 7, D), m.wv[:, c:c + 1].to_broadcast([P, P]), op[:, c, :],
                                       start=(c == 0), stop=(c == CI - 1))
            ins.then_inc(mixed, 1)

        @block.scalar
        def _(act):
            for c in range(CI):
                act.wait_ge(acts_in, c + 1)
                if c >= 2:
                    act.wait_ge(acts_out, c - 1)
                nc.scalar.activation(m.actj[:, c % 2, :], bank(m, c % 4), ACT.Gelu,
                                     accum_out=m.acc[:, c:c + 1]).then_inc(acts_out, 1)
            act.wait_ge(proc_in, 1)
            nc.scalar.activation(m.acc[:, 0:CP], m.ps[:, 6, 0:CP], ACT.Gelu).then_inc(proc_out, 1)
            act.wait_ge(shifted, 1)
            nc.scalar.activation(m.ex[:, 0:CP], m.acc[:, 0:CP], ACT.Exp, bias=m.nm[:, 0:1]).then_inc(shifted, 1)
            act.wait_ge(outs_in, 1)
            nc.scalar.activation(m.acc[:, 0:CI], m.ps[:, 6, 0:CI], ACT.Gelu).then_inc(outs, 1)

        @block.vector
        def _(dve):
            n = Count()
            dve.wait_ge(row, 1)
            rank_and_pick(nc, m, dve, step, n, m.acc, flat2, CI, KI, m.pick[:, 0:CI])
            nc.vector.scalar_tensor_tensor(out=m.wv[:, 0:CI], in0=m.acc[:, 0:CI], scalar=1.0 / L, in1=m.pick[:, 0:CI],
                                           op0=ALU.mult, op1=ALU.mult).then_inc(picked, 1)
            dve.wait_ge(row, 2)
            nc.vector.tensor_reduce(m.nm[:, 0:1], bank(m, 4), AX.X, ALU.max, negate=True).then_inc(shifted, 1)
            rank_and_pick(nc, m, dve, step, n, m.acc, bank(m, 4), CP, KP, m.pick[:, 0:CP])
            dve.wait_ge(shifted, 2)
            nc.vector.tensor_tensor(m.wv[:, 0:CP], m.ex[:, 0:CP], m.pick[:, 0:CP], ALU.mult).then_inc(picked, 1)
            dve.wait_ge(agg_in, 1)
            nc.vector.reciprocal(m.aggv[0:DV, 1:2], m.ps[0:DV, 7, 1:2]).then_inc(step, 1)
            dve.wait_ge(step, n.up())
            nc.vector.tensor_tensor(m.aggv[0:DV, 0:1], m.ps[0:DV, 7, 0:1], m.aggv[0:DV, 1:2], ALU.mult).then_inc(agg, 1)
            dve.wait_ge(row, 3)
            rank_and_pick(nc, m, dve, step, n, m.acc, flat2, CI, KI, m.pick[:, 0:CI])
            nc.vector.tensor_tensor(m.wv[:, 0:CI], m.acc[:, 0:CI], m.pick[:, 0:CI], ALU.mult).then_inc(picked, 1)
            dve.wait_ge(mixed, 1)
            for t in range(NT):
                nc.vector.scalar_tensor_tensor(out=m.x[:, t, :], in0=bank(m, 7, D), scalar=0.5, in1=m.x[:, t, :],
                                               op0=ALU.mult, op1=ALU.add)


def l0_attn(nc, m):
    normalize(nc, m, m.x, m.h, out_T=m.hT)
    project_tok(nc, m, m.hT, m.weight["l0_qkv"], 3 * D)
    split_heads(nc, m, HD ** -0.5)
    turn_heads(nc, m)
    with stage(nc, "rel_ready", "rel_out", "stored") as (block, rel_ready, rel_out, stored):
        @block.tensor
        def _(pe):
            for j in range(4):
                for qt in range(NT):
                    for g in range(4):
                        r = slice(32 * j, 32 * j + HD)
                        at = (4 * qt + g) * REL
                        ins = nc.tensor.matmul(m.ps[:, j, at:at + REL], m.QP[r, g, qt * P:(qt + 1) * P],
                                               m.weight["rel_T"][r, :], start=True, stop=True)
                ins.then_inc(rel_ready, 1)

        @block.scalar
        def _(act):
            for j in range(4):
                act.wait_ge(rel_ready, j + 1)
                nc.scalar.copy(m.actj2.rearrange("p q (g j r) -> p q g j r", g=4, j=4)[:, :, :, j, :],
                               bank(m, j).rearrange("p (q g r) -> p q g r", q=NT, g=4)).then_inc(rel_out, 1)

        @block.sync
        def _(sp):
            sp.wait_ge(rel_out, 4)
            for qt in range(NT):
                base = RW + qt * H * P * RW
                dst = m.shear[base:base + H * P * RW].rearrange("(h i w) -> i h w", h=H, w=RW)[:, :, 0:REL]
                sp.dma_start(dst, m.actj2[:, qt, :].rearrange("p (h r) -> p h r", h=H)).then_inc(stored, 16)
            sp.wait_ge(stored, 16 * NT)

    def rel_load(qt):
        return bass.AP(tensor=m.shear.tensor, offset=RW + qt * H * P * RW - (P - REL + 1),
                       ap=[[RW - 1, P], [P * RW, H], [1, 2 * P]])

    def bias(qt, h, nk):
        return (m.weight["ident"], m.rel[:, h, 2 * P - nk:2 * P], 0)

    attend(nc, m, H, HD, lambda h: head_rows(m, h), lambda qt: (max(qt - 1, 0), qt + 1), bias, rel_load)
    out_project(nc, m, m.weight["l0_out"], None, m.x, m.x)



def gates(nc, m, src_T, weight, row, k, keep_probability):
    with stage(nc, "logits", "shifted", "exped", "step") as (block, logits, shifted, exped, step):
        lg = m.ps[:, 0, 0:NT * NE].rearrange("p (t e) -> p t e", t=NT)
        full = [P, NT, NE]

        @block.tensor
        def _(pe):
            for t in range(NT):
                nc.tensor.matmul(lg[:, t, :], src_T[:, t * P:(t + 1) * P], weight, start=True, stop=False)
                ins = add_row(nc, m, lg[:, t, :], row)
            ins.then_inc(logits, 1)

        @block.scalar
        def _(act):
            act.wait_ge(shifted, 1)
            nc.scalar.activation(m.gp[:, :, :], m.gl[:, :, :], ACT.Exp).then_inc(exped, 1)

        @block.vector
        def _(dve):
            n = Count()
            dve.wait_ge(logits, 1)
            nc.vector.tensor_reduce(m.g4[:, 0:NT], lg, AX.X, ALU.max).then_inc(step, 1)
            dve.wait_ge(step, n.up())
            nc.vector.tensor_tensor(m.gl[:, :, :], lg, m.g4[:, 0:NT].unsqueeze(2).to_broadcast(full),
                                    ALU.subtract).then_inc(shifted, 1)
            dve.wait_ge(exped, 1)
            nc.vector.tensor_reduce(m.g4[:, NT:2 * NT], m.gp[:, :, :], AX.X, ALU.add).then_inc(step, 1)
            dve.wait_ge(step, n.up())
            nc.vector.reciprocal(m.g4[:, 2 * NT:3 * NT], m.g4[:, NT:2 * NT]).then_inc(step, 1)
            dve.wait_ge(step, n.up())
            nc.vector.tensor_tensor(m.gl[:, :, :], m.gp[:, :, :],
                                    m.g4[:, 2 * NT:3 * NT].unsqueeze(2).to_broadcast(full), ALU.mult).then_inc(step, 1)
            dve.wait_ge(step, n.up())
            wide = [P, NT, NE, NE]
            other, own = m.gl[:, :, :].unsqueeze(2).to_broadcast(wide), m.gl[:, :, :].unsqueeze(3).to_broadcast(wide)
            nc.vector.tensor_tensor(m.cmp[:, 0], other, own, ALU.is_gt).then_inc(step, 1)
            nc.vector.tensor_tensor(m.cmp[:, 1], other, own, ALU.is_equal).then_inc(step, 1)
            dve.wait_ge(step, n.up(2))
            tri8 = m.weight["tri8"].unsqueeze(1).to_broadcast([P, NT, NE * NE])
            nc.vector.tensor_tensor(m.cmp[:, 1].rearrange("p t a b -> p t (a b)"),
                                    m.cmp[:, 1].rearrange("p t a b -> p t (a b)"), tri8, ALU.mult).then_inc(step, 1)
            dve.wait_ge(step, n.up())
            nc.vector.tensor_tensor(m.cmp[:, 0], m.cmp[:, 0], m.cmp[:, 1], ALU.add).then_inc(step, 1)
            dve.wait_ge(step, n.up())
            nc.vector.tensor_reduce(m.grank[:, :, :], m.cmp[:, 0], AX.X, ALU.add).then_inc(step, 1)
            dve.wait_ge(step, n.up())
            if keep_probability:
                nc.vector.scalar_tensor_tensor(out=m.sel[:, :, :], in0=m.grank[:, :, :], scalar=float(k),
                                               in1=m.gl[:, :, :], op0=ALU.is_lt, op1=ALU.mult)
            else:
                nc.vector.tensor_scalar(m.sel[:, :, :], m.grank[:, :, :], float(k), None, ALU.is_lt)



def l1_ffn(nc, m):
    normalize(nc, m, m.x, m.h)
    with stage(nc, "products") as (block, products):
        @block.vector
        def _(dve):
            x = m.h[:, :, :].rearrange("p t (h e) -> p t h e", e=HD)
            o = m.y[:, :, :].rearrange("p t (h e) -> p t h e", e=HD)
            x1, x2 = x[:, :, :, 0:HD:2], x[:, :, :, 1:HD:2]
            full = [P, NT, H, 4]
            c = m.weight["rope_cos"].rearrange("p (t i) -> p t i", t=NT).unsqueeze(2).to_broadcast(full)
            s = m.weight["rope_sin"].rearrange("p (t i) -> p t i", t=NT).unsqueeze(2).to_broadcast(full)
            tmp = [m.tmp[:, i, 0:NT * H * 4].rearrange("p (t h e) -> p t h e", t=NT, e=4) for i in range(4)]
            nc.vector.tensor_tensor(tmp[0], x1, c, ALU.mult)
            nc.vector.tensor_tensor(tmp[1], x2, s, ALU.mult)
            nc.vector.tensor_tensor(tmp[2], x1, s, ALU.mult)
            nc.vector.tensor_tensor(tmp[3], x2, c, ALU.mult).then_inc(products, 1)
            dve.wait_ge(products, 1)
            nc.vector.tensor_tensor(o[:, :, :, 0:HD:2], tmp[0], tmp[1], ALU.subtract)
            nc.vector.tensor_tensor(o[:, :, :, 1:HD:2], tmp[2], tmp[3], ALU.add)
    turn_tok(nc, m, m.y, m.hT)
    turn_tok(nc, m, m.h, m.hT2)
    with stage(nc) as (block,):
        @block.tensor
        def _(pe):
            qkv = m.weight["l1f_qkv"]
            for t in range(NT):
                for src, a, b in ((m.hT, 0, 2 * D), (m.hT2, 2 * D, 3 * D)):
                    nc.tensor.matmul(m.ps[:, t, a:b], src[:, t * P:(t + 1) * P], qkv[:, a:b], start=True, stop=False)
                    add_row(nc, m, m.ps[:, t, a:b], "l1f_qkv_b", a, b)
    split_heads(nc, m, HD ** -0.5)
    turn_heads(nc, m)
    attend(nc, m, H, HD, lambda h: head_rows(m, h), lambda qt: (0, qt + 1), causal_from(nc, m))
    out_project(nc, m, m.weight["l1f_out"], "l1f_out_b", m.y, m.h)
    normalize(nc, m, m.y, m.y, gain=m.weight["l1f_ln1_w"], shift=m.weight["l1f_ln1_b"], out_T=m.hT)
    gates(nc, m, m.hT, m.weight["l1f_gate"], "l1f_gate_b", 2, True)
    with stage(nc, "experts", "summed") as (block, experts, summed):
        HW = NE * D // 2

        @block.tensor
        def _(pe):
            for t in range(NT):
                for s in range(2):
                    u = 2 * t + s
                    if u >= 4:
                        pe.wait_ge(summed, NE // 2 * (u - 3))
                    nc.tensor.matmul(bank(m, u % 4), m.hT[:, t * P:(t + 1) * P],
                                     m.weight["l1f_exp"][:, s * HW:(s + 1) * HW], start=True, stop=False)
                    add_row(nc, m, bank(m, u % 4), "l1f_exp_b", s * HW, (s + 1) * HW).then_inc(experts, 1)

        @block.vector
        def _(dve):
            for t in range(NT):
                for e in range(NE):
                    u = 2 * t + e // 4
                    if e % 4 == 0:
                        dve.wait_ge(experts, u + 1)
                    if e > 0:
                        dve.wait_ge(summed, NE * t + e)
                    nc.vector.scalar_tensor_tensor(out=m.y[:, t, :], in0=m.ps[:, u % 4, (e % 4) * D:(e % 4 + 1) * D],
                                                   scalar=m.sel[:, t, e:e + 1], in1=m.y[:, t, :],
                                                   op0=ALU.mult, op1=ALU.add).then_inc(summed, 1)
    normalize(nc, m, m.y, m.y, gain=m.weight["l1f_ln2_w"], shift=m.weight["l1f_ln2_b"])
    add_scaled(nc, m, m.x[:, :, :], m.y[:, :, :], 0.5)


def l1_attn(nc, m):
    normalize(nc, m, m.x, m.h, out_T=m.hT)
    project_tok(nc, m, m.hT, m.weight["l1a_qkvb"], 3 * D + H, "l1a_bb", 3 * D)
    with stage(nc, "squared", "summed", "rooted", "beta_ready", "step", "qk_ready") as (
            block, squared, summed, rooted, beta_ready, step, qk_ready):
        @block.scalar
        def _(act):
            nc.scalar.activation(m.raw[:, :, :], m.ps[:, 0:NT, 0:2 * D], ACT.Square).then_inc(squared, 1)
            nc.scalar.activation(m.beta[:, :, :], m.ps[:, 0:NT, 3 * D:3 * D + H], ACT.Sigmoid).then_inc(beta_ready, 1)

        @block.gpsimd
        def _(pool):
            pool.wait_ge(summed, 1)
            nc.gpsimd.tensor_tensor(m.ss[:, 1, :], m.ss[:, 0, :], m.weight["half"], ALU.pow).then_inc(rooted, 1)
            pool.wait_ge(qk_ready, 1)
            nc.gpsimd.tensor_copy(m.pad[:, :, :, 0:HD], m.qk[:, :, :].rearrange("p t (h e) -> p t h e", e=HD))

        @block.vector
        def _(dve):
            dve.wait_ge(squared, 1)
            nc.vector.tensor_reduce(m.ss[:, 0, :].rearrange("p (t h) -> p t h", t=NT),
                                    m.raw[:, :, :].rearrange("p t (h e) -> p t h e", e=HD),
                                    AX.X, ALU.add).then_inc(summed, 1)
            dve.wait_ge(beta_ready, 1)
            dve.wait_ge(rooted, 1)
            nc.vector.tensor_scalar(m.ss[:, 0, :], m.ss[:, 1, :], 1e-12, None, ALU.max).then_inc(step, 1)
            dve.wait_ge(step, 1)
            nc.vector.reciprocal(m.ss[:, 1, :], m.ss[:, 0, :]).then_inc(step, 1)
            dve.wait_ge(step, 2)
            nc.vector.tensor_tensor(m.qk[:, :, :].rearrange("p t (h e) -> p t h e", e=HD),
                                    m.ps[:, 0:NT, 0:2 * D].rearrange("p t (h e) -> p t h e", e=HD),
                                    m.ss[:, 1, :].rearrange("p (t h) -> p t h", t=NT).unsqueeze(3).to_broadcast(
                                        [P, NT, 2 * H, HD]), ALU.mult).then_inc(qk_ready, 1)
            nc.vector.tensor_tensor(m.V[:, :, 0:D].rearrange("p t (h e) -> p t h e", e=HD),
                                    m.ps[:, 0:NT, 2 * D:3 * D].rearrange("p t (h e) -> p t h e", e=HD),
                                    m.beta[:, :, :].unsqueeze(3).to_broadcast([P, NT, H, HD]), ALU.mult)
    turn_heads(nc, m)
    turn_tok(nc, m, m.qk[:, :, 0:D], m.hT)
    with stage(nc, "states", "state_ready", "scores", "masked", "av", "o_done") as (
            block, states, state_ready, scores, masked, av, o_done):
        units = [(t, j) for t in range(NT) for j in range(4)]
        U = len(units)

        @block.tensor
        def _(pe):
            for t in range(1, NT):
                for s in range(t):
                    ins = nc.tensor.matmul(m.ps[:, 0, t * P:(t + 1) * P], m.qk[:, s, D:2 * D], m.V[:, s, 0:D],
                                           start=(s == 0), stop=(s == t - 1))
            ins.then_inc(states, 1)
            for i in range(U + 2):
                if i < U:
                    t, j = units[i]
                    if i >= 3:
                        pe.wait_ge(masked, i - 2)
                    for g in range(4):
                        q, k = head_rows(m, 4 * g + j)
                        ins = nc.tensor.matmul(m.ps[:, 1 + i % 3, g * P:(g + 1) * P], k[:, t * P:(t + 1) * P],
                                               q[:, t * P:(t + 1) * P], start=True, stop=True)
                    ins.then_inc(scores, 1)
                if i >= 2:
                    t, j = units[i - 2]
                    if j == 0:
                        if t >= 2:
                            pe.wait_ge(o_done, t - 1)
                        if t > 0:
                            pe.wait_ge(state_ready, 1)
                            nc.tensor.matmul(m.ps[:, 5 + t % 2, 0:D], m.hT[:, t * P:(t + 1) * P], m.state[:, t, :],
                                             start=True, stop=True, skip_group_check=True)
                    pe.wait_ge(masked, i - 1)
                    for g in range(4):
                        h = 4 * g + j
                        ins = nc.tensor.matmul(m.ps[:, 5 + t % 2, h * HD:(h + 1) * HD],
                                               m.prob[:, (i - 2) % 3, g * P:(g + 1) * P],
                                               m.V[:, t, h * HD:(h + 1) * HD], start=(t == 0), stop=True,
                                               skip_group_check=True)
                    ins.then_inc(av, 1)

        @block.vector
        def _(dve):
            dve.wait_ge(states, 1)
            nc.vector.tensor_tensor(m.state[:, 1:NT, :], m.ps[:, 0, P:NT * P].rearrange("p (t d) -> p t d", d=D),
                                    m.weight["blockdiag"].unsqueeze(1).to_broadcast([P, NT - 1, D]),
                                    ALU.mult).then_inc(state_ready, 1)
            for i in range(U):
                dve.wait_ge(scores, i + 1)
                if i >= 3:
                    dve.wait_ge(av, i - 2)
                nc.vector.tensor_tensor(m.prob[:, i % 3, :].rearrange("p (j q) -> p j q", j=4),
                                        m.ps[:, 1 + i % 3, :].rearrange("p (j q) -> p j q", j=4),
                                        m.weight["causalT"].unsqueeze(1).to_broadcast([P, 4, P]),
                                        ALU.mult).then_inc(masked, 1)

        @block.scalar
        def _(act):
            for t in range(NT):
                act.wait_ge(av, 4 * (t + 1))
                nc.scalar.copy(m.otok[:, t, 0:D], m.ps[:, 5 + t % 2, 0:D]).then_inc(o_done, 1)
    out_project(nc, m, m.weight["l1a_out"], None, m.x, m.x)



def l2_ffn(nc, m):
    normalize(nc, m, m.x, m.h, out_T=m.hT)
    gates(nc, m, m.hT, m.weight["l2f_rw"], "l2f_rb", 1, False)
    w1 = m.weight["l2f_w1"].rearrange("p (e f) -> p e f", e=NE)
    b1 = m.weight["l2f_b1"].rearrange("p (e c) -> p e c", e=NE)
    w2 = m.weight["l2f_w2"].rearrange("p (e c d) -> p e c d", e=NE, c=NC2)
    units = [(e, c) for e in range(NE) for c in range(NC2)]
    U = len(units)
    LAG = 2
    with stage(nc, "pair", "sig", "gated", "mixed", "summed", "zeroed") as (
            block, pair, sig, gated, mixed, summed, zeroed):
        @block.tensor
        def _(pe):
            def mix(e):
                pe.wait_ge(gated, NC2 * (e + 1))
                if e >= 2:
                    pe.wait_ge(summed, NT * (e - 1))
                for t in range(NT):
                    for c in range(NC2):
                        nc.tensor.matmul(m.ps[:, 4 + e % 2, t * P:(t + 1) * P],
                                         m.act[:, e % 2, c, t * P:(t + 1) * P], w2[:, e, c, :],
                                         start=(c == 0), stop=False)
                    ins = add_row(nc, m, m.ps[:, 4 + e % 2, t * P:(t + 1) * P], "l2f_b2", e * D, (e + 1) * D)
                ins.then_inc(mixed, 1)

            for u, (e, c) in enumerate(units):
                if u >= 2:
                    pe.wait_ge(gated, u - 1)
                for s in range(2):
                    at = s * HID2 + c * P
                    ins = nc.tensor.matmul(bank(m, 2 * (u % 2) + s), w1[:, e, at:at + P], m.hT[:, :],
                                           start=True, stop=True)
                ins.then_inc(pair, 1)
                if e >= 1 and c == LAG:
                    mix(e - 1)
            mix(NE - 1)

        @block.scalar
        def _(act):
            for u, (e, c) in enumerate(units):
                act.wait_ge(pair, u + 1)
                if u >= 2:
                    act.wait_ge(gated, u - 1)
                nc.scalar.activation(m.actj[:, u % 2, :], bank(m, 2 * (u % 2) + 1), ACT.Sigmoid,
                                     bias=b1[:, e, NC2 + c:NC2 + c + 1]).then_inc(sig, 1)

        @block.vector
        def _(dve):
            def weigh(e):
                dve.wait_ge(mixed, e + 1)
                if e > 0:
                    dve.wait_ge(summed, NT * e)
                for t in range(NT):
                    nc.vector.scalar_tensor_tensor(out=m.y[:, t, :], in0=m.ps[:, 4 + e % 2, t * P:(t + 1) * P],
                                                   scalar=m.sel[:, t, e:e + 1], in1=m.y[:, t, :],
                                                   op0=ALU.mult, op1=ALU.add).then_inc(summed, 1)

            nc.vector.memset(m.y[:, :, :], 0.0).then_inc(zeroed, 1)
            dve.wait_ge(zeroed, 1)
            for u, (e, c) in enumerate(units):
                dve.wait_ge(sig, u + 1)
                if c == 0 and e >= 2:
                    dve.wait_ge(mixed, e - 1)
                nc.vector.scalar_tensor_tensor(out=m.act[:, e % 2, c, :], in0=bank(m, 2 * (u % 2)),
                                               scalar=b1[:, e, c:c + 1], in1=m.actj[:, u % 2, :],
                                               op0=ALU.add, op1=ALU.mult).then_inc(gated, 1)
                if c == NC2 - 1 and e >= 1:
                    weigh(e - 1)
            weigh(NE - 1)
            dve.wait_ge(summed, NT * NE)
            nc.vector.scalar_tensor_tensor(out=m.x[:, :, :], in0=m.y[:, :, :], scalar=0.5, in1=m.x[:, :, :],
                                           op0=ALU.mult, op1=ALU.add)


def l2_attn(nc, m):
    normalize(nc, m, m.x, m.h, out_T=m.hT)
    project_tok(nc, m, m.hT, m.weight["l2a_qkv"], 3 * D)
    rope_heads(nc, m, HD ** -0.5, interleaved=False)
    turn_heads(nc, m)
    attend(nc, m, H, HD, lambda h: head_rows(m, h), lambda qt: (qt, qt + 1),
           lambda qt, h, nk: (m.identb[:, :], m.negblock[:, :], 0))
    out_project(nc, m, m.weight["l2a_out"], None, m.x, m.x)



def l3_attn(nc, m):
    normalize(nc, m, m.x, m.h, out_T=m.hT)
    project_tok(nc, m, m.hT, m.weight["l3a_qkv"], 3 * D, "l3a_qkv_b", 0)
    rope_heads(nc, m, HD ** -0.5, interleaved=True)
    turn_heads(nc, m)
    attend(nc, m, H, HD, lambda h: head_rows(m, h), lambda qt: (0, NT), lambda qt, h, nk: None)
    out_project(nc, m, m.weight["l3a_out"], "l3a_out_b", m.x, m.x)


def shift_tokens(nc, m, src, dst):
    half = D // 2
    with stage(nc, "moved") as (block, moved):
        @block.sync
        def _(sp):
            sp.dma_start(dst[1:P, :, half:D], src[0:P - 1, :, half:D]).then_inc(moved, 16)
            sp.dma_start(dst[0:1, 1:NT, half:D], src[P - 1:P, 0:NT - 1, half:D]).then_inc(moved, 16)
            sp.wait_ge(moved, 32)

        @block.gpsimd
        def _(pool):
            nc.gpsimd.memset(dst[0:1, 0, half:D], 0.0)

        @block.vector
        def _(dve):
            nc.vector.tensor_copy(dst[:, :, 0:half], src[:, :, 0:half])


def l3_layer(nc, m, l):
    shift_tokens(nc, m, m.y, m.h)
    turn_tok(nc, m, m.h, m.hT)
    qkv = m.weight["l3f_qkv"].rearrange("p (l s n) -> p l s n", l=DEPTH, s=3)
    with stage(nc, "projected", "squared", "summed", "rooted", "v_out", "step", "scaled", "turned_half", "roped") as (
            block, projected, squared, summed, rooted, v_out, step, scaled, turned_half, roped):
        def heads(ap):
            return ap.rearrange("p (s h e) -> p s h e", s=2, e=LHD)

        full = [P, 2, LH, LHD]

        @block.tensor
        def _(pe):
            for t in range(NT):
                b = 3 * (t % 2)
                if t >= 2:
                    pe.wait_ge(scaled, t - 1)
                    pe.wait_ge(v_out, t - 1)
                for s in range(3):
                    ins = nc.tensor.matmul(bank(m, b + s), m.hT[:, t * P:(t + 1) * P], qkv[:, l, s, :],
                                           start=True, stop=True)
                ins.then_inc(projected, 1)

        @block.scalar
        def _(act):
            for t in range(NT):
                b = 3 * (t % 2)
                act.wait_ge(projected, t + 1)
                if t >= 1:
                    act.wait_ge(summed, t)
                nc.scalar.activation(m.sq[:, :], m.ps[:, b:b + 2, :].rearrange("p a b -> p (a b)"),
                                     ACT.Square).then_inc(squared, 1)
                nc.scalar.copy(m.V[:, t, :], bank(m, b + 2)).then_inc(v_out, 1)

        @block.gpsimd
        def _(pool):
            sn = m.rotary["sin"][:, l]
            for t in range(NT):
                pool.wait_ge(summed, t + 1)
                nc.gpsimd.tensor_tensor(m.ss[:, 1, 0:2 * LH], m.ss[:, 0, 0:2 * LH], m.weight["half"][:, 0:2 * LH],
                                        ALU.pow).then_inc(rooted, 1)
                pool.wait_ge(scaled, t + 1)
                if t >= 1:
                    pool.wait_ge(roped, t)
                x, o = heads(m.qn[:, t % 2, :]), heads(m.rot[:, :])
                hl = LHD // 2
                for a, b in ((0, hl), (hl, 0)):
                    ins = nc.gpsimd.tensor_tensor(o[:, :, :, a:a + hl], x[:, :, :, b:b + hl],
                                                  sn[:, t, :, a:a + hl].unsqueeze(2).to_broadcast([P, 2, LH, hl]),
                                                  ALU.mult)
                ins.then_inc(turned_half, 1)

        @block.vector
        def _(dve):
            n = Count()
            cs = m.rotary["cos"][:, l]

            def finish(t):
                dve.wait_ge(turned_half, t + 1)
                nc.vector.tensor_tensor(m.qt3[:, t, :], m.qt3[:, t, :], m.rot[:, :], ALU.add).then_inc(roped, 1)

            for t in range(NT):
                b = 3 * (t % 2)
                dve.wait_ge(squared, t + 1)
                nc.vector.tensor_reduce(m.ss[:, 0, 0:2 * LH], m.sq[:, :].rearrange("p (h e) -> p h e", e=LHD),
                                        AX.X, ALU.add).then_inc(summed, 1)
                dve.wait_ge(rooted, t + 1)
                nc.vector.tensor_scalar(m.ss[:, 2, 0:2 * LH], m.ss[:, 1, 0:2 * LH], 1e-12, None,
                                        ALU.max).then_inc(step, 1)
                dve.wait_ge(step, n.up())
                nc.vector.reciprocal(m.ss[:, 3, 0:2 * LH], m.ss[:, 2, 0:2 * LH]).then_inc(step, 1)
                dve.wait_ge(step, n.up())
                if t >= 2:
                    dve.wait_ge(turned_half, t - 1)
                nc.vector.tensor_tensor(m.qn[:, t % 2, :].rearrange("p (h e) -> p h e", e=LHD),
                                        m.ps[:, b:b + 2, :].rearrange("p a (h e) -> p (a h) e", e=LHD),
                                        m.ss[:, 3, 0:2 * LH].unsqueeze(2).to_broadcast([P, 2 * LH, LHD]),
                                        ALU.mult).then_inc(scaled, 1)
                dve.wait_ge(scaled, t + 1)
                nc.vector.tensor_tensor(heads(m.qt3[:, t, :]), heads(m.qn[:, t % 2, :]),
                                        cs[:, t, :, :].unsqueeze(2).to_broadcast(full), ALU.mult).then_inc(step, 1)
                dve.wait_ge(step, n.up())
                if t >= 1:
                    finish(t - 1)
            finish(NT - 1)
    with stage(nc, "turned") as (block, turned):
        @block.tensor
        def _(pe):
            for c in range(8):
                for t in range(NT):
                    ins = nc.tensor.transpose(m.ps[:, c, t * P:(t + 1) * P], m.qt3[:, t, c * P:(c + 1) * P],
                                              m.weight["ident"])
                ins.then_inc(turned, 1)

        @block.scalar
        def _(act):
            for c in range(4):
                act.wait_ge(turned, c + 1)
                nc.scalar.copy(m.QP[:, c, :], bank(m, c))

        @block.vector
        def _(dve):
            for c in range(4):
                dve.wait_ge(turned, 4 + c + 1)
                nc.vector.tensor_copy(m.KP[:, c, :], bank(m, 4 + c))

    def rows(h):
        r = slice(LHD * (h % 2), LHD * (h % 2) + LHD)
        return m.QP[r, h // 2, :], m.KP[r, h // 2, :]

    attend(nc, m, LH, LHD, rows, lambda qt: (max(qt - 1, 0), qt + 1),
           lambda qt, h, nk: (m.identb[:, :], m.negband[:, 2 * P - nk:2 * P], 0))
    out_project(nc, m, m.weight["l3f_wo"][:, l * 4 * D:(l + 1) * 4 * D], None, m.y, m.y, chunks=4)
    shift_tokens(nc, m, m.y, m.h)
    normalize(nc, m, m.h, m.h, out_T=m.hT, col_gain=m.weight["l3f_lng"][:, l:l + 1], col_shift=m.weight["l3f_lnb"][:, l:l + 1])
    w1 = m.weight["l3f_w1"].rearrange("p (l f) -> p l f", l=DEPTH)
    b1 = m.weight["l3f_b1"].rearrange("p (l s c) -> p l s c", l=DEPTH, s=2)
    w2 = m.weight["l3f_w2"].rearrange("p (l c d) -> p l c d", l=DEPTH, c=NC3)
    with stage(nc, "pair", "gelus", "gated", "mixed") as (block, pair, gelus, gated, mixed):
        size = [min(P, HID3 - c * P) for c in range(NC3)]

        @block.tensor
        def _(pe):
            for c in range(NC3):
                for s in range(2):
                    at = s * HID3 + c * P
                    ins = nc.tensor.matmul(m.ps[0:size[c], 2 * c + s, :], w1[:, l, at:at + size[c]], m.hT[:, :],
                                           start=True, stop=True)
                ins.then_inc(pair, 1)
            pe.wait_ge(gated, NC3)
            for t in range(NT):
                for c in range(NC3):
                    nc.tensor.matmul(m.ps[:, 6, t * P:(t + 1) * P], m.act3[0:size[c], c, t * P:(t + 1) * P],
                                     w2[0:size[c], l, c, :], start=(c == 0), stop=False)
                ins = add_row(nc, m, m.ps[:, 6, t * P:(t + 1) * P], "l3f_b2", l * D, (l + 1) * D)
            ins.then_inc(mixed, 1)

        @block.scalar
        def _(act):
            for c in range(NC3):
                act.wait_ge(pair, c + 1)
                nc.scalar.activation(m.prob[0:size[c], c, :], m.ps[0:size[c], 2 * c + 1, :], ACT.Gelu,
                                     bias=b1[0:size[c], l, 1, c:c + 1]).then_inc(gelus, 1)

        @block.vector
        def _(dve):
            for c in range(NC3):
                dve.wait_ge(gelus, c + 1)
                nc.vector.scalar_tensor_tensor(out=m.act3[0:size[c], c, :], in0=m.ps[0:size[c], 2 * c, :],
                                               scalar=b1[0:size[c], l, 0, c:c + 1], in1=m.prob[0:size[c], c, :],
                                               op0=ALU.add, op1=ALU.mult).then_inc(gated, 1)
            dve.wait_ge(mixed, 1)
            nc.vector.tensor_tensor(m.y[:, :, :].rearrange("p t d -> p (t d)"), bank(m, 6),
                                    m.y[:, :, :].rearrange("p t d -> p (t d)"), ALU.add)


def l3_ffn(nc, m):
    normalize(nc, m, m.x, m.y)
    for l in range(DEPTH):
        l3_layer(nc, m, l)
    add_scaled(nc, m, m.x[:, :, :], m.y[:, :, :], 0.5)



def macaron(nc, packs, stream, rows, masks, rope3, qk_scale, x_in, out):
    ctx = ExitStack()
    with ctx:
        def sb(name, *shape, dt=F32):
            return ctx.enter_context(nc.sbuf_tensor(name, [P, *shape], dt))[(slice(None),) * (1 + len(shape))]

        m = Buffers()
        m.ps = ctx.enter_context(nc.psum_tensor("ps", [P, 8, 512], F32))
        m.x, m.h, m.y = sb("x", NT, D), sb("h", NT, D), sb("y", NT, D)
        m.hT, m.hT2 = sb("hT", L), sb("hT2", L)
        m.QP, m.KP = sb("QP", 4, L), sb("KP", 4, L)
        m.V, m.otok = sb("V", NT, INNER), sb("otok", NT, INNER)
        m.pad = sb("pad", NT, 2 * H, 32)
        m.prob, m.pT = sb("prob", 3, 512), sb("pT", 2, 512)
        big = sb("big", 16 * 256)
        m.piw = big[:, :]
        m.oiw, m.op = m.QP[:, 0:2, :].rearrange("p a b -> p (a b)"), m.QP[:, 2:4, :].rearrange("p a b -> p (a b)")
        m.rel = big[:, :].rearrange("p (h j) -> p h j", h=H)
        m.act = big[:, :].rearrange("p (s c t) -> p s c t", s=2, c=NC2)
        m.qt3 = big[:, :].rearrange("p (t n) -> p t n", t=NT)
        m.raw = big[:, 0:NT * 2 * D].rearrange("p (t n) -> p t n", t=NT)
        m.tmp = big[:, 2 * NT * D:2 * NT * D + 4 * 512].rearrange("p (i n) -> p i n", i=4)
        m.qk = big[:, NT * 2 * D:2 * NT * 2 * D].rearrange("p (t n) -> p t n", t=NT)
        m.qn = m.otok[:, :, :].rearrange("p (a b) n -> p a (b n)", a=2)
        m.actj2 = m.otok
        m.rot = m.prob[:, 0:2, :].rearrange("p a b -> p (a b)")
        m.sq = m.pT[:, :, :].rearrange("p a b -> p (a b)")
        m.state = sb("state", NT, D)
        m.actj = m.pT
        m.junk = m.prob[:, 0:2, :].rearrange("p a b -> p (a b)")
        m.act3 = m.V
        m.st6, m.mv = sb("st6", NT, 6), sb("mv", NT, 2)
        m.ve, m.rstd = sb("ve", NT), sb("rstd", NT)
        m.nm, m.sums, m.rsum = sb("nm", NT * H), sb("sums", NT * H), sb("rsum", NT * H)
        m.acc, m.wv, m.ex, m.pick, m.rank = sb("acc", 8), sb("wv", 8), sb("ex", 8), sb("pick", 8), sb("rank", 8)
        m.cnt, m.aggv = sb("cnt", 8, 4), sb("aggv", 2)
        m.gp, m.gl, m.g4, m.sel, m.grank = (sb("gp", NT, NE), sb("gl", NT, NE), sb("g4", 3 * NT),
                                            sb("sel", NT, NE), sb("grank", NT, NE))
        m.cmp = sb("cmp", 2, NT, NE, NE)
        m.ss, m.beta = sb("ss", 4, NT * 2 * H), sb("beta", NT, H)
        m.identb, m.negcausal, m.negblock = sb("identb", P, dt=BF16), sb("negcausal", P, dt=BF16), sb("negblock", P, dt=BF16)
        m.negband = sb("negband", 2 * P, dt=BF16)
        m.rotary["cos"], m.rotary["sin"] = sb("cos3", DEPTH, NT, 2, LHD), sb("sin3", DEPTH, NT, 2, LHD)
        neg = m.KP[:, 0:1, :]

        wt = []
        for i, fields in enumerate(LEVELS):
            offs, total = offsets(fields)
            t = sb(f"weights{i}", total)
            wt.append(t)
            for name, (a, n) in offs.items():
                m.weight[name] = t[:, a:a + n]
        m.stream = stream
        m.rows = sb("rows", ROW_COLS)
        for i, fields in enumerate(ROWS):
            for name, (a, n) in offsets(fields)[0].items():
                m.row_at[name] = (32 * i, a, n)

        nrows = NT * H * P + 2
        m.shear = nc.dram_tensor("shear", [nrows * RW], F32).ap()
        loaded = [ctx.enter_context(nc.semaphore(f"weights{i}_loaded")) for i in range(len(LEVELS))]

        with stage(nc, "small_in", "neg_set", "neg_out", "row_in", "rope_in") as (
                block, small_in, neg_set, neg_out, row_in, rope_in):
            rt = big[:, 0:2 * NT * 2 * LHD].rearrange("p (a t s e) -> p a t s e", a=2, t=NT, s=2)
            qs = big[:, 4 * NT * LHD:4 * NT * LHD + DEPTH * 2 * LHD].rearrange("p (l s e) -> p l s e", l=DEPTH, s=2)
            mk = big[:, 2048:2048 + 5 * P]

            @block.sync
            def _(sp):
                for i in range(len(LEVELS)):
                    sp.dma_start(wt[i][:, :], packs[i]).then_inc(loaded[i], 16)
                sp.wait_ge(neg_set, 1)
                body = m.shear[0:(nrows - 2) * RW].rearrange("(a p w) -> p a w", p=P, w=2 * RW)
                per = body.shape[1]
                for a in range(per):
                    sp.dma_start(body[:, a, :], neg[:, 0, :]).then_inc(neg_out, 16)
                sp.dma_start(m.shear[(nrows - 2) * RW:nrows * RW].rearrange("(p w) -> p w", p=1),
                             neg[0:1, 0, :]).then_inc(neg_out, 16)
                sp.wait_ge(neg_out, 16 * (per + 1))

            @block.scalar
            def _(act):
                for i, fields in enumerate(ROWS):
                    n = offsets(fields)[1]
                    act.dma_start(m.rows[32 * i:32 * i + 1, 0:n], rows[i:i + 1, 0:n]).then_inc(row_in, 16)
                act.wait_ge(row_in, 16 * len(ROWS))
                act.dma_start(mk, masks).then_inc(small_in, 16)
                act.dma_start(rt.rearrange("p a t s e -> p (a t s e)"), rope3).then_inc(rope_in, 16)
                act.dma_start(qs.rearrange("p l s e -> p (l s e)"),
                              qk_scale.to_broadcast([P, DEPTH * 2 * LHD])).then_inc(rope_in, 16)
                for i in range(len(LEVELS)):
                    act.wait_ge(loaded[i], 16)

            @block.gpsimd
            def _(pool):
                nc.gpsimd.memset(neg, NEG).then_inc(neg_set, 1)
                nc.gpsimd.memset(m.pad[:, :, :, :], 0.0)

            @block.vector
            def _(dve):
                dve.wait_ge(small_in, 16)
                for i, dst in enumerate((m.identb, m.negcausal, m.negblock)):
                    nc.vector.tensor_copy(dst[:, :], mk[:, i * P:(i + 1) * P])
                nc.vector.tensor_copy(m.negband[:, :], mk[:, 3 * P:5 * P])
                dve.wait_ge(rope_in, 32)
                hl = LHD // 2
                for l in range(DEPTH):
                    nc.vector.tensor_tensor(m.rotary["cos"][:, l], rt[:, 0],
                                            qs[:, l].unsqueeze(1).to_broadcast([P, NT, 2, LHD]), ALU.mult)
                    for a, b in ((0, hl), (hl, 0)):
                        nc.vector.tensor_tensor(m.rotary["sin"][:, l, :, :, a:a + hl], rt[:, 1, :, :, a:a + hl],
                                                qs[:, l, :, b:b + hl].unsqueeze(1).to_broadcast([P, NT, 2, hl]),
                                                ALU.mult)

        with nc.Fori(0, B) as b:
            with stage(nc, "x_in") as (block, x_got):
                @block.sync
                def _(sp):
                    sp.dma_start(m.x[:, :, :], x_in[bass.ds(b, 1)].rearrange("o (t p) d -> p (o t) d", p=P)).then_inc(x_got, 16)
                    sp.wait_ge(x_got, 16)
            steps = [l0_ffn, l0_attn, l0_ffn, l1_ffn, l1_attn, l1_ffn, l2_ffn, l2_attn, l2_ffn,
                     l3_ffn, l3_attn, l3_ffn]
            for sub in steps:
                sub(nc, m)
            with stage(nc, "stored") as (block, stored):
                @block.sync
                def _(sp):
                    sp.dma_start(out[bass.ds(b, 1)].rearrange("o (t p) d -> p (o t) d", p=P), m.x[:, :, :]).then_inc(stored, 16)
                    sp.wait_ge(stored, 16)



def shape_constants():
    i = np.arange(P)
    f = np.float32
    c = {"ident": np.eye(P, dtype=f), "tri": (i[None, :] < i[:, None]).astype(f),
         "causalT": (i[:, None] <= i[None, :]).astype(f), "blockdiag": (i[:, None] // HD == i[None, :] // HD).astype(f),
         "tri8": np.broadcast_to(np.tril(np.ones((NE, NE), f), -1).reshape(1, -1), (P, NE * NE)),
         "neg_half": np.full((P, NT), -0.5, f), "half": np.full((P, NT * 32), 0.5, f), "ones": np.ones((P, P), f)}
    pos = np.arange(L, dtype=f)
    inv = (f(1.0) / f(10000.0) ** (np.arange(0, HD, 2, dtype=f) / f(HD))).astype(f)
    ang = (pos[:, None] * inv[None, :]).astype(f).astype(np.float64)
    for name, fn in (("rope_cos", np.cos), ("rope_sin", np.sin)):
        c[name] = fn(ang).astype(f).reshape(NT, P, 4).transpose(1, 0, 2).reshape(P, NT * 4)
    q, k = i[:, None], i[None, :]
    causal = np.where(k <= q, 0, NEG)
    block32 = np.where((k <= q) & (k // 32 == q // 32), 0, NEG)
    kk = np.arange(2 * P)[None, :] - P
    band = np.where((kk <= q) & (q - kk <= WIN), 0, NEG)
    masks = np.concatenate([np.eye(P), causal, block32, band], 1).astype(f)
    half = np.arange(0, LHD, 2, dtype=f)
    inv = (f(1.0) / f(10000.0) ** (half / f(LHD))).astype(f)
    ang = (pos[:, None] * inv[None, :]).astype(f).astype(np.float64)
    base = ((half + f(0.4 * LHD)) / f(1.4 * LHD)).astype(f)
    power = ((pos - L // 2) / f(WIN // 2)).astype(f)
    scale = (base[None, :].astype(np.float64) ** power[:, None]).astype(f).astype(np.float64)
    tabs = []
    for fn, first in ((np.cos, 1.0), (np.sin, -1.0)):
        v = fn(ang).astype(f).astype(np.float64)
        t = np.stack([np.concatenate([first * v * s, v * s], 1) for s in (8.0 * scale, 1.0 / scale)], 1)
        tabs.append(t.reshape(NT, P, 2, LHD).transpose(1, 0, 2, 3))
    rope3 = np.stack(tabs, 1).astype(f).reshape(P, -1)
    return c, masks, rope3



def lay_out(g, c):
    def tiles(a, n):
        return a.reshape(n, P, -1).transpose(1, 0, 2).reshape(P, -1)

    def on_128(a):
        out = np.zeros((P, a.shape[1]), a.dtype)
        out[:a.shape[0]] = a
        return out

    d = dict(c)
    e = g["L0_attn_rel_emb"][MAX_REL - REL + 1:MAX_REL + 1].T
    rel = np.zeros((P, REL), e.dtype)
    for j in range(4):
        rel[32 * j:32 * j + HD] = e
    d["rel_T"] = rel
    d["ip_T"] = g["L0_ffn_input_patterns"].T
    d["piw_T"] = tiles(g["L0_ffn_process_input_weights"].T, 8)
    d["pv"] = tiles(g["L0_ffn_process_values"], 4)
    d["oiw_T"] = on_128(g["L0_ffn_output_input_weights"].T)
    d["op"] = tiles(g["L0_ffn_output_patterns"], 8)
    d["l0_qkv"], d["l0_out"] = g["L0_attn_w_qkv"].T, g["L0_attn_w_out"].T
    d["l1f_qkv"], d["l1f_out"], d["l1f_gate"] = g["L1_ffn_in_proj_w"].T, g["L1_ffn_out_proj_w"].T, g["L1_ffn_gate_w"].T
    d["l1f_exp"] = g["L1_ffn_expert_w"].transpose(2, 0, 1).reshape(D, -1)
    for n in ("ln1_w", "ln1_b", "ln2_w", "ln2_b"):
        d["l1f_" + n] = np.broadcast_to(g["L1_ffn_" + n][None, :], (P, D))
    d["l1a_qkvb"] = np.concatenate([g["L1_attn_" + n] for n in ("Wq", "Wk", "Wv", "Wb")], 1)
    d["l1a_out"] = g["L1_attn_Wo"]
    d["l2f_rw"] = g["L2_ffn_router_w"]
    d["l2f_w1"] = g["L2_ffn_w1"].transpose(1, 0, 2).reshape(D, -1)
    d["l2f_b1"] = g["L2_ffn_b1"].reshape(NE, 2 * NC2, P).transpose(2, 0, 1).reshape(P, -1)
    d["l2f_w2"] = g["L2_ffn_w2"].reshape(NE, NC2, P, D).transpose(2, 0, 1, 3).reshape(P, -1)
    d["l2a_qkv"], d["l2a_out"] = g["L2_attn_Wqkv"].T, g["L2_attn_Wout"].T
    d["l3a_qkv"] = np.concatenate([g["L3_attn_" + n].T for n in ("Wq", "Wk", "Wv")], 1)
    d["l3a_out"] = g["L3_attn_Wo"].T
    d["l3f_qkv"] = g["L3_ffn_wqkv"].transpose(1, 0, 2).reshape(D, -1)
    d["l3f_wo"] = g["L3_ffn_wo"].reshape(DEPTH, 4, P, D).transpose(2, 0, 1, 3).reshape(P, -1)
    d["l3f_w1"] = g["L3_ffn_w1"].transpose(1, 0, 2).reshape(D, -1)
    b1 = np.zeros((DEPTH, 2, NC3 * P), np.float32)
    b1[:, :, :HID3] = g["L3_ffn_b1"].reshape(DEPTH, 2, HID3)
    d["l3f_b1"] = b1.reshape(DEPTH, 2, NC3, P).transpose(3, 0, 1, 2).reshape(P, -1)
    w2 = np.zeros((DEPTH, NC3 * P, D), np.float32)
    w2[:, :HID3] = g["L3_ffn_w2"]
    d["l3f_w2"] = w2.reshape(DEPTH, NC3, P, D).transpose(2, 0, 1, 3).reshape(P, -1)
    d["l3f_lng"], d["l3f_lnb"] = g["L3_ffn_ln_g"].T, g["L3_ffn_ln_b"].T
    packs = [np.concatenate([d[n] for n, _ in fields], 1) for fields in LEVELS]
    r = {"l1f_qkv_b": g["L1_ffn_in_proj_b"], "l1f_out_b": g["L1_ffn_out_proj_b"],
         "l1f_gate_b": g["L1_ffn_gate_b"], "l1f_exp_b": g["L1_ffn_expert_b"], "l1a_bb": g["L1_attn_bb"],
         "l2f_rb": g["L2_ffn_router_b"], "l2f_b2": g["L2_ffn_b2"],
         "l3a_qkv_b": np.concatenate([g["L3_attn_" + n] for n in ("bq", "bk", "bv")]), "l3a_out_b": g["L3_attn_bo"],
         "l3f_b2": g["L3_ffn_b2"]}
    rows = np.zeros((len(ROWS), ROW_COLS), np.float32)
    for i, fields in enumerate(ROWS):
        for name, (a, n) in offsets(fields)[0].items():
            rows[i, a:a + n] = r[name].reshape(-1)
    stream = np.concatenate([d[n] for n, _ in STREAM], 1)
    qk_scale = np.stack([g["L3_ffn_q_scale"], g["L3_ffn_k_scale"]], 1).reshape(1, -1)
    return packs, stream, rows, qk_scale


def kernel(**inputs):
    import concourse.bacc as bacc
    from concourse.bass_utils import run_bass_kernel_spmd

    g = {k: np.asarray(v) for k, v in inputs.items()}
    c, masks, rope3 = shape_constants()
    packs, stream, rows, qk_scale = lay_out(g, c)
    arrays = {f"pack{i}": a for i, a in enumerate(packs)}
    arrays.update(stream=stream, rows=rows, masks=masks, rope3=rope3, qk_scale=qk_scale, x=g["L0_attn_x"])
    arrays = {k: np.ascontiguousarray(v) for k, v in arrays.items()}
    nc = bacc.Bacc("TRN2", target_bir_lowering=False, num_devices=1)
    ap = {k: nc.dram_tensor(f"in_{k}", v.shape, mybir.dt.from_np(v.dtype), kind="ExternalInput").ap()
          for k, v in arrays.items()}
    out = nc.dram_tensor("out_0", (B, L, D), F32, kind="ExternalOutput").ap()
    macaron(nc, [ap[f"pack{i}"] for i in range(len(LEVELS))], ap["stream"], ap["rows"], ap["masks"], ap["rope3"], ap["qk_scale"],
            ap["x"], out)
    r = run_bass_kernel_spmd(nc, [{f"in_{k}": v for k, v in arrays.items()}], core_ids=[0])
    return r.results[0]["out_0"]
```

```python
from contextlib import ExitStack, contextmanager

import numpy as np

import concourse.bass as bass
from concourse import mybir

F32 = mybir.dt.float32
BF16 = mybir.dt.bfloat16
ALU = mybir.AluOpType
ACT = mybir.ActivationFunctionType
AX = mybir.AxisListType

P = 128
B, L, D = 4, 512, 128
NT = L // P
H, HD = 16, 8
NI, NP_, DV = 1024, 512, 64
KI, KP = NI // 8, NP_ // 8
NE = 8
HID2 = 512
NC2 = HID2 // P
DEPTH, LH, LHD, WIN = 2, 8, 64, 64
INNER = LH * LHD
HID3 = int(D * 4 * 2 / 3)
NC3 = -(-HID3 // P)
REL = 32
MAX_REL = 64
RW = 256
NEG = -1e30
EPS = 1e-5

LEVELS = [
    [("ident", P), ("tri", P), ("causalT", P), ("blockdiag", P), ("tri8", NE * NE), ("rope_cos", NT * 4),
     ("rope_sin", NT * 4), ("neg_half", NT), ("half", NT * 32), ("ones", P),
     ("ip_T", NI), ("pv", 4 * DV),
     ("l0_qkv", 3 * D), ("l0_out", 4 * D)],
    [("l1f_qkv", 3 * D), ("l1f_out", D), ("l1f_gate", NE), ("l1f_exp", NE * D),
     ("l1f_ln1_w", D), ("l1f_ln1_b", D), ("l1f_ln2_w", D), ("l1f_ln2_b", D),
     ("l1a_qkvb", 3 * D + H), ("l1a_out", 4 * D)],
    [("l2f_rw", NE), ("l2f_w1", NE * 2 * HID2), ("l2f_b1", NE * 2 * NC2), ("l2f_w2", NE * NC2 * D),
     ("l2a_qkv", 3 * D), ("l2a_out", D)],
    [("l3a_qkv", 3 * D), ("l3a_out", D), ("l3f_qkv", DEPTH * 3 * INNER), ("l3f_wo", DEPTH * 4 * D),
     ("l3f_w1", DEPTH * 2 * HID3), ("l3f_b1", DEPTH * 2 * NC3), ("l3f_w2", DEPTH * NC3 * D),
     ("l3f_lng", DEPTH), ("l3f_lnb", DEPTH)],
]
STREAM = [("piw_T", 8 * NP_), ("oiw_T", NI), ("op", 8 * D)]
ROWS = [[("l1f_exp_b", NE * D)], [("l2f_b2", NE * D)],
        [("l1f_qkv_b", 3 * D), ("l1f_out_b", D), ("l1f_gate_b", NE), ("l1a_bb", H), ("l2f_rb", NE)],
        [("l3a_qkv_b", 3 * D), ("l3a_out_b", D), ("l3f_b2", DEPTH * D)]]
ROW_COLS = NE * D


def offsets(fields):
    at, out = 0, {}
    for name, n in fields:
        out[name] = (at, n)
        at += n
    return out, at


class Buffers:

    def __init__(self):
        self.weight, self.row_at, self.rotary = {}, {}, {}


class Count:

    def __init__(self):
        self.n = 0

    def up(self, by=1):
        self.n += by
        return self.n


@contextmanager
def stage(nc, *names):
    sems = [nc.alloc_semaphore(f"{n}_{nc.next_id()}") for n in names]
    with nc.Block() as block:
        yield (block, *sems)
    nc.clear_and_free_semaphores(sems)
    nc.all_engine_barrier(sem_only=True)


def add_row(nc, m, out, name, a=0, b=None, **kw):
    p, at, n = m.row_at[name]
    b = n if b is None else b
    return nc.tensor.matmul(out, m.onesb[p:p + 3, :], m.rowparts[p:p + 3, at + a:at + b], start=False, stop=True, **kw)


def bank(m, i, n=512):
    return m.ps[:, i, 0:n]



def normalize(nc, m, src, dst, clear=False, gain=None, shift=None, out_T=None, col_gain=None, col_shift=None):
    with stage(nc, "dve_step", "pow_done", "norm_ready", "turned") as (block, dve_step, pow_done, norm_ready, turned):
        @block.vector
        def _(dve):
            n = Count()
            for t in range(NT):
                nc.vector.bn_stats(m.st6[:, t, :], src[:, t, :]).then_inc(dve_step, 1)
                n.up()
            dve.wait_ge(dve_step, n.n)
            for t in range(NT):
                nc.vector.bn_aggr(m.mv[:, t, :], m.st6[:, t, :]).then_inc(dve_step, 1)
                n.up()
            dve.wait_ge(dve_step, n.n)
            nc.vector.tensor_scalar(m.ve[:, 0:NT], m.mv[:, :, 1], EPS, None, ALU.add).then_inc(dve_step, 1)
            dve.wait_ge(pow_done, 1)
            for t in range(NT):
                ins = nc.vector.tensor_scalar(dst[:, t, :], src[:, t, :], m.mv[:, t, 0:1], m.rstd[:, t:t + 1],
                                              ALU.subtract, ALU.mult)
                if gain is None:
                    ins.then_inc(norm_ready, 1)
                else:
                    ins.then_inc(dve_step, 1)
            n.up(NT + 1)
            if gain is not None:
                dve.wait_ge(dve_step, n.n)
                nc.vector.tensor_tensor(dst, dst, gain.unsqueeze(1).to_broadcast([P, NT, D]),
                                        ALU.mult).then_inc(dve_step, 1)
                dve.wait_ge(dve_step, n.up())
                nc.vector.tensor_tensor(dst, dst, shift.unsqueeze(1).to_broadcast([P, NT, D]),
                                        ALU.add).then_inc(norm_ready, NT)

        @block.gpsimd
        def _(pool):
            pool.wait_ge(dve_step, 2 * NT + 1)
            nc.gpsimd.tensor_tensor(m.rstd[:, 0:NT], m.ve[:, 0:NT], m.weight["neg_half"], ALU.pow).then_inc(pow_done, 1)
            if clear:
                v = m.V.rearrange("p t (h e) -> p t h e", h=H)
                nc.gpsimd.memset(v[:, :, :, HD + 1:32], 0.0)
                nc.gpsimd.memset(v[:, :, :, HD:HD + 1], 1.0)

        if out_T is not None:
            @block.tensor
            def _(pe):
                for t in range(NT):
                    pe.wait_ge(norm_ready, NT if gain is not None else t + 1)
                    ins = nc.tensor.transpose(bank(m, 0)[:, t * P:(t + 1) * P], dst[:, t, :], m.weight["ident"])
                ins.then_inc(turned, 1)

            @block.scalar
            def _(act):
                act.wait_ge(turned, 1)
                if col_gain is None:
                    nc.scalar.copy(out_T, bank(m, 0))
                else:
                    nc.scalar.activation(out_T, bank(m, 0), ACT.Identity, bias=col_shift, scale=col_gain)


def turn_tok(nc, m, *pairs):
    with stage(nc, "turned") as (block, turned):
        @block.tensor
        def _(pe):
            for i, (src, _) in enumerate(pairs):
                for t in range(NT):
                    ins = nc.tensor.transpose(bank(m, i)[:, t * P:(t + 1) * P], src[:, t, :], m.weight["ident"])
                ins.then_inc(turned, 1)

        @block.scalar
        def _(act):
            for i, (_, out_T) in enumerate(pairs):
                act.wait_ge(turned, i + 1)
                nc.scalar.copy(out_T, bank(m, i))


def add_scaled(nc, m, dst, src, coef):
    with stage(nc) as (block,):
        @block.vector
        def _(dve):
            nc.vector.scalar_tensor_tensor(out=dst, in0=src, scalar=coef, in1=dst, op0=ALU.mult, op1=ALU.add)



def project_tok(nc, m, src_T, weight, width, row=None, row_at=0):
    with stage(nc) as (block,):
        @block.tensor
        def _(pe):
            for t in range(NT):
                nc.tensor.matmul(m.ps[:, t, 0:width], src_T[:, t * P:(t + 1) * P], weight,
                                 start=True, stop=True)
                if row is not None:
                    add_row(nc, m, m.ps[:, t, row_at:width], row, skip_group_check=True)


STACK = 6 * HD


def stack_block(m, s, i):
    return m.stk[:, :, s, :, i * HD:(i + 1) * HD]


def stack_parts(nc, m, q_scale, from_psum):
    both = [P, NT, 2, H, HD]
    with stage(nc, "copied", "split", "part1", "part2", "part3") as (block, copied, split, part1, part2, part3):
        raw = m.raw.rearrange("p t (s h e) -> p t s h e", s=2, e=HD)
        res = m.tmp.rearrange("p i n -> p (i n)")[:, 0:NT * 2 * D].rearrange("p (t s h e) -> p t s h e", t=NT, s=2, e=HD)

        def per_side(op):
            for s in range(2):
                ins = op(s)
            return ins

        @block.scalar
        def _(act):
            if from_psum:
                nc.scalar.activation(m.raw[:, :, 0:D], m.ps[:, 0:NT, 0:D], ACT.Copy, scale=q_scale).then_inc(copied, 1)
                nc.scalar.copy(m.raw[:, :, D:2 * D], m.ps[:, 0:NT, D:2 * D]).then_inc(copied, 1)
                nc.scalar.copy(m.V.rearrange("p t (h e) -> p t h e", h=H)[:, :, :, 0:HD],
                               m.ps[:, 0:NT, 2 * D:3 * D].rearrange("p t (h e) -> p t h e", h=H))
            act.wait_ge(part1, 2)
            for s, i in ((0, 3), (0, 5), (1, 2)):
                nc.scalar.copy(stack_block(m, s, i), stack_block(m, s, 0))

        @block.gpsimd
        def _(pool):
            nc.gpsimd.memset(m.stk[:, :, 1, :, STACK:STACK + 3], 1.0)
            nc.gpsimd.memset(m.stk[:, :, 0, :, STACK:STACK + 3], 0.0)
            pool.wait_ge(part1, 2)
            nc.gpsimd.tensor_copy(stack_block(m, 1, 4), stack_block(m, 1, 0))
            pool.wait_ge(part2, 2)
            nc.gpsimd.tensor_copy(stack_block(m, 0, 4), stack_block(m, 0, 1))
            nc.gpsimd.tensor_copy(stack_block(m, 1, 3), stack_block(m, 1, 1))

        @block.vector
        def _(dve):
            if from_psum:
                dve.wait_ge(copied, 2)
            for s in range(2):
                nc.vector.tensor_copy(stack_block(m, s, 0), raw[:, :, s]).then_inc(part1, 1)
            dve.wait_ge(part1, 2)
            for s in range(2):
                nc.vector.tensor_tensor(res[:, :, s], raw[:, :, s], stack_block(m, s, 0), ALU.subtract).then_inc(split, 1)
            dve.wait_ge(split, 2)
            for s in range(2):
                nc.vector.tensor_copy(stack_block(m, s, 1), res[:, :, s]).then_inc(part2, 1)
            dve.wait_ge(part2, 2)
            for s in range(2):
                nc.vector.tensor_tensor(res[:, :, s], res[:, :, s], stack_block(m, s, 1), ALU.subtract).then_inc(part3, 1)
            dve.wait_ge(part3, 2)
            nc.vector.tensor_copy(stack_block(m, 0, 2), res[:, :, 0])
            nc.vector.tensor_copy(stack_block(m, 1, 5), res[:, :, 1])


def q_slot(h):
    return 4 * (h // 4) + 2 * (h % 2) + (h // 2) % 2


def copy_pair(copy, dst, src):
    for e in range(2):
        ins = copy(dst(e)[64 * e:64 * e + 64, :], src[64 * e:64 * e + 64, :])
    return ins


def turn_stacks(nc, m):
    with stage(nc, "turned", "even_out", "odd_out") as (block, turned, even_out, odd_out):
        def half(i):
            return m.psb[:, i // 2, (i % 2) * L:(i % 2 + 1) * L]

        @block.tensor
        def _(pe):
            for i in range(16):
                pair, side = i // 2, i % 2
                for t in range(NT):
                    ins = nc.tensor.transpose(half(i)[:, t * P:(t + 1) * P],
                                              m.stk[:, t, side, 2 * pair:2 * pair + 2, :].rearrange("p a b -> p (a b)"),
                                              m.identb)
                if side == 1:
                    ins.then_inc(turned, 1)

        def evacuate(eng, copy, pair):
            eng.wait_ge(turned, pair + 1)
            copy_pair(copy, lambda e: m.QX[:, q_slot(2 * pair + e), :], half(2 * pair))
            copy(m.KX[:, pair, :], half(2 * pair + 1))

        @block.scalar
        def _(act):
            for pair in range(0, 8, 2):
                evacuate(act, nc.scalar.copy, pair)

        @block.vector
        def _(dve):
            for pair in range(1, 8, 2):
                evacuate(dve, nc.vector.tensor_copy, pair)


FULL, CAUSAL, BLOCK32 = range(3)


def attend8(nc, m, kind):
    PAIRS = H // 2
    if kind == FULL:
        first = [([qt], L) for qt in range(NT)]
        second = [([kt], 0) for kt in range(NT)]
    elif kind == CAUSAL:
        first = [([qt], (qt + 1) * P) for qt in range(NT)]
        second = [([kt], kt * P) for kt in range(NT)]
    else:
        first, second = [(list(range(NT)), P)], [(list(range(NT)), 0)]
    nf, ns = 2 * len(first), 2 * len(second)
    LEAD = 4 if kind == BLOCK32 else 6
    TURN_AT = max(ns - 3, 0)

    with stage(nc, "scores", "negmax", "max_split", "q_turned", "q_ready", "shifted", "exps", "av", "o_out",
               "pstep") as (block, scores, negmax, max_split, q_turned, q_ready, shifted, exps, av, o_out, pstep):
        def rows(h):
            return m.QX[:, q_slot(h), :], m.KX[:, h // 2, :]

        def nm_of(h, qts):
            return m.nm[:, h * NT + qts[0]:h * NT + qts[-1] + 1]

        @block.tensor
        def _(pe):
            def score(i):
                pair, (e, u) = i // nf, divmod(i % nf, len(first))
                h = 2 * pair + e
                q, k = rows(h)
                qts, nk = first[u]
                if i >= 3:
                    pe.wait_ge(negmax, i - 2)
                b = m.ps[:, (0, 1, 7)[i % 3], :]
                if kind == BLOCK32:
                    nc.tensor.matmul(b, m.identb, m.negblock.unsqueeze(1).to_broadcast([P, NT, P]),
                                     start=True, stop=True)
                for n, qt in enumerate(qts):
                    lo = qt * P if kind == BLOCK32 else 0
                    ins = nc.tensor.matmul(b[:, n * P:n * P + nk], q[:, qt * P:(qt + 1) * P], k[:, lo:lo + nk],
                                           start=kind != BLOCK32, stop=True, skip_group_check=kind == BLOCK32)
                if kind == CAUSAL:
                    ins = nc.tensor.matmul(b[:, nk - P:nk], m.identb, m.negcausal, start=False, stop=True,
                                           skip_group_check=True)
                ins.then_inc(scores, 1)

            def turn_q(pair):
                pe.wait_ge(max_split, pair + 1)
                if pair >= 1:
                    pe.wait_ge(q_ready, pair)
                for t in range(NT):
                    ins = nc.tensor.transpose(m.psb[:, 6, t * P:(t + 1) * P],
                                              m.stk[:, t, 0, 2 * pair:2 * pair + 2, :].rearrange("p a b -> p (a b)"),
                                              m.identb)
                ins.then_inc(q_turned, 1)

            def shifted_score(i):
                pair, (e, u) = i // ns, divmod(i % ns, len(second))
                h = 2 * pair + e
                q, k = rows(h)
                kts, q0 = second[u]
                if i % ns == 0:
                    pe.wait_ge(q_ready, pair + 1)
                if i >= 2:
                    pe.wait_ge(exps, i - 1)
                b = m.ps[:, 2 + i % 2, :]
                if kind == BLOCK32:
                    nc.tensor.matmul(b, m.negblock, m.identb.unsqueeze(1).to_broadcast([P, NT, P]),
                                     start=True, stop=True)
                for n, kt in enumerate(kts):
                    a, z = (kt * P, (kt + 1) * P) if kind == BLOCK32 else (q0, L)
                    ins = nc.tensor.matmul(b[:, n * P:n * P + z - a], k[:, kt * P:(kt + 1) * P], q[:, a:z],
                                           start=kind != BLOCK32, stop=True, skip_group_check=kind == BLOCK32)
                if kind == CAUSAL:
                    ins = nc.tensor.matmul(b[:, 0:P], m.negcausal, m.identb, start=False, stop=True,
                                           skip_group_check=True)
                ins.then_inc(shifted, 1)

            def weigh(i):
                pair, (e, u) = i // ns, divmod(i % ns, len(second))
                h = 2 * pair + e
                kts, q0 = second[u]
                pe.wait_ge(exps, i + 1)
                g, j = h // 4, h % 4
                if j == 0 and u == 0 and g >= 2:
                    pe.wait_ge(o_out, g - 1)
                for n, kt in enumerate(kts):
                    a, z = (kt * P, (kt + 1) * P) if kind == BLOCK32 else (q0, L)
                    ins = nc.tensor.matmul(m.ps[32 * j:32 * j + 32, 4 + g % 2, a:z], m.V[:, kt, 32 * h:32 * h + 32],
                                           m.prob[:, i % 3, n * P:n * P + z - a],
                                           start=(kind == BLOCK32 or u == 0), stop=(kind == BLOCK32 or u == len(second) - 1),
                                           skip_group_check=True)
                ins.then_inc(av, 1)

            for i in range(nf + LEAD):
                score(i)
            turn_q(0)
            for i in range(PAIRS * ns):
                shifted_score(i)
                if nf + LEAD + i < PAIRS * nf:
                    score(nf + LEAD + i)
                if i % ns == TURN_AT and i // ns + 1 < PAIRS:
                    turn_q(i // ns + 1)
                if i >= 2:
                    weigh(i - 2)
            for i in range(PAIRS * ns - 2, PAIRS * ns):
                weigh(i)

        @block.vector
        def _(dve):
            def maximum(i):
                pair, (e, u) = i // nf, divmod(i % nf, len(first))
                qts, nk = first[u]
                dve.wait_ge(scores, i + 1)
                src = m.ps[:, (0, 1, 7)[i % 3], 0:len(qts) * nk]
                if len(qts) > 1:
                    src = src.rearrange("p (a b) -> p a b", a=len(qts))
                nc.vector.tensor_reduce(nm_of(2 * pair + e, qts), src, AX.X, ALU.max, negate=True).then_inc(negmax, 1)

            def take_q(pair):
                dve.wait_ge(q_turned, pair + 1)
                copy_pair(nc.vector.tensor_copy, lambda e: m.QX[:, q_slot(2 * pair + e), :],
                          m.psb[:, 6, 0:L]).then_inc(q_ready, 1)

            for i in range(nf + LEAD):
                maximum(i)
            take_q(0)
            for i in range(PAIRS * ns):
                if nf + LEAD + i < PAIRS * nf:
                    maximum(nf + LEAD + i)
                if i % ns == TURN_AT and i // ns + 1 < PAIRS:
                    take_q(i // ns + 1)

        @block.gpsimd
        def _(pool):
            n = Count()
            for pair in range(PAIRS):
                pool.wait_ge(negmax, nf * (pair + 1))
                res = m.nm[:, 2 * pair * NT:(2 * pair + 2) * NT].rearrange("p (h t) -> p t h", h=2)
                for c in range(3):
                    part = m.stk[:, :, 0, 2 * pair:2 * pair + 2, STACK + c]
                    ins = nc.gpsimd.tensor_copy(part, res)
                    if c == 2:
                        ins.then_inc(max_split, 1)
                    else:
                        ins.then_inc(pstep, 1)
                        pool.wait_ge(pstep, n.up())
                        nc.gpsimd.tensor_tensor(res, res, part, ALU.subtract).then_inc(pstep, 1)
                        pool.wait_ge(pstep, n.up())

        @block.scalar
        def _(act):
            for i in range(PAIRS * ns + 2):
                if i < PAIRS * ns:
                    kts, q0 = second[i % len(second)]
                    act.wait_ge(shifted, i + 1)
                    if i >= 3:
                        act.wait_ge(av, i - 2)
                    nc.scalar.activation(m.prob[:, i % 3, 0:L - q0], m.ps[:, 2 + i % 2, 0:L - q0],
                                         ACT.Exp).then_inc(exps, 1)
                if i >= 3 and (i - 2) % (2 * ns) == 0:
                    g = (i - 2) // (2 * ns) - 1
                    act.wait_ge(av, 2 * ns * (g + 1))
                    nc.scalar.copy(m.otok[:, g, :], m.ps[:, 4 + g % 2, :]).then_inc(o_out, 1)
            act.wait_ge(av, PAIRS * ns)
            nc.scalar.copy(m.otok[:, 3, :], m.ps[:, 5, :])


def divide(nc, m):
    with stage(nc, "turned", "inverted") as (block, turned, inverted):
        @block.tensor
        def _(pe):
            for t in range(NT):
                for g in range(4):
                    ins = nc.tensor.transpose(m.ps[:, t, g * P:(g + 1) * P], m.otok[:, g, t * P:(t + 1) * P],
                                              m.weight["ident"])
            ins.then_inc(turned, 1)

        @block.vector
        def _(dve):
            dve.wait_ge(turned, 1)
            o = m.ps[:, 0:NT, :].rearrange("p t (h e) -> p t h e", e=32)
            nc.vector.reciprocal(m.rsum[:, :].rearrange("p (t h) -> p t h", t=NT), o[:, :, :, HD]).then_inc(inverted, 1)
            dve.wait_ge(inverted, 1)
            nc.vector.tensor_tensor(m.ot.rearrange("p t (h e) -> p t h e", e=HD), o[:, :, :, 0:HD],
                                    m.rsum[:, :].rearrange("p (t h) -> p t h", t=NT).unsqueeze(3).to_broadcast(
                                        [P, NT, H, HD]), ALU.mult)


def rope_heads(nc, m, scale, interleaved):
    with stage(nc, "copied", "products") as (block, copied, products):
        src = m.qk.rearrange("p t (h e) -> p t h e", e=HD)
        dst = m.raw.rearrange("p t (h e) -> p t h e", e=HD)

        def out_half(i):
            return dst[:, :, :, i:HD:2] if interleaved else dst[:, :, :, 4 * i:4 * i + 4]

        @block.scalar
        def _(act):
            nc.scalar.activation(m.qk[:, :, 0:D], m.ps[:, 0:NT, 0:D], ACT.Copy, scale=scale).then_inc(copied, 1)
            nc.scalar.copy(m.qk[:, :, D:2 * D], m.ps[:, 0:NT, D:2 * D]).then_inc(copied, 1)
            nc.scalar.copy(m.V.rearrange("p t (h e) -> p t h e", h=H)[:, :, :, 0:HD],
                           m.ps[:, 0:NT, 2 * D:3 * D].rearrange("p t (h e) -> p t h e", h=H))

        @block.vector
        def _(dve):
            dve.wait_ge(copied, 2)
            x1, x2 = src[:, :, :, 0:HD:2], src[:, :, :, 1:HD:2]
            full = [P, NT, 2 * H, 4]
            c = m.weight["rope_cos"].rearrange("p (t i) -> p t i", t=NT).unsqueeze(2).to_broadcast(full)
            s = m.weight["rope_sin"].rearrange("p (t i) -> p t i", t=NT).unsqueeze(2).to_broadcast(full)
            tmp = [m.tmp[:, i, :].rearrange("p (t h e) -> p t h e", t=NT, e=4) for i in range(4)]
            nc.vector.tensor_tensor(tmp[0], x1, c, ALU.mult)
            nc.vector.tensor_tensor(tmp[1], x2, s, ALU.mult)
            nc.vector.tensor_tensor(tmp[2], x2, c, ALU.mult)
            nc.vector.tensor_tensor(tmp[3], x1, s, ALU.mult).then_inc(products, 1)
            dve.wait_ge(products, 1)
            nc.vector.tensor_tensor(out_half(0), tmp[0], tmp[1], ALU.subtract)
            nc.vector.tensor_tensor(out_half(1), tmp[2], tmp[3], ALU.add)


def attend_near(nc, m, heads, rows_of, value_of, place_of, sheared):
    units = [(h, qt) for h in range(heads) for qt in range(NT)]
    U = len(units)
    NS, NPR, NTB, NTS = 3, 6, 3, 4
    AVB = NS + NTB
    TURN, WEIGH = 3, 5

    def width(qt):
        return 2 * P if qt else P

    with stage(nc, "scores", "negmax", "exps", "inverted", "scaled", "turned", "pT_ready", "av", "o_out",
               "rel0", "rel1", "rel2", "rel3") as (
            block, scores, negmax, exps, inverted, scaled, turned, pT_ready, av, o_out, *rel_in):
        prob = m.prob.rearrange("p a b -> p (a b)").rearrange("p (a b) -> p a b", b=2 * P)
        pT = m.pT[:, :, :].rearrange("p a b -> p (a b)").rearrange("p (a b) -> p a b", b=2 * P)

        if sheared is not None:
            @block.sync
            def _(sp):
                for h in range(heads):
                    if h >= 4:
                        sp.wait_ge(negmax, NT * (h - 3))
                    sp.dma_start(m.rel[:, h % 4], sheared(h)).then_inc(rel_in[h % 4], 16)

        @block.tensor
        def _(pe):
            for i in range(U + WEIGH):
                if i < U:
                    h, qt = units[i]
                    nk = width(qt)
                    k0 = (qt + 1) * P - nk
                    q, k = rows_of(h)
                    if i >= NS:
                        pe.wait_ge(negmax if sheared is not None else exps, i - NS + 1)
                    ins = nc.tensor.matmul(bank(m, i % NS, nk), q[:, qt * P:(qt + 1) * P], k[:, k0:k0 + nk],
                                           start=True, stop=True)
                    if sheared is None:
                        ins = nc.tensor.matmul(bank(m, i % NS, nk), m.identb, m.negband[:, 2 * P - nk:2 * P],
                                               start=False, stop=True, skip_group_check=True)
                    ins.then_inc(scores, 1)
                if TURN <= i < U + TURN:
                    u = i - TURN
                    nk = width(units[u][1])
                    pe.wait_ge(scaled, u + 1)
                    if u >= NTB:
                        pe.wait_ge(pT_ready, u - NTB + 1)
                    for c in range(nk // P):
                        ins = nc.tensor.transpose(m.ps[:, NS + u % NTB, c * P:(c + 1) * P],
                                                  prob[:, u % NPR, c * P:(c + 1) * P], m.weight["ident"])
                    ins.then_inc(turned, 1)
                if i >= WEIGH:
                    u = i - WEIGH
                    h, qt = units[u]
                    nc_ = width(qt) // P
                    at, chunk, last = place_of(h)
                    pe.wait_ge(pT_ready, u + 1)
                    if at.start == 0 and qt == 0 and chunk >= 2:
                        pe.wait_ge(o_out, chunk - 1)
                    for c in range(nc_):
                        ins = nc.tensor.matmul(m.ps[at, AVB + chunk % 2, qt * P:(qt + 1) * P],
                                               value_of(h, qt + 1 - nc_ + c), pT[:, u % NTS, c * P:(c + 1) * P],
                                               start=(c == 0), stop=(c == nc_ - 1))
                    ins.then_inc(av, 1)

        @block.scalar
        def _(act):
            for i in range(U + TURN):
                if i < U:
                    nk = width(units[i][1])
                    act.wait_ge(negmax, i + 1)
                    if i >= NPR:
                        act.wait_ge(turned, i - NPR + 1)
                    src = bank(m, i % NS, nk) if sheared is None else prob[:, i % NPR, 0:nk]
                    nc.scalar.activation(prob[:, i % NPR, 0:nk], src, ACT.Exp, bias=m.nm[:, i:i + 1],
                                         scale=1.0 if sheared is None else -1.0,
                                         accum_out=m.sums[:, i:i + 1]).then_inc(exps, 1)
                if i >= TURN:
                    u = i - TURN
                    nk = width(units[u][1])
                    act.wait_ge(turned, u + 1)
                    if u >= NTS:
                        act.wait_ge(av, u - NTS + 1)
                    nc.scalar.copy(pT[:, u % NTS, 0:nk], bank(m, NS + u % NTB, nk)).then_inc(pT_ready, 1)

        @block.vector
        def _(dve):
            for i in range(U + WEIGH + 1):
                if i < U:
                    h, qt = units[i]
                    nk = width(qt)
                    dve.wait_ge(scores, i + 1)
                    if sheared is None:
                        nc.vector.tensor_reduce(m.nm[:, i:i + 1], bank(m, i % NS, nk), AX.X, ALU.max,
                                                negate=True).then_inc(negmax, 1)
                    else:
                        if qt == 0:
                            dve.wait_ge(rel_in[h % 4], 16 * (h // 4 + 1))
                        if i >= NPR:
                            dve.wait_ge(turned, i - NPR + 1)
                        nc.vector.tensor_tensor_reduce(prob[:, i % NPR, 0:nk], bank(m, i % NS, nk),
                                                       m.rel[:, h % 4, qt, 2 * P - nk:2 * P], 1.0, -NEG * 4,
                                                       ALU.add, ALU.min, m.nm[:, i:i + 1]).then_inc(negmax, 1)
                if 1 <= i <= U:
                    dve.wait_ge(exps, i)
                    nc.vector.reciprocal(m.rsum[:, i - 1:i], m.sums[:, i - 1:i]).then_inc(inverted, 1)
                    dve.wait_ge(inverted, i)
                    p = prob[:, (i - 1) % NPR, 0:width(units[i - 1][1])]
                    nc.vector.tensor_scalar(p, p, m.rsum[:, i - 1:i], None, ALU.mult).then_inc(scaled, 1)
                if i >= WEIGH + 1:
                    u = i - WEIGH - 1
                    h, qt = units[u]
                    at, chunk, last = place_of(h)
                    if last and qt == NT - 1:
                        dve.wait_ge(av, u + 1)
                        nc.vector.tensor_copy(m.otok[:, chunk, :], bank(m, AVB + chunk % 2)).then_inc(o_out, 1)


def project_turned(nc, m, weight, dst, add):
    with stage(nc, "projected") as (block, projected):
        @block.tensor
        def _(pe):
            for t in range(NT):
                for c in range(4):
                    ins = nc.tensor.matmul(m.ps[:, 4, t * P:(t + 1) * P], m.otok[:, c, t * P:(t + 1) * P],
                                           weight[:, c * D:(c + 1) * D], start=(c == 0), stop=(c == 3))
            ins.then_inc(projected, 1)

        @block.vector
        def _(dve):
            dve.wait_ge(projected, 1)
            nc.vector.tensor_tensor(dst.rearrange("p t d -> p (t d)"), bank(m, 4),
                                    add.rearrange("p t d -> p (t d)"), ALU.add)


def out_project(nc, m, src, weight, row, dst, add, chunks=1):
    with stage(nc, "turned", "oT_ready", "projected") as (block, turned, oT_ready, projected):
        @block.tensor
        def _(pe):
            for c in range(chunks):
                for t in range(NT):
                    ins = nc.tensor.transpose(m.ps[:, c, t * P:(t + 1) * P], src[:, t, c * P:(c + 1) * P],
                                              m.weight["ident"])
                ins.then_inc(turned, 1)
            pe.wait_ge(oT_ready, chunks)
            for t in range(NT):
                for c in range(chunks):
                    ins = nc.tensor.matmul(m.ps[:, 4, t * P:(t + 1) * P], m.oT[:, c, t * P:(t + 1) * P],
                                           weight[:, c * D:(c + 1) * D], start=(c == 0),
                                           stop=(c == chunks - 1 and row is None))
                if row is not None:
                    ins = add_row(nc, m, m.ps[:, 4, t * P:(t + 1) * P], row)
            ins.then_inc(projected, 1)

        @block.scalar
        def _(act):
            for c in range(chunks):
                act.wait_ge(turned, c + 1)
                nc.scalar.copy(m.oT[:, c, :], bank(m, c)).then_inc(oT_ready, 1)

        @block.vector
        def _(dve):
            dve.wait_ge(projected, 1)
            nc.vector.tensor_tensor(dst.rearrange("p t d -> p (t d)"), bank(m, 4),
                                    add.rearrange("p t d -> p (t d)"), ALU.add)



def rank_and_pick(nc, m, dve, step, n, vals, row, chunks, k, picked):
    N = chunks * P
    nc.vector.memset(m.cnt[:, 0:chunks, :], 0.0).then_inc(step, 1)
    dve.wait_ge(step, n.up())
    done = []
    for c in range(chunks):
        v = vals[:, c:c + 1]
        a, b = c * P, (c + 1) * P
        if c >= 2:
            dve.wait_ge(step, done[c - 2])
        junk = m.junk[:, c % 2, :]
        if a > 0:
            nc.vector.tensor_scalar(junk[:, 0:a], row[:, 0:a], v, 0.0, ALU.is_ge, ALU.add,
                                    accum_out=m.cnt[:, c, 0:1]).then_inc(step, 1)
            n.up()
        nc.vector.tensor_scalar(junk[:, a:N], row[:, a:N], v, 0.0, ALU.is_gt, ALU.add,
                                accum_out=m.cnt[:, c, 1:2]).then_inc(step, 1)
        nc.vector.scalar_tensor_tensor(out=m.prob[:, 0, (c % 2) * P:(c % 2 + 1) * P], in0=row[:, a:b], scalar=v,
                                       in1=m.weight["tri"], op0=ALU.is_equal, op1=ALU.mult,
                                       accum_out=m.cnt[:, c, 2:3]).then_inc(step, 1)
        done.append(n.up(2))
    dve.wait_ge(step, n.n)
    nc.vector.tensor_reduce(m.rank[:, 0:chunks], m.cnt[:, 0:chunks, :], AX.X, ALU.add).then_inc(step, 1)
    dve.wait_ge(step, n.up())
    nc.vector.tensor_scalar(picked, m.rank[:, 0:chunks], float(k), None, ALU.is_lt).then_inc(step, 1)
    dve.wait_ge(step, n.up())


def spread_row(nc, m, vals, chunks, first_bank):
    for c in range(chunks):
        ins = nc.tensor.transpose(m.ps[:, first_bank + c // 4, (c % 4) * P:(c % 4 + 1) * P],
                                  vals[:, c:c + 1].to_broadcast([P, P]), m.weight["ident"])
    return ins


def l0_ffn(nc, m):
    CI, CP = NI // P, NP_ // P
    normalize(nc, m, m.x, m.h, out_T=m.hT)
    with stage(nc, "acts_in", "acts_out", "row", "picked", "proc_in", "proc_out", "shifted", "agg_in", "agg",
               "outs_in", "outs", "mixed", "step", "piw_in", "out_w_in") as (
            block, acts_in, acts_out, row, picked, proc_in, proc_out, shifted, agg_in, agg, outs_in, outs, mixed, step,
            piw_in, out_w_in):
        ip = m.weight["ip_T"]
        piw = m.piw.rearrange("p (c n) -> p c n", c=CI)
        pv = m.weight["pv"].rearrange("p (c n) -> p c n", c=CP)
        oiw = m.oiw
        op = m.op.rearrange("p (c n) -> p c n", c=CI)
        flat2 = m.ps[:, 4:6, :].rearrange("p a b -> p (a b)")

        @block.sync
        def _(sp):
            sp.dma_start(m.piw, m.stream[:, 0:8 * NP_]).then_inc(piw_in, 16)
            sp.dma_start(m.oT[:, :, :].rearrange("p a b -> p (a b)"), m.stream[:, 8 * NP_:8 * NP_ + 2 * NI]).then_inc(out_w_in, 16)

        @block.tensor
        def _(pe):
            for c in range(CI):
                if c >= 4:
                    pe.wait_ge(acts_out, c - 3)
                nc.tensor.matmul(bank(m, c % 4), ip[:, c * P:(c + 1) * P], m.hT[:, :],
                                 start=True, stop=True).then_inc(acts_in, 1)
            pe.wait_ge(acts_out, CI)
            spread_row(nc, m, m.acc, CI, 4).then_inc(row, 1)
            pe.wait_ge(picked, 1)
            pe.wait_ge(piw_in, 16)
            for pc in range(CP):
                for c in range(CI):
                    ins = nc.tensor.matmul(m.ps[:, 6, pc:pc + 1], piw[:, c, pc * P:(pc + 1) * P], m.wv[:, c:c + 1],
                                           start=(c == 0), stop=(c == CI - 1))
            ins.then_inc(proc_in, 1)
            pe.wait_ge(proc_out, 1)
            spread_row(nc, m, m.acc, CP, 4).then_inc(row, 1)
            pe.wait_ge(picked, 2)
            for c in range(CP):
                nc.tensor.matmul(m.ps[0:DV, 7, 0:1], pv[:, c, :], m.wv[:, c:c + 1], start=(c == 0), stop=(c == CP - 1))
            for c in range(CP):
                ins = nc.tensor.matmul(m.ps[0:DV, 7, 1:2], m.weight["ones"][:, 0:DV], m.wv[:, c:c + 1],
                                       start=(c == 0), stop=(c == CP - 1))
            ins.then_inc(agg_in, 1)
            pe.wait_ge(agg, 1)
            pe.wait_ge(out_w_in, 16)
            for c in range(CI):
                ins = nc.tensor.matmul(m.ps[:, 6, c:c + 1], oiw[0:DV, c * P:(c + 1) * P], m.aggv[0:DV, 0:1],
                                       start=True, stop=True)
            ins.then_inc(outs_in, 1)
            pe.wait_ge(outs, 1)
            spread_row(nc, m, m.acc, CI, 4).then_inc(row, 1)
            pe.wait_ge(picked, 3)
            for c in range(CI):
                ins = nc.tensor.matmul(bank(m, 7, D), m.wv[:, c:c + 1].to_broadcast([P, P]), op[:, c, :],
                                       start=(c == 0), stop=(c == CI - 1))
            ins.then_inc(mixed, 1)

        @block.scalar
        def _(act):
            for c in range(CI):
                act.wait_ge(acts_in, c + 1)
                if c >= 2:
                    act.wait_ge(acts_out, c - 1)
                nc.scalar.activation(m.actj[:, c % 2, :], bank(m, c % 4), ACT.Gelu,
                                     accum_out=m.acc[:, c:c + 1]).then_inc(acts_out, 1)
            act.wait_ge(proc_in, 1)
            nc.scalar.activation(m.acc[:, 0:CP], m.ps[:, 6, 0:CP], ACT.Gelu).then_inc(proc_out, 1)
            act.wait_ge(shifted, 1)
            nc.scalar.activation(m.ex[:, 0:CP], m.acc[:, 0:CP], ACT.Exp, bias=m.nm[:, 0:1]).then_inc(shifted, 1)
            act.wait_ge(outs_in, 1)
            nc.scalar.activation(m.acc[:, 0:CI], m.ps[:, 6, 0:CI], ACT.Gelu).then_inc(outs, 1)

        @block.vector
        def _(dve):
            n = Count()
            dve.wait_ge(row, 1)
            rank_and_pick(nc, m, dve, step, n, m.acc, flat2, CI, KI, m.pick[:, 0:CI])
            nc.vector.scalar_tensor_tensor(out=m.wv[:, 0:CI], in0=m.acc[:, 0:CI], scalar=1.0 / L, in1=m.pick[:, 0:CI],
                                           op0=ALU.mult, op1=ALU.mult).then_inc(picked, 1)
            dve.wait_ge(row, 2)
            nc.vector.tensor_reduce(m.nm[:, 0:1], bank(m, 4), AX.X, ALU.max, negate=True).then_inc(shifted, 1)
            rank_and_pick(nc, m, dve, step, n, m.acc, bank(m, 4), CP, KP, m.pick[:, 0:CP])
            dve.wait_ge(shifted, 2)
            nc.vector.tensor_tensor(m.wv[:, 0:CP], m.ex[:, 0:CP], m.pick[:, 0:CP], ALU.mult).then_inc(picked, 1)
            dve.wait_ge(agg_in, 1)
            nc.vector.reciprocal(m.aggv[0:DV, 1:2], m.ps[0:DV, 7, 1:2]).then_inc(step, 1)
            dve.wait_ge(step, n.up())
            nc.vector.tensor_tensor(m.aggv[0:DV, 0:1], m.ps[0:DV, 7, 0:1], m.aggv[0:DV, 1:2], ALU.mult).then_inc(agg, 1)
            dve.wait_ge(row, 3)
            rank_and_pick(nc, m, dve, step, n, m.acc, flat2, CI, KI, m.pick[:, 0:CI])
            nc.vector.tensor_tensor(m.wv[:, 0:CI], m.acc[:, 0:CI], m.pick[:, 0:CI], ALU.mult).then_inc(picked, 1)
            dve.wait_ge(mixed, 1)
            for t in range(NT):
                nc.vector.scalar_tensor_tensor(out=m.x[:, t, :], in0=bank(m, 7, D), scalar=0.5, in1=m.x[:, t, :],
                                               op0=ALU.mult, op1=ALU.add)


def l0_attn(nc, m):
    normalize(nc, m, m.x, m.h, clear=True, out_T=m.hT)
    project_tok(nc, m, m.hT, m.weight["l0_qkv"], 3 * D)
    stack_parts(nc, m, -HD ** -0.5, True)
    turn_stacks(nc, m)
    with stage(nc, "rel_ready", "rel_out", "stored") as (block, rel_ready, rel_out, stored):
        @block.tensor
        def _(pe):
            for b in range(4):
                e = b // 2
                for i in range(4):
                    for qt in range(NT):
                        h = 2 * (4 * (b % 2) + i) + e
                        at = (NT * i + qt) * REL
                        ins = nc.tensor.matmul(m.ps[:, b, at:at + REL], m.QX[:, q_slot(h), qt * P:(qt + 1) * P],
                                               m.EX, start=True, stop=True)
                ins.then_inc(rel_ready, 1)

        @block.scalar
        def _(act):
            for b in range(4):
                act.wait_ge(rel_ready, b + 1)
                nc.scalar.copy(m.otok[:, b, :], bank(m, b)).then_inc(rel_out, 1)

        @block.sync
        def _(sp):
            for b in range(4):
                sp.wait_ge(rel_out, b + 1)
                n = NT * 4
                base = RW + b * n * P * RW
                dst = m.shear[base:base + n * P * RW].rearrange("(h i w) -> i h w", h=n, w=RW)[:, :, 0:REL]
                sp.dma_start(dst, m.otok[:, b, :].rearrange("p (h r) -> p h r", h=n)).then_inc(stored, 16)
            sp.wait_ge(stored, 16 * 4)

    def sheared(h):
        return bass.AP(tensor=m.shear.tensor, offset=RW + ((h % 2) * 8 + h // 2) * NT * P * RW - (P - REL + 1),
                       ap=[[RW - 1, P], [P * RW, NT], [1, 2 * P]])

    def rows(h):
        return m.QX[:, q_slot(h), :], m.KX[:, h // 2, :]

    attend_near(nc, m, H, rows, lambda h, kt: m.V[:, kt, 32 * h:32 * h + 32],
                lambda h: (slice(32 * (h % 4), 32 * (h % 4) + 32), h // 4, h % 4 == 3), sheared)
    project_turned(nc, m, m.weight["l0_out"], m.x, m.x)



def gates(nc, m, src_T, weight, row, k, keep_probability):
    with stage(nc, "logits", "shifted", "exped", "step") as (block, logits, shifted, exped, step):
        lg = m.ps[:, 0, 0:NT * NE].rearrange("p (t e) -> p t e", t=NT)
        full = [P, NT, NE]

        @block.tensor
        def _(pe):
            for t in range(NT):
                nc.tensor.matmul(lg[:, t, :], src_T[:, t * P:(t + 1) * P], weight, start=True, stop=False)
                ins = add_row(nc, m, lg[:, t, :], row)
            ins.then_inc(logits, 1)

        @block.scalar
        def _(act):
            act.wait_ge(shifted, 1)
            nc.scalar.activation(m.gp[:, :, :], m.gl[:, :, :], ACT.Exp).then_inc(exped, 1)

        @block.vector
        def _(dve):
            n = Count()
            dve.wait_ge(logits, 1)
            nc.vector.tensor_reduce(m.g4[:, 0:NT], lg, AX.X, ALU.max).then_inc(step, 1)
            dve.wait_ge(step, n.up())
            nc.vector.tensor_tensor(m.gl[:, :, :], lg, m.g4[:, 0:NT].unsqueeze(2).to_broadcast(full),
                                    ALU.subtract).then_inc(shifted, 1)
            dve.wait_ge(exped, 1)
            nc.vector.tensor_reduce(m.g4[:, NT:2 * NT], m.gp[:, :, :], AX.X, ALU.add).then_inc(step, 1)
            dve.wait_ge(step, n.up())
            nc.vector.reciprocal(m.g4[:, 2 * NT:3 * NT], m.g4[:, NT:2 * NT]).then_inc(step, 1)
            dve.wait_ge(step, n.up())
            nc.vector.tensor_tensor(m.gl[:, :, :], m.gp[:, :, :],
                                    m.g4[:, 2 * NT:3 * NT].unsqueeze(2).to_broadcast(full), ALU.mult).then_inc(step, 1)
            dve.wait_ge(step, n.up())
            wide = [P, NT, NE, NE]
            other, own = m.gl[:, :, :].unsqueeze(2).to_broadcast(wide), m.gl[:, :, :].unsqueeze(3).to_broadcast(wide)
            nc.vector.tensor_tensor(m.cmp[:, 0], other, own, ALU.is_gt).then_inc(step, 1)
            nc.vector.tensor_tensor(m.cmp[:, 1], other, own, ALU.is_equal).then_inc(step, 1)
            dve.wait_ge(step, n.up(2))
            tri8 = m.weight["tri8"].unsqueeze(1).to_broadcast([P, NT, NE * NE])
            nc.vector.tensor_tensor(m.cmp[:, 1].rearrange("p t a b -> p t (a b)"),
                                    m.cmp[:, 1].rearrange("p t a b -> p t (a b)"), tri8, ALU.mult).then_inc(step, 1)
            dve.wait_ge(step, n.up())
            nc.vector.tensor_tensor(m.cmp[:, 0], m.cmp[:, 0], m.cmp[:, 1], ALU.add).then_inc(step, 1)
            dve.wait_ge(step, n.up())
            nc.vector.tensor_reduce(m.grank[:, :, :], m.cmp[:, 0], AX.X, ALU.add).then_inc(step, 1)
            dve.wait_ge(step, n.up())
            if keep_probability:
                nc.vector.scalar_tensor_tensor(out=m.sel[:, :, :], in0=m.grank[:, :, :], scalar=float(k),
                                               in1=m.gl[:, :, :], op0=ALU.is_lt, op1=ALU.mult)
            else:
                nc.vector.tensor_scalar(m.sel[:, :, :], m.grank[:, :, :], float(k), None, ALU.is_lt)



def l1_ffn(nc, m):
    normalize(nc, m, m.x, m.h, clear=True)
    with stage(nc, "products") as (block, products):
        @block.vector
        def _(dve):
            x = m.h[:, :, :].rearrange("p t (h e) -> p t h e", e=HD)
            o = m.y[:, :, :].rearrange("p t (h e) -> p t h e", e=HD)
            x1, x2 = x[:, :, :, 0:HD:2], x[:, :, :, 1:HD:2]
            full = [P, NT, H, 4]
            c = m.weight["rope_cos"].rearrange("p (t i) -> p t i", t=NT).unsqueeze(2).to_broadcast(full)
            s = m.weight["rope_sin"].rearrange("p (t i) -> p t i", t=NT).unsqueeze(2).to_broadcast(full)
            tmp = [m.tmp[:, i, 0:NT * H * 4].rearrange("p (t h e) -> p t h e", t=NT, e=4) for i in range(4)]
            nc.vector.tensor_tensor(tmp[0], x1, c, ALU.mult)
            nc.vector.tensor_tensor(tmp[1], x2, s, ALU.mult)
            nc.vector.tensor_tensor(tmp[2], x1, s, ALU.mult)
            nc.vector.tensor_tensor(tmp[3], x2, c, ALU.mult).then_inc(products, 1)
            dve.wait_ge(products, 1)
            nc.vector.tensor_tensor(o[:, :, :, 0:HD:2], tmp[0], tmp[1], ALU.subtract)
            nc.vector.tensor_tensor(o[:, :, :, 1:HD:2], tmp[2], tmp[3], ALU.add)
    turn_tok(nc, m, (m.y, m.hT), (m.h, m.hT2))
    with stage(nc) as (block,):
        @block.tensor
        def _(pe):
            qkv = m.weight["l1f_qkv"]
            for t in range(NT):
                for src, a, b in ((m.hT, 0, 2 * D), (m.hT2, 2 * D, 3 * D)):
                    nc.tensor.matmul(m.ps[:, t, a:b], src[:, t * P:(t + 1) * P], qkv[:, a:b], start=True, stop=False)
                    add_row(nc, m, m.ps[:, t, a:b], "l1f_qkv_b", a, b)
    stack_parts(nc, m, HD ** -0.5, True)
    turn_stacks(nc, m)
    attend8(nc, m, CAUSAL)
    divide(nc, m)
    out_project(nc, m, m.ot, m.weight["l1f_out"], "l1f_out_b", m.y, m.h)
    normalize(nc, m, m.y, m.y, gain=m.weight["l1f_ln1_w"], shift=m.weight["l1f_ln1_b"], out_T=m.hT)
    gates(nc, m, m.hT, m.weight["l1f_gate"], "l1f_gate_b", 2, True)
    with stage(nc, "experts", "summed") as (block, experts, summed):
        HW = NE * D // 2

        @block.tensor
        def _(pe):
            for t in range(NT):
                for s in range(2):
                    u = 2 * t + s
                    if u >= 4:
                        pe.wait_ge(summed, NE // 2 * (u - 3))
                    nc.tensor.matmul(bank(m, u % 4), m.hT[:, t * P:(t + 1) * P],
                                     m.weight["l1f_exp"][:, s * HW:(s + 1) * HW], start=True, stop=False)
                    add_row(nc, m, bank(m, u % 4), "l1f_exp_b", s * HW, (s + 1) * HW).then_inc(experts, 1)

        @block.vector
        def _(dve):
            for t in range(NT):
                for e in range(NE):
                    u = 2 * t + e // 4
                    if e % 4 == 0:
                        dve.wait_ge(experts, u + 1)
                    if e > 0:
                        dve.wait_ge(summed, NE * t + e)
                    nc.vector.scalar_tensor_tensor(out=m.y[:, t, :], in0=m.ps[:, u % 4, (e % 4) * D:(e % 4 + 1) * D],
                                                   scalar=m.sel[:, t, e:e + 1], in1=m.y[:, t, :],
                                                   op0=ALU.mult, op1=ALU.add).then_inc(summed, 1)
    normalize(nc, m, m.y, m.y, gain=m.weight["l1f_ln2_w"], shift=m.weight["l1f_ln2_b"])
    add_scaled(nc, m, m.x[:, :, :], m.y[:, :, :], 0.5)


def l1_attn(nc, m):
    normalize(nc, m, m.x, m.h, clear=True, out_T=m.hT)
    project_tok(nc, m, m.hT, m.weight["l1a_qkvb"], 3 * D + H, "l1a_bb", 3 * D)
    with stage(nc, "squared", "summed", "rooted", "beta_ready", "step") as (
            block, squared, summed, rooted, beta_ready, step):
        @block.scalar
        def _(act):
            nc.scalar.activation(m.qk[:, :, :], m.ps[:, 0:NT, 0:2 * D], ACT.Square).then_inc(squared, 1)
            nc.scalar.activation(m.beta[:, :, :], m.ps[:, 0:NT, 3 * D:3 * D + H], ACT.Sigmoid).then_inc(beta_ready, 1)

        @block.gpsimd
        def _(pool):
            pool.wait_ge(summed, 1)
            nc.gpsimd.tensor_tensor(m.ss[:, 1, :], m.ss[:, 0, :], m.weight["half"], ALU.pow).then_inc(rooted, 1)

        @block.vector
        def _(dve):
            dve.wait_ge(squared, 1)
            nc.vector.tensor_reduce(m.ss[:, 0, :].rearrange("p (t h) -> p t h", t=NT),
                                    m.qk[:, :, :].rearrange("p t (h e) -> p t h e", e=HD),
                                    AX.X, ALU.add).then_inc(summed, 1)
            dve.wait_ge(beta_ready, 1)
            dve.wait_ge(rooted, 1)
            nc.vector.tensor_scalar(m.ss[:, 0, :], m.ss[:, 1, :], 1e-12, None, ALU.max).then_inc(step, 1)
            dve.wait_ge(step, 1)
            nc.vector.reciprocal(m.ss[:, 1, :], m.ss[:, 0, :]).then_inc(step, 1)
            dve.wait_ge(step, 2)
            nc.vector.tensor_tensor(m.raw[:, :, :].rearrange("p t (h e) -> p t h e", e=HD),
                                    m.ps[:, 0:NT, 0:2 * D].rearrange("p t (h e) -> p t h e", e=HD),
                                    m.ss[:, 1, :].rearrange("p (t h) -> p t h", t=NT).unsqueeze(3).to_broadcast(
                                        [P, NT, 2 * H, HD]), ALU.mult)
            nc.vector.tensor_tensor(m.V.rearrange("p t (h e) -> p t h e", h=H)[:, :, :, 0:HD],
                                    m.ps[:, 0:NT, 2 * D:3 * D].rearrange("p t (h e) -> p t h e", e=HD),
                                    m.beta[:, :, :].unsqueeze(3).to_broadcast([P, NT, H, HD]), ALU.mult)
    stack_parts(nc, m, 1.0, False)
    turn_stacks(nc, m)
    turn_tok(nc, m, (m.raw[:, :, 0:D], m.hT))
    with stage(nc, "states", "state_ready", "scores", "masked", "av", "o_out") as (
            block, states, state_ready, scores, masked, av, o_out):
        units = [(g, t) for g in range(4) for t in range(NT)]
        U = len(units)
        order = [0, 2, 1, 3]

        @block.tensor
        def _(pe):
            for t in range(NT - 1):
                nc.tensor.matmul(bank(m, 4 + t), m.raw[:, t, D:2 * D], m.V[:, t, :], start=True, stop=True).then_inc(states, 1)
            for i in range(U + 1):
                if i < U:
                    g, t = units[i]
                    if i >= 2:
                        pe.wait_ge(masked, i - 1)
                    for n, j in enumerate(order):
                        h = 4 * g + j
                        ins = nc.tensor.matmul(m.ps[:, 2 * (i % 2) + n // 2, (n % 2) * P:(n % 2 + 1) * P],
                                               m.KX[:, h // 2, t * P:(t + 1) * P], m.QX[:, q_slot(h), t * P:(t + 1) * P],
                                               start=True, stop=True)
                    ins.then_inc(scores, 1)
                if i >= 1:
                    g, t = units[i - 1]
                    out = m.ps[:, 4 + g % 2, t * P:(t + 1) * P]
                    if i == 1:
                        pe.wait_ge(state_ready, 2 * NT - 3)
                    if t == 0 and g >= 2:
                        pe.wait_ge(o_out, g - 1)
                    if t > 0:
                        nc.tensor.matmul(out, m.state[:, t - 1, g * P:(g + 1) * P], m.hT[:, t * P:(t + 1) * P],
                                         start=True, stop=True)
                    pe.wait_ge(masked, i)
                    for n, j in enumerate(order):
                        h = 4 * g + j
                        ins = nc.tensor.matmul(out[32 * j:32 * j + 32], m.V[:, t, 32 * h:32 * h + 32],
                                               m.prob[:, (i - 1) % 2, n * P:(n + 1) * P], start=(t == 0), stop=True,
                                               skip_group_check=True)
                    ins.then_inc(av, 1)

        @block.vector
        def _(dve):
            same_head = m.weight["blockdiag"].rearrange("p (h e) -> p h e", e=HD)[:, :, 0:1].to_broadcast([P, H, 32])
            for t in range(NT - 1):
                dve.wait_ge(states, t + 1)
                nc.vector.tensor_tensor(m.state[:, t, :].rearrange("p (h e) -> p h e", e=32),
                                        bank(m, 4 + t).rearrange("p (h e) -> p h e", e=32), same_head,
                                        ALU.mult).then_inc(state_ready, 1)
            for t in range(1, NT - 1):
                dve.wait_ge(state_ready, NT - 2 + t)
                nc.vector.tensor_tensor(m.state[:, t, :], m.state[:, t, :], m.state[:, t - 1, :],
                                        ALU.add).then_inc(state_ready, 1)
            for i in range(U):
                dve.wait_ge(scores, i + 1)
                if i >= 2:
                    dve.wait_ge(av, i - 1)
                nc.vector.tensor_tensor(m.prob[:, i % 2, :].rearrange("p (b j q) -> p b j q", b=2, j=2),
                                        m.ps[:, 2 * (i % 2):2 * (i % 2) + 2, 0:2 * P].rearrange("p b (j q) -> p b j q", j=2),
                                        m.weight["causalT"].unsqueeze(1).unsqueeze(1).to_broadcast([P, 2, 2, P]),
                                        ALU.mult).then_inc(masked, 1)

        @block.scalar
        def _(act):
            for g in range(4):
                act.wait_ge(av, 4 * (g + 1))
                nc.scalar.copy(m.otok[:, g, :], bank(m, 4 + g % 2)).then_inc(o_out, 1)
    project_turned(nc, m, m.weight["l1a_out"], m.x, m.x)



def l2_ffn(nc, m):
    normalize(nc, m, m.x, m.h, out_T=m.hT)
    gates(nc, m, m.hT, m.weight["l2f_rw"], "l2f_rb", 1, False)
    w1 = m.weight["l2f_w1"].rearrange("p (e f) -> p e f", e=NE)
    b1 = m.weight["l2f_b1"].rearrange("p (e c) -> p e c", e=NE)
    w2 = m.weight["l2f_w2"].rearrange("p (e c d) -> p e c d", e=NE, c=NC2)
    units = [(e, c) for e in range(NE) for c in range(NC2)]
    U = len(units)
    LAG = 2
    with stage(nc, "pair", "sig", "gated", "mixed", "summed", "zeroed") as (
            block, pair, sig, gated, mixed, summed, zeroed):
        @block.tensor
        def _(pe):
            def mix(e):
                pe.wait_ge(gated, NC2 * (e + 1))
                if e >= 2:
                    pe.wait_ge(summed, NT * (e - 1))
                for t in range(NT):
                    for c in range(NC2):
                        nc.tensor.matmul(m.ps[:, 4 + e % 2, t * P:(t + 1) * P],
                                         m.act[:, e % 2, c, t * P:(t + 1) * P], w2[:, e, c, :],
                                         start=(c == 0), stop=False)
                    ins = add_row(nc, m, m.ps[:, 4 + e % 2, t * P:(t + 1) * P], "l2f_b2", e * D, (e + 1) * D)
                ins.then_inc(mixed, 1)

            for u, (e, c) in enumerate(units):
                if u >= 2:
                    pe.wait_ge(gated, u - 1)
                for s in range(2):
                    at = s * HID2 + c * P
                    ins = nc.tensor.matmul(bank(m, 2 * (u % 2) + s), w1[:, e, at:at + P], m.hT[:, :],
                                           start=True, stop=True)
                ins.then_inc(pair, 1)
                if e >= 1 and c == LAG:
                    mix(e - 1)
            mix(NE - 1)

        @block.scalar
        def _(act):
            for u, (e, c) in enumerate(units):
                act.wait_ge(pair, u + 1)
                if u >= 2:
                    act.wait_ge(gated, u - 1)
                nc.scalar.activation(m.actj[:, u % 2, :], bank(m, 2 * (u % 2) + 1), ACT.Sigmoid,
                                     bias=b1[:, e, NC2 + c:NC2 + c + 1]).then_inc(sig, 1)

        @block.vector
        def _(dve):
            def weigh(e):
                dve.wait_ge(mixed, e + 1)
                if e > 0:
                    dve.wait_ge(summed, NT * e)
                for t in range(NT):
                    nc.vector.scalar_tensor_tensor(out=m.y[:, t, :], in0=m.ps[:, 4 + e % 2, t * P:(t + 1) * P],
                                                   scalar=m.sel[:, t, e:e + 1], in1=m.y[:, t, :],
                                                   op0=ALU.mult, op1=ALU.add).then_inc(summed, 1)

            nc.vector.memset(m.y[:, :, :], 0.0).then_inc(zeroed, 1)
            dve.wait_ge(zeroed, 1)
            for u, (e, c) in enumerate(units):
                dve.wait_ge(sig, u + 1)
                if c == 0 and e >= 2:
                    dve.wait_ge(mixed, e - 1)
                nc.vector.scalar_tensor_tensor(out=m.act[:, e % 2, c, :], in0=bank(m, 2 * (u % 2)),
                                               scalar=b1[:, e, c:c + 1], in1=m.actj[:, u % 2, :],
                                               op0=ALU.add, op1=ALU.mult).then_inc(gated, 1)
                if c == NC2 - 1 and e >= 1:
                    weigh(e - 1)
            weigh(NE - 1)
            dve.wait_ge(summed, NT * NE)
            nc.vector.scalar_tensor_tensor(out=m.x[:, :, :], in0=m.y[:, :, :], scalar=0.5, in1=m.x[:, :, :],
                                           op0=ALU.mult, op1=ALU.add)


def l2_attn(nc, m):
    normalize(nc, m, m.x, m.h, clear=True, out_T=m.hT)
    project_tok(nc, m, m.hT, m.weight["l2a_qkv"], 3 * D)
    rope_heads(nc, m, HD ** -0.5, interleaved=False)
    stack_parts(nc, m, 1.0, False)
    turn_stacks(nc, m)
    attend8(nc, m, BLOCK32)
    divide(nc, m)
    out_project(nc, m, m.ot, m.weight["l2a_out"], None, m.x, m.x)



def l3_attn(nc, m):
    normalize(nc, m, m.x, m.h, clear=True, out_T=m.hT)
    project_tok(nc, m, m.hT, m.weight["l3a_qkv"], 3 * D, "l3a_qkv_b", 0)
    rope_heads(nc, m, HD ** -0.5, interleaved=True)
    stack_parts(nc, m, 1.0, False)
    turn_stacks(nc, m)
    attend8(nc, m, FULL)
    divide(nc, m)
    out_project(nc, m, m.ot, m.weight["l3a_out"], "l3a_out_b", m.x, m.x)


def shift_tokens(nc, m, src, dst):
    half = D // 2
    with stage(nc, "moved") as (block, moved):
        @block.sync
        def _(sp):
            sp.dma_start(dst[1:P, :, half:D], src[0:P - 1, :, half:D]).then_inc(moved, 16)
            sp.dma_start(dst[0:1, 1:NT, half:D], src[P - 1:P, 0:NT - 1, half:D]).then_inc(moved, 16)
            sp.wait_ge(moved, 32)

        @block.gpsimd
        def _(pool):
            nc.gpsimd.memset(dst[0:1, 0, half:D], 0.0)

        @block.vector
        def _(dve):
            nc.vector.tensor_copy(dst[:, :, 0:half], src[:, :, 0:half])


def l3_layer(nc, m, l):
    shift_tokens(nc, m, m.y, m.h)
    turn_tok(nc, m, (m.h, m.hT))
    qkv = m.weight["l3f_qkv"].rearrange("p (l s n) -> p l s n", l=DEPTH, s=3)
    with stage(nc, "projected", "squared", "summed", "rooted", "v_out", "step", "scaled", "roped") as (
            block, projected, squared, summed, rooted, v_out, step, scaled, roped):
        def heads(ap):
            return ap.rearrange("p (s h e) -> p s h e", s=2, e=LHD)

        full = [P, 2, LH, LHD]

        @block.tensor
        def _(pe):
            for t in range(NT):
                b = 3 * (t % 2)
                if t >= 2:
                    pe.wait_ge(scaled, t - 1)
                    pe.wait_ge(v_out, t - 1)
                for s in range(3):
                    ins = nc.tensor.matmul(bank(m, b + s), m.hT[:, t * P:(t + 1) * P], qkv[:, l, s, :],
                                           start=True, stop=True)
                ins.then_inc(projected, 1)

        @block.scalar
        def _(act):
            for t in range(NT):
                b = 3 * (t % 2)
                act.wait_ge(projected, t + 1)
                if t >= 1:
                    act.wait_ge(summed, t)
                nc.scalar.activation(m.sq[:, :], m.ps[:, b:b + 2, :].rearrange("p a b -> p (a b)"),
                                     ACT.Square).then_inc(squared, 1)
                nc.scalar.copy(m.V[:, t, :], bank(m, b + 2)).then_inc(v_out, 1)

        @block.gpsimd
        def _(pool):
            for t in range(NT):
                pool.wait_ge(summed, t + 1)
                nc.gpsimd.tensor_tensor(m.ss[:, 1, 0:2 * LH], m.ss[:, 0, 0:2 * LH], m.weight["half"][:, 0:2 * LH],
                                        ALU.pow).then_inc(rooted, 1)

        @block.vector
        def _(dve):
            n = Count()
            cs, sn = m.rotary["cos"][:, l], m.rotary["sin"][:, l]
            hl = LHD // 2

            def sum_squares(t):
                dve.wait_ge(squared, t + 1)
                if t >= 1:
                    dve.wait_ge(rooted, t)
                nc.vector.tensor_reduce(m.ss[:, 0, 0:2 * LH], m.sq[:, :].rearrange("p (h e) -> p h e", e=LHD),
                                        AX.X, ALU.add).then_inc(summed, 1)

            sum_squares(0)
            for t in range(NT):
                b = 3 * (t % 2)
                dve.wait_ge(rooted, t + 1)
                nc.vector.tensor_scalar(m.ss[:, 2, 0:2 * LH], m.ss[:, 1, 0:2 * LH], 1e-12, None,
                                        ALU.max).then_inc(step, 1)
                dve.wait_ge(step, n.up())
                nc.vector.reciprocal(m.ss[:, 3, 0:2 * LH], m.ss[:, 2, 0:2 * LH]).then_inc(step, 1)
                dve.wait_ge(step, n.up())
                if t + 1 < NT:
                    sum_squares(t + 1)
                nc.vector.tensor_tensor(m.qn[:, t % 2, :].rearrange("p (h e) -> p h e", e=LHD),
                                        m.ps[:, b:b + 2, :].rearrange("p a (h e) -> p (a h) e", e=LHD),
                                        m.ss[:, 3, 0:2 * LH].unsqueeze(2).to_broadcast([P, 2 * LH, LHD]),
                                        ALU.mult).then_inc(scaled, 1)
                dve.wait_ge(scaled, t + 1)
                nc.vector.tensor_tensor(heads(m.qt3[:, t, :]), heads(m.qn[:, t % 2, :]),
                                        cs[:, t, :, :].unsqueeze(2).to_broadcast(full), ALU.mult).then_inc(step, 1)
                n.up()
                if t >= 1:
                    dve.wait_ge(roped, t)
                x, o = heads(m.qn[:, t % 2, :]), heads(m.rot[:, :])
                for a, z in ((0, hl), (hl, 0)):
                    nc.vector.tensor_tensor(o[:, :, :, a:a + hl], x[:, :, :, z:z + hl],
                                            sn[:, t, :, a:a + hl].unsqueeze(2).to_broadcast([P, 2, LH, hl]),
                                            ALU.mult).then_inc(step, 1)
                dve.wait_ge(step, n.up(2))
                nc.vector.tensor_tensor(m.qt3[:, t, :], m.qt3[:, t, :], m.rot[:, :], ALU.add).then_inc(roped, 1)
    with stage(nc, "turned") as (block, turned):
        @block.tensor
        def _(pe):
            for c in range(8):
                for t in range(NT):
                    ins = nc.tensor.transpose(m.ps[:, c, t * P:(t + 1) * P], m.qt3[:, t, c * P:(c + 1) * P],
                                              m.weight["ident"])
                ins.then_inc(turned, 1)

        @block.scalar
        def _(act):
            for c in range(4):
                act.wait_ge(turned, c + 1)
                copy_pair(nc.scalar.copy, lambda e: m.QP[:, 2 * c + e, :], bank(m, c))

        @block.vector
        def _(dve):
            for c in range(4):
                dve.wait_ge(turned, 4 + c + 1)
                nc.vector.tensor_copy(m.KP[:, c, :], bank(m, 4 + c))

    def rows(h):
        return m.QP[:, h, :], m.KP[:, h // 2, :]

    attend_near(nc, m, LH, rows, lambda h, kt: m.V[:, kt, LHD * h:LHD * (h + 1)],
                lambda h: (slice(LHD * (h % 2), LHD * (h % 2) + LHD), h // 2, h % 2 == 1), None)
    project_turned(nc, m, m.weight["l3f_wo"][:, l * 4 * D:(l + 1) * 4 * D], m.y, m.y)
    shift_tokens(nc, m, m.y, m.h)
    normalize(nc, m, m.h, m.h, out_T=m.hT, col_gain=m.weight["l3f_lng"][:, l:l + 1], col_shift=m.weight["l3f_lnb"][:, l:l + 1])
    w1 = m.weight["l3f_w1"].rearrange("p (l f) -> p l f", l=DEPTH)
    b1 = m.weight["l3f_b1"].rearrange("p (l s c) -> p l s c", l=DEPTH, s=2)
    w2 = m.weight["l3f_w2"].rearrange("p (l c d) -> p l c d", l=DEPTH, c=NC3)
    with stage(nc, "pair", "gelus", "gated", "mixed") as (block, pair, gelus, gated, mixed):
        size = [min(P, HID3 - c * P) for c in range(NC3)]

        @block.tensor
        def _(pe):
            for c in range(NC3):
                for s in range(2):
                    at = s * HID3 + c * P
                    ins = nc.tensor.matmul(m.ps[0:size[c], 2 * c + s, :], w1[:, l, at:at + size[c]], m.hT[:, :],
                                           start=True, stop=True)
                ins.then_inc(pair, 1)
            pe.wait_ge(gated, NC3)
            for t in range(NT):
                for c in range(NC3):
                    nc.tensor.matmul(m.ps[:, 6, t * P:(t + 1) * P], m.act3[0:size[c], c, t * P:(t + 1) * P],
                                     w2[0:size[c], l, c, :], start=(c == 0), stop=False)
                ins = add_row(nc, m, m.ps[:, 6, t * P:(t + 1) * P], "l3f_b2", l * D, (l + 1) * D)
            ins.then_inc(mixed, 1)

        @block.scalar
        def _(act):
            for c in range(NC3):
                act.wait_ge(pair, c + 1)
                nc.scalar.activation(m.prob[0:size[c], c, :], m.ps[0:size[c], 2 * c + 1, :], ACT.Gelu,
                                     bias=b1[0:size[c], l, 1, c:c + 1]).then_inc(gelus, 1)

        @block.vector
        def _(dve):
            for c in range(NC3):
                dve.wait_ge(gelus, c + 1)
                nc.vector.scalar_tensor_tensor(out=m.act3[0:size[c], c, :], in0=m.ps[0:size[c], 2 * c, :],
                                               scalar=b1[0:size[c], l, 0, c:c + 1], in1=m.prob[0:size[c], c, :],
                                               op0=ALU.add, op1=ALU.mult).then_inc(gated, 1)
            dve.wait_ge(mixed, 1)
            nc.vector.tensor_tensor(m.y[:, :, :].rearrange("p t d -> p (t d)"), bank(m, 6),
                                    m.y[:, :, :].rearrange("p t d -> p (t d)"), ALU.add)


def l3_ffn(nc, m):
    normalize(nc, m, m.x, m.y)
    for l in range(DEPTH):
        l3_layer(nc, m, l)
    add_scaled(nc, m, m.x[:, :, :], m.y[:, :, :], 0.5)



def macaron(nc, packs, stream, rel_emb, rows, masks, rope3, qk_scale, x_in, out):
    ctx = ExitStack()
    with ctx:
        def sb(name, *shape, dt=F32):
            return ctx.enter_context(nc.sbuf_tensor(name, [P, *shape], dt))[(slice(None),) * (1 + len(shape))]

        m = Buffers()
        m.ps = ctx.enter_context(nc.psum_tensor("ps", [P, 8, 512], F32))
        m.ps = m.ps[:, :, :]
        m.psb = m.ps.bitcast(BF16)
        m.x, m.h, m.y = sb("x", NT, D), sb("h", NT, D), sb("y", NT, D)
        m.hT = sb("hT", L)
        m.QP, m.KP = sb("QP", LH, L), sb("KP", 4, L)
        m.oT = m.KP
        m.QX, m.KX = m.QP.bitcast(BF16).rearrange("p a b -> p (a b)").rearrange("p (a b) -> p a b", b=L), \
            m.KP.bitcast(BF16).rearrange("p a b -> p (a b)").rearrange("p (a b) -> p a b", b=L)
        m.V, m.otok = sb("V", NT, INNER), sb("otok", NT, INNER)
        m.stk = sb("stk", NT, 2, H, 64, dt=BF16)
        m.prob, m.pT = sb("prob", 3, 512), sb("pT", 2, 512)
        big = sb("big", 16 * 256)
        m.piw = big[:, :]
        m.oiw, m.op = m.oT[:, 0:2, :].rearrange("p a b -> p (a b)"), m.oT[:, 2:4, :].rearrange("p a b -> p (a b)")
        m.rel = big[:, :].rearrange("p (h q j) -> p h q j", h=4, q=NT)
        m.act = big[:, :].rearrange("p (s c t) -> p s c t", s=2, c=NC2)
        m.qt3 = big[:, :].rearrange("p (t n) -> p t n", t=NT)
        m.raw = big[:, 0:NT * 2 * D].rearrange("p (t n) -> p t n", t=NT)
        m.tmp = big[:, 4 * NT * D:4 * NT * D + 4 * 512].rearrange("p (i n) -> p i n", i=4)
        m.ot = big[:, 0:NT * D].rearrange("p (t n) -> p t n", t=NT)
        m.qk = big[:, NT * 2 * D:2 * NT * 2 * D].rearrange("p (t n) -> p t n", t=NT)
        m.qn = m.otok[:, :, :].rearrange("p (a b) n -> p a (b n)", a=2)
        m.rot = m.prob[:, 0:2, :].rearrange("p a b -> p (a b)")
        m.sq = m.pT[:, :, :].rearrange("p a b -> p (a b)")
        m.state = m.tmp.rearrange("p i n -> p (i n)")[:, 0:(NT - 1) * 4 * P].rearrange("p (t n) -> p t n", n=4 * P)
        m.actj = m.pT
        m.hT2 = m.pT[:, 0, :]
        m.junk = m.otok.rearrange("p a b -> p (a b)")[:, 0:2 * NI].rearrange("p (a b) -> p a b", a=2)
        m.act3 = m.V
        m.st6, m.mv = sb("st6", NT, 6), sb("mv", NT, 2)
        m.ve, m.rstd = sb("ve", NT), sb("rstd", NT)
        m.nm, m.sums, m.rsum = sb("nm", NT * H), sb("sums", NT * H), sb("rsum", NT * H)
        m.acc, m.wv, m.ex, m.pick, m.rank = sb("acc", 8), sb("wv", 8), sb("ex", 8), sb("pick", 8), sb("rank", 8)
        m.cnt, m.aggv = sb("cnt", 8, 4), sb("aggv", 2)
        m.gp, m.gl, m.g4, m.sel, m.grank = (sb("gp", NT, NE), sb("gl", NT, NE), sb("g4", 3 * NT),
                                            sb("sel", NT, NE), sb("grank", NT, NE))
        m.cmp = m.pT[:, 0, :].rearrange("p (i t a b) -> p i t a b", i=2, t=NT, a=NE)
        m.ss, m.beta = sb("ss", 4, NT * 2 * H), sb("beta", NT, H)
        m.identb, m.negcausal, m.negblock = sb("identb", P, dt=BF16), sb("negcausal", P, dt=BF16), sb("negblock", P, dt=BF16)
        m.negband = sb("negband", 2 * P, dt=BF16)
        m.rotary["cos"], m.rotary["sin"] = sb("cos3", DEPTH, NT, 2, LHD), sb("sin3", DEPTH, NT, 2, LHD)
        m.EX = sb("EX", REL, dt=BF16)
        neg = m.KP[:, 0:1, :]

        wt = []
        for i, fields in enumerate(LEVELS):
            offs, total = offsets(fields)
            t = sb(f"weights{i}", total)
            wt.append(t)
            for name, (a, n) in offs.items():
                m.weight[name] = t[:, a:a + n]
        m.stream = stream
        m.rowparts = sb("rowparts", ROW_COLS, dt=BF16)
        m.onesb = sb("onesb", P, dt=BF16)
        for i, fields in enumerate(ROWS):
            for name, (a, n) in offsets(fields)[0].items():
                m.row_at[name] = (32 * i, a, n)

        nrows = NT * H * P + 2
        m.shear = nc.dram_tensor("shear", [nrows * RW], F32).ap()
        loaded = [ctx.enter_context(nc.semaphore(f"weights{i}_loaded")) for i in range(len(LEVELS))]

        with stage(nc, "small_in", "neg_set", "neg_out", "row_in", "rope_in", "emb_in", "estep", "masks_set", "e_turned",
                   "row_zero", "row_step", "row_moved") as (
                block, small_in, neg_set, neg_out, row_in, rope_in, emb_in, estep, masks_set, e_turned,
                row_zero, row_step, row_moved):
            rt = big[:, 0:2 * NT * 2 * LHD].rearrange("p (a t s e) -> p a t s e", a=2, t=NT, s=2)
            qs = big[:, 4 * NT * LHD:4 * NT * LHD + DEPTH * 2 * LHD].rearrange("p (l s e) -> p l s e", l=DEPTH, s=2)
            mk = big[:, 2048:2048 + 5 * P]
            rowf = [m.V.rearrange("p a b -> p (a b)")[:, i * ROW_COLS:(i + 1) * ROW_COLS] for i in range(2)]
            rowp = [m.otok.rearrange("p a b -> p (a b)")[:, i * 512:(i + 1) * 512].bitcast(BF16) for i in range(3)]
            emb = [big[0:REL, 3072 + i * HD:3072 + (i + 1) * HD] for i in range(3)]
            est = m.prob[0:REL, 0, 0:64].bitcast(BF16)

            @block.sync
            def _(sp):
                for i in range(len(LEVELS)):
                    sp.dma_start(wt[i][:, :], packs[i]).then_inc(loaded[i], 16)
                sp.wait_ge(neg_set, 1)
                body = m.shear[0:(nrows - 2) * RW].rearrange("(a p w) -> p a w", p=P, w=2 * RW)
                per = body.shape[1]
                for a in range(per):
                    sp.dma_start(body[:, a, :], neg[:, 0, :]).then_inc(neg_out, 16)
                sp.dma_start(m.shear[(nrows - 2) * RW:nrows * RW].rearrange("(p w) -> p w", p=1),
                             neg[0:1, 0, :]).then_inc(neg_out, 16)
                sp.wait_ge(neg_out, 16 * (per + 1))

            @block.tensor
            def _(pe):
                pe.wait_ge(masks_set, 1)
                pe.wait_ge(estep, 1 + 2 * 6 + 2)
                nc.tensor.transpose(m.psb[:, 0, 0:REL], est, m.identb[0:REL, 0:REL]).then_inc(e_turned, 1)

            @block.scalar
            def _(act):
                act.dma_start(emb[0], rel_emb).then_inc(emb_in, 16)
                act.wait_ge(row_zero, 1)
                for i, fields in enumerate(ROWS):
                    n = offsets(fields)[1]
                    act.dma_start(rowf[0][32 * i:32 * i + 1, 0:n], rows[i:i + 1, 0:n]).then_inc(row_in, 16)
                act.dma_start(mk, masks).then_inc(small_in, 16)
                act.dma_start(rt.rearrange("p a t s e -> p (a t s e)"), rope3).then_inc(rope_in, 16)
                act.dma_start(qs.rearrange("p l s e -> p (l s e)"),
                              qk_scale.to_broadcast([P, DEPTH * 2 * LHD])).then_inc(rope_in, 16)
                act.wait_ge(row_step, 5)
                for i in range(len(ROWS)):
                    for k in range(3):
                        act.dma_start(m.rowparts[32 * i + k:32 * i + k + 1, :],
                                      rowp[k][32 * i:32 * i + 1, :]).then_inc(row_moved, 16)
                act.wait_ge(row_moved, 16 * 3 * len(ROWS))
                for i in range(len(LEVELS)):
                    act.wait_ge(loaded[i], 16)

            @block.gpsimd
            def _(pool):
                nc.gpsimd.memset(neg, -NEG).then_inc(neg_set, 1)
                nc.gpsimd.memset(m.stk[:, :, :, :, :], 0.0)
                nc.gpsimd.memset(m.QP[:, :, :], 0.0)

            @block.vector
            def _(dve):
                nc.vector.memset(rowf[0], 0.0).then_inc(row_zero, 1)
                nc.vector.memset(m.onesb, 1.0)
                dve.wait_ge(row_in, 16 * len(ROWS))
                nc.vector.tensor_copy(rowp[0], rowf[0]).then_inc(row_step, 1)
                dve.wait_ge(row_step, 1)
                nc.vector.tensor_tensor(rowf[1], rowf[0], rowp[0], ALU.subtract).then_inc(row_step, 1)
                dve.wait_ge(row_step, 2)
                nc.vector.tensor_copy(rowp[1], rowf[1]).then_inc(row_step, 1)
                dve.wait_ge(row_step, 3)
                nc.vector.tensor_tensor(rowf[0], rowf[1], rowp[1], ALU.subtract).then_inc(row_step, 1)
                dve.wait_ge(row_step, 4)
                nc.vector.tensor_copy(rowp[2], rowf[0]).then_inc(row_step, 1)
                dve.wait_ge(small_in, 16)
                for i, dst in enumerate((m.identb, m.negcausal, m.negblock)):
                    nc.vector.tensor_copy(dst[:, :], mk[:, i * P:(i + 1) * P])
                nc.vector.tensor_copy(m.negband[:, :], mk[:, 3 * P:5 * P]).then_inc(masks_set, 1)
                dve.wait_ge(emb_in, 16)
                nc.vector.memset(est, 0.0).then_inc(estep, 1)
                n = Count()
                dve.wait_ge(estep, n.up())
                for part, blocks in enumerate(((0, 2, 4), (1, 3), (5,))):
                    for base in (0, 64):
                        for i in blocks:
                            nc.vector.tensor_copy(est[:, base + HD * i:base + HD * (i + 1)], emb[part]).then_inc(estep, 1)
                            n.up()
                    dve.wait_ge(estep, n.n)
                    if part < 2:
                        nc.vector.tensor_tensor(emb[part + 1], emb[part], est[:, HD * blocks[0]:HD * (blocks[0] + 1)],
                                                ALU.subtract).then_inc(estep, 1)
                        dve.wait_ge(estep, n.up())
                dve.wait_ge(e_turned, 1)
                nc.vector.tensor_copy(m.EX, m.psb[:, 0, 0:REL])
                dve.wait_ge(rope_in, 32)
                hl = LHD // 2
                for l in range(DEPTH):
                    nc.vector.tensor_tensor(m.rotary["cos"][:, l], rt[:, 0],
                                            qs[:, l].unsqueeze(1).to_broadcast([P, NT, 2, LHD]), ALU.mult)
                    for a, b in ((0, hl), (hl, 0)):
                        nc.vector.tensor_tensor(m.rotary["sin"][:, l, :, :, a:a + hl], rt[:, 1, :, :, a:a + hl],
                                                qs[:, l, :, b:b + hl].unsqueeze(1).to_broadcast([P, NT, 2, hl]),
                                                ALU.mult)

        with nc.Fori(0, B) as b:
            with stage(nc, "x_in") as (block, x_got):
                @block.sync
                def _(sp):
                    sp.dma_start(m.x[:, :, :], x_in[bass.ds(b, 1)].rearrange("o (t p) d -> p (o t) d", p=P)).then_inc(x_got, 16)
                    sp.wait_ge(x_got, 16)
            steps = [l0_ffn, l0_attn, l0_ffn, l1_ffn, l1_attn, l1_ffn, l2_ffn, l2_attn, l2_ffn,
                     l3_ffn, l3_attn, l3_ffn]
            for sub in steps:
                sub(nc, m)
            with stage(nc, "stored") as (block, stored):
                @block.sync
                def _(sp):
                    sp.dma_start(out[bass.ds(b, 1)].rearrange("o (t p) d -> p (o t) d", p=P), m.x[:, :, :]).then_inc(stored, 16)
                    sp.wait_ge(stored, 16)



def shape_constants():
    i = np.arange(P)
    f = np.float32
    c = {"ident": np.eye(P, dtype=f), "tri": (i[None, :] < i[:, None]).astype(f),
         "causalT": (i[:, None] <= i[None, :]).astype(f), "blockdiag": (i[:, None] // HD == i[None, :] // HD).astype(f),
         "tri8": np.broadcast_to(np.tril(np.ones((NE, NE), f), -1).reshape(1, -1), (P, NE * NE)),
         "neg_half": np.full((P, NT), -0.5, f), "half": np.full((P, NT * 32), 0.5, f), "ones": np.ones((P, P), f)}
    pos = np.arange(L, dtype=f)
    inv = (f(1.0) / f(10000.0) ** (np.arange(0, HD, 2, dtype=f) / f(HD))).astype(f)
    ang = (pos[:, None] * inv[None, :]).astype(f).astype(np.float64)
    for name, fn in (("rope_cos", np.cos), ("rope_sin", np.sin)):
        c[name] = fn(ang).astype(f).reshape(NT, P, 4).transpose(1, 0, 2).reshape(P, NT * 4)
    q, k = i[:, None], i[None, :]
    causal = np.where(k <= q, 0, NEG)
    block32 = np.where((k <= q) & (k // 32 == q // 32), 0, NEG)
    kk = np.arange(2 * P)[None, :] - P
    band = np.where((kk <= q) & (q - kk <= WIN), 0, NEG)
    masks = np.concatenate([np.eye(P), causal, block32, band], 1).astype(f)
    half = np.arange(0, LHD, 2, dtype=f)
    inv = (f(1.0) / f(10000.0) ** (half / f(LHD))).astype(f)
    ang = (pos[:, None] * inv[None, :]).astype(f).astype(np.float64)
    base = ((half + f(0.4 * LHD)) / f(1.4 * LHD)).astype(f)
    power = ((pos - L // 2) / f(WIN // 2)).astype(f)
    scale = (base[None, :].astype(np.float64) ** power[:, None]).astype(f).astype(np.float64)
    tabs = []
    for fn, first in ((np.cos, 1.0), (np.sin, -1.0)):
        v = fn(ang).astype(f).astype(np.float64)
        t = np.stack([np.concatenate([first * v * s, v * s], 1) for s in (8.0 * scale, 1.0 / scale)], 1)
        tabs.append(t.reshape(NT, P, 2, LHD).transpose(1, 0, 2, 3))
    rope3 = np.stack(tabs, 1).astype(f).reshape(P, -1)
    return c, masks, rope3



def lay_out(g, c):
    def tiles(a, n):
        return a.reshape(n, P, -1).transpose(1, 0, 2).reshape(P, -1)

    def on_128(a):
        out = np.zeros((P, a.shape[1]), a.dtype)
        out[:a.shape[0]] = a
        return out

    def on_heads(a):
        out = np.zeros((4, 4, 32, a.shape[1]), a.dtype)
        out[:, :, :HD] = a.reshape(4, 4, HD, -1)
        return out.transpose(1, 2, 0, 3).reshape(P, -1)

    d = dict(c)
    d["ip_T"] = g["L0_ffn_input_patterns"].T
    d["piw_T"] = tiles(g["L0_ffn_process_input_weights"].T, 8)
    d["pv"] = tiles(g["L0_ffn_process_values"], 4)
    d["oiw_T"] = on_128(g["L0_ffn_output_input_weights"].T)
    d["op"] = tiles(g["L0_ffn_output_patterns"], 8)
    d["l0_qkv"], d["l0_out"] = g["L0_attn_w_qkv"].T, on_heads(g["L0_attn_w_out"].T)
    d["l1f_qkv"], d["l1f_out"], d["l1f_gate"] = g["L1_ffn_in_proj_w"].T, g["L1_ffn_out_proj_w"].T, g["L1_ffn_gate_w"].T
    d["l1f_exp"] = g["L1_ffn_expert_w"].transpose(2, 0, 1).reshape(D, -1)
    for n in ("ln1_w", "ln1_b", "ln2_w", "ln2_b"):
        d["l1f_" + n] = np.broadcast_to(g["L1_ffn_" + n][None, :], (P, D))
    d["l1a_qkvb"] = np.concatenate([g["L1_attn_" + n] for n in ("Wq", "Wk", "Wv", "Wb")], 1)
    d["l1a_out"] = on_heads(g["L1_attn_Wo"])
    d["l2f_rw"] = g["L2_ffn_router_w"]
    d["l2f_w1"] = g["L2_ffn_w1"].transpose(1, 0, 2).reshape(D, -1)
    d["l2f_b1"] = g["L2_ffn_b1"].reshape(NE, 2 * NC2, P).transpose(2, 0, 1).reshape(P, -1)
    d["l2f_w2"] = g["L2_ffn_w2"].reshape(NE, NC2, P, D).transpose(2, 0, 1, 3).reshape(P, -1)
    d["l2a_qkv"], d["l2a_out"] = g["L2_attn_Wqkv"].T, g["L2_attn_Wout"].T
    d["l3a_qkv"] = np.concatenate([g["L3_attn_" + n].T for n in ("Wq", "Wk", "Wv")], 1)
    d["l3a_out"] = g["L3_attn_Wo"].T
    d["l3f_qkv"] = g["L3_ffn_wqkv"].transpose(1, 0, 2).reshape(D, -1)
    d["l3f_wo"] = g["L3_ffn_wo"].reshape(DEPTH, 4, P, D).transpose(2, 0, 1, 3).reshape(P, -1)
    d["l3f_w1"] = g["L3_ffn_w1"].transpose(1, 0, 2).reshape(D, -1)
    b1 = np.zeros((DEPTH, 2, NC3 * P), np.float32)
    b1[:, :, :HID3] = g["L3_ffn_b1"].reshape(DEPTH, 2, HID3)
    d["l3f_b1"] = b1.reshape(DEPTH, 2, NC3, P).transpose(3, 0, 1, 2).reshape(P, -1)
    w2 = np.zeros((DEPTH, NC3 * P, D), np.float32)
    w2[:, :HID3] = g["L3_ffn_w2"]
    d["l3f_w2"] = w2.reshape(DEPTH, NC3, P, D).transpose(2, 0, 1, 3).reshape(P, -1)
    d["l3f_lng"], d["l3f_lnb"] = g["L3_ffn_ln_g"].T, g["L3_ffn_ln_b"].T
    packs = [np.concatenate([d[n] for n, _ in fields], 1) for fields in LEVELS]
    r = {"l1f_qkv_b": g["L1_ffn_in_proj_b"], "l1f_out_b": g["L1_ffn_out_proj_b"],
         "l1f_gate_b": g["L1_ffn_gate_b"], "l1f_exp_b": g["L1_ffn_expert_b"], "l1a_bb": g["L1_attn_bb"],
         "l2f_rb": g["L2_ffn_router_b"], "l2f_b2": g["L2_ffn_b2"],
         "l3a_qkv_b": np.concatenate([g["L3_attn_" + n] for n in ("bq", "bk", "bv")]), "l3a_out_b": g["L3_attn_bo"],
         "l3f_b2": g["L3_ffn_b2"]}
    rows = np.zeros((len(ROWS), ROW_COLS), np.float32)
    for i, fields in enumerate(ROWS):
        for name, (a, n) in offsets(fields)[0].items():
            rows[i, a:a + n] = r[name].reshape(-1)
    stream = np.concatenate([d[n] for n, _ in STREAM], 1)
    qk_scale = np.stack([g["L3_ffn_q_scale"], g["L3_ffn_k_scale"]], 1).reshape(1, -1)
    return packs, stream, rows, qk_scale


def kernel(**inputs):
    import concourse.bacc as bacc
    from concourse.bass_utils import run_bass_kernel_spmd

    g = {k: np.asarray(v) for k, v in inputs.items()}
    c, masks, rope3 = shape_constants()
    packs, stream, rows, qk_scale = lay_out(g, c)
    arrays = {f"pack{i}": a for i, a in enumerate(packs)}
    arrays.update(stream=stream, rel_emb=g["L0_attn_rel_emb"][MAX_REL - REL + 1:MAX_REL + 1], rows=rows, masks=masks, rope3=rope3, qk_scale=qk_scale, x=g["L0_attn_x"])
    arrays = {k: np.ascontiguousarray(v) for k, v in arrays.items()}
    nc = bacc.Bacc("TRN2", target_bir_lowering=False, num_devices=1)
    ap = {k: nc.dram_tensor(f"in_{k}", v.shape, mybir.dt.from_np(v.dtype), kind="ExternalInput").ap()
          for k, v in arrays.items()}
    out = nc.dram_tensor("out_0", (B, L, D), F32, kind="ExternalOutput").ap()
    macaron(nc, [ap[f"pack{i}"] for i in range(len(LEVELS))], ap["stream"], ap["rel_emb"], ap["rows"], ap["masks"], ap["rope3"], ap["qk_scale"],
            ap["x"], out)
    r = run_bass_kernel_spmd(nc, [{f"in_{k}": v for k, v in arrays.items()}], core_ids=[0])
    return r.results[0]["out_0"]
```
